# Optimizing a Trainium2 kernel written in Bass

```python
import numpy as np
import jax
import jax.numpy as jnp

def _softmax(x, axis=-1):
    return jax.nn.softmax(x, axis=axis)

def _gelu(x):
    return jax.nn.gelu(x, approximate=True)

def _silu(x):
    return jax.nn.silu(x)

def _sigmoid(x):
    return jax.nn.sigmoid(x)

def _layernorm(x, axis=-1, eps=1e-05):
    m = jnp.mean(x, axis=axis, keepdims=True)
    v = jnp.var(x, axis=axis, keepdims=True)
    return (x - m) / jnp.sqrt(v + eps)

def _scatter_add(tgt, idx, src, axis=0):
    return tgt.at[idx].add(src)

def _segment_sum(src, seg, n):
    return jax.ops.segment_sum(src, seg, n)
kernel_name = 'mk_seq_postln_d2_jaxref_r8_8b5587'

def setup_inputs(seed: int=0):
    np.random.seed(seed)
    _w = jnp.asarray

    def _L0_attn_setup():
        import jax, jax.numpy as jnp
        import numpy as np
        N_HEADS = 16
        MAX_DIST = 64
        key = jax.random.key(seed)
        ks = jax.random.split(key, 7)
        B, S, D = (16, 64, 128)
        hd = D // N_HEADS
        num_rel = 2 * MAX_DIST + 1
        s = 0.02
        return {'x': jax.random.normal(ks[0], (B, S, D), dtype=jnp.float32), 'Wq': jax.random.normal(ks[1], (D, D), dtype=jnp.float32) * s, 'Wk': jax.random.normal(ks[2], (D, D), dtype=jnp.float32) * s, 'Wv': jax.random.normal(ks[3], (D, D), dtype=jnp.float32) * s, 'Eq': jax.random.normal(ks[4], (num_rel, hd), dtype=jnp.float32) * s, 'Ek': jax.random.normal(ks[5], (num_rel, hd), dtype=jnp.float32) * s, 'Ev': jax.random.normal(ks[6], (num_rel, hd), dtype=jnp.float32) * s}
    _L0_attn_in = _L0_attn_setup()

    def _L0_ffn_setup():
        import jax, jax.numpy as jnp
        import numpy as np
        DIM = 128
        DEPTH = 6
        HEADS = 16
        DIM_HEAD = 64
        WINDOW = 32
        INNER = HEADS * DIM_HEAD
        DIM_INNER = int(DIM * 4 * 2 / 3)
        QK_SCALE = 8.0

        def shift_tokens(t):
            a, s = jnp.split(t, 2, -1)
            s = jnp.pad(s, ((0, 0), (1, 0), (0, 0)))[:, :-1]
            return jnp.concatenate([a, s], -1)

        def l2norm(t):
            return t / jnp.maximum(jnp.linalg.norm(t, axis=-1, keepdims=True), 1e-12)

        def rotate_half(x):
            x1, x2 = jnp.split(x, 2, -1)
            return jnp.concatenate([-x2, x1], -1)

        def rotary_tables(n):
            half = jnp.arange(0, DIM_HEAD, 2, dtype=jnp.float32)
            inv_freq = 1.0 / 10000.0 ** (half / DIM_HEAD)
            t = jnp.arange(n, dtype=jnp.float32)
            freqs = t[:, None] * inv_freq[None, :]
            freqs = jnp.concatenate([freqs, freqs], -1)
            base_scale = (half + 0.4 * DIM_HEAD) / (1.4 * DIM_HEAD)
            power = (t - n // 2) / (WINDOW // 2)
            scale = base_scale[None, :] ** power[:, None]
            scale = jnp.concatenate([scale, scale], -1)
            return (freqs, scale)

        def local_attention(q, k, v):
            b, h, n, d = q.shape
            w = WINDOW
            nw = n // w
            bq = q.reshape(b, h, nw, w, d)
            bk = k.reshape(b, h, nw, w, d)
            bv = v.reshape(b, h, nw, w, d)

            def look(t):
                p = jnp.pad(t, ((0, 0), (0, 0), (1, 0), (0, 0), (0, 0)))
                return jnp.concatenate([p[:, :, :nw], p[:, :, 1:]], axis=3)
            bk2, bv2 = (look(bk), look(bv))
            seq = jnp.arange(n).reshape(nw, w)
            seq_p = jnp.pad(seq, ((1, 0), (0, 0)), constant_values=-1)
            jt = jnp.concatenate([seq_p[:nw], seq_p[1:]], axis=1)
            it = seq[:, :, None]
            jb = jt[:, None, :]
            mask = (it < jb) | (it > jb + w) | (jb == -1)
            sim = jnp.einsum('bhwie,bhwje->bhwij', bq, bk2) * QK_SCALE
            sim = jnp.where(mask, -jnp.finfo(sim.dtype).max, sim)
            attn = jax.nn.softmax(sim, -1)
            out = jnp.einsum('bhwij,bhwje->bhwie', attn, bv2)
            return out.reshape(b, h, n, d)

        def attn_layer(x, Wqkv, qs, ksc, Wo):
            b, n, _ = x.shape
            qkv = x @ Wqkv
            q, k, v = jnp.split(qkv, 3, -1)
            sh = lambda t: t.reshape(b, n, HEADS, DIM_HEAD).transpose(0, 2, 1, 3)
            q, k, v = (sh(q), sh(k), sh(v))
            q = l2norm(q) * qs
            k = l2norm(k) * ksc
            freqs, scale = rotary_tables(n)
            cos, sin = (jnp.cos(freqs), jnp.sin(freqs))
            q = q * cos * scale + rotate_half(q) * sin * scale
            inv = 1.0 / scale
            k = k * cos * inv + rotate_half(k) * sin * inv
            out = local_attention(q, k, v)
            out = out.transpose(0, 2, 1, 3).reshape(b, n, INNER)
            return out @ Wo

        def ffn_layer(x, g, bln, W1, b1, W2, b2):
            mu = x.mean(-1, keepdims=True)
            var = ((x - mu) ** 2).mean(-1, keepdims=True)
            xn = (x - mu) / jnp.sqrt(var + 1e-05) * g + bln
            hg = xn @ W1 + b1
            a, gate = jnp.split(hg, 2, -1)
            return a * jax.nn.gelu(gate, approximate=False) @ W2 + b2
        key = jax.random.key(seed)
        ks = jax.random.split(key, 8)
        B, N = (2, 256)
        init = lambda k, shape: jax.random.normal(k, shape, jnp.float32) * 0.02
        return {'x': jax.random.normal(ks[0], (B, N, DIM), jnp.float32), 'Wqkv': init(ks[1], (DEPTH, DIM, 3 * INNER)), 'q_scale': jnp.ones((DEPTH, DIM_HEAD), jnp.float32), 'k_scale': jnp.ones((DEPTH, DIM_HEAD), jnp.float32), 'Wo': init(ks[2], (DEPTH, INNER, DIM)), 'ln_g': jnp.ones((DEPTH, DIM), jnp.float32), 'ln_b': jnp.zeros((DEPTH, DIM), jnp.float32), 'W1': init(ks[3], (DEPTH, DIM, 2 * DIM_INNER)), 'b1': jnp.zeros((DEPTH, 2 * DIM_INNER), jnp.float32), 'W2': init(ks[4], (DEPTH, DIM_INNER, DIM)), 'b2': jnp.zeros((DEPTH, DIM), jnp.float32)}
    _L0_ffn_in = _L0_ffn_setup()

    def _L1_attn_setup():
        import jax, jax.numpy as jnp
        import numpy as np
        EMBED_DIM = 128
        NUM_HEADS = 16
        HEAD_DIM = EMBED_DIM // NUM_HEADS
        key = jax.random.key(seed)
        k0, k1, k2, k3, k4 = jax.random.split(key, 5)
        B, S = (1, 512)
        scale = 1.0 / np.sqrt(EMBED_DIM)
        x = jax.random.normal(k0, (B, S, EMBED_DIM), dtype=jnp.float32)
        Wqkv = jax.random.normal(k1, (EMBED_DIM, 3 * EMBED_DIM), dtype=jnp.float32) * scale
        bqkv = jax.random.normal(k2, (3 * EMBED_DIM,), dtype=jnp.float32) * 0.02
        Wout = jax.random.normal(k3, (EMBED_DIM, EMBED_DIM), dtype=jnp.float32) * scale
        bout = jax.random.normal(k4, (EMBED_DIM,), dtype=jnp.float32) * 0.02
        return {'x': x, 'Wqkv': Wqkv, 'bqkv': bqkv, 'Wout': Wout, 'bout': bout}
    _L1_attn_in = _L1_attn_setup()

    def _L1_ffn_setup():
        import jax, jax.numpy as jnp
        import numpy as np
        NUM_EXPERTS = 8
        TOP_K = 2
        D_MODEL = 128
        EXPERT_CAP = 64
        B, S = (4, 256)
        key = jax.random.key(seed)
        ks = jax.random.split(key, 4)
        scale = 1.0 / np.sqrt(D_MODEL)
        x = jax.random.normal(ks[0], (B, S, D_MODEL), dtype=jnp.float32)
        gate_w = jax.random.normal(ks[1], (D_MODEL, NUM_EXPERTS), dtype=jnp.float32) * scale
        w1 = jax.random.normal(ks[2], (NUM_EXPERTS, D_MODEL, EXPERT_CAP), dtype=jnp.float32) * scale
        b1 = jnp.zeros((NUM_EXPERTS, EXPERT_CAP), dtype=jnp.float32)
        w2 = jax.random.normal(ks[3], (NUM_EXPERTS, EXPERT_CAP, D_MODEL), dtype=jnp.float32) * (1.0 / np.sqrt(EXPERT_CAP))
        b2 = jnp.zeros((NUM_EXPERTS, D_MODEL), dtype=jnp.float32)
        return {'x': x, 'gate_w': gate_w, 'w1': w1, 'b1': b1, 'w2': w2, 'b2': b2}
    _L1_ffn_in = _L1_ffn_setup()
    _d = {'L0_attn_x': _L0_attn_in['x'], 'L0_attn_Wq': _L0_attn_in['Wq'], 'L0_attn_Wk': _L0_attn_in['Wk'], 'L0_attn_Wv': _L0_attn_in['Wv'], 'L0_attn_Eq': _L0_attn_in['Eq'], 'L0_attn_Ek': _L0_attn_in['Ek'], 'L0_attn_Ev': _L0_attn_in['Ev'], 'L0_ffn_Wqkv': _L0_ffn_in['Wqkv'], 'L0_ffn_q_scale': _L0_ffn_in['q_scale'], 'L0_ffn_k_scale': _L0_ffn_in['k_scale'], 'L0_ffn_Wo': _L0_ffn_in['Wo'], 'L0_ffn_ln_g': _L0_ffn_in['ln_g'], 'L0_ffn_ln_b': _L0_ffn_in['ln_b'], 'L0_ffn_W1': _L0_ffn_in['W1'], 'L0_ffn_b1': _L0_ffn_in['b1'], 'L0_ffn_W2': _L0_ffn_in['W2'], 'L0_ffn_b2': _L0_ffn_in['b2'], 'L1_attn_Wqkv': _L1_attn_in['Wqkv'], 'L1_attn_bqkv': _L1_attn_in['bqkv'], 'L1_attn_Wout': _L1_attn_in['Wout'], 'L1_attn_bout': _L1_attn_in['bout'], 'L1_ffn_gate_w': _L1_ffn_in['gate_w'], 'L1_ffn_w1': _L1_ffn_in['w1'], 'L1_ffn_b1': _L1_ffn_in['b1'], 'L1_ffn_w2': _L1_ffn_in['w2'], 'L1_ffn_b2': _L1_ffn_in['b2']}
    _x0 = _d['L0_attn_x']
    _d['L0_attn_x'] = jax.random.normal(jax.random.fold_in(jax.random.key(seed), 1), (16, 256, 128), dtype=_x0.dtype)
    del _x0
    return _d

def reference(L0_attn_x, L0_attn_Wq, L0_attn_Wk, L0_attn_Wv, L0_attn_Eq, L0_attn_Ek, L0_attn_Ev, L0_ffn_Wqkv, L0_ffn_q_scale, L0_ffn_k_scale, L0_ffn_Wo, L0_ffn_ln_g, L0_ffn_ln_b, L0_ffn_W1, L0_ffn_b1, L0_ffn_W2, L0_ffn_b2, L1_attn_Wqkv, L1_attn_bqkv, L1_attn_Wout, L1_attn_bout, L1_ffn_gate_w, L1_ffn_w1, L1_ffn_b1, L1_ffn_w2, L1_ffn_b2):

    def _L0_attn_ref(x, Wq, Wk, Wv, Eq, Ek, Ev):
        import jax, jax.numpy as jnp
        import numpy as np
        N_HEADS = 16
        MAX_DIST = 64
        B, S, D = x.shape
        H = N_HEADS
        hd = D // H
        r = jnp.arange(S)
        rel = jnp.clip(r[:, None] - r[None, :], -MAX_DIST, MAX_DIST) + MAX_DIST

        def proj(W):
            return jnp.einsum('bsd,de->bse', x, W).reshape(B, S, H, hd).transpose(0, 2, 1, 3)
        q, k, v = (proj(Wq), proj(Wk), proj(Wv))
        a_q = Eq[rel]
        a_k = Ek[rel]
        a_v = Ev[rel]
        content = jnp.einsum('bhld,bhmd->bhlm', q, k)
        rel_k = jnp.einsum('bhld,lmd->bhlm', q, a_k)
        rel_q = jnp.einsum('bhmd,lmd->bhlm', k, a_q)
        pos_pos = jnp.einsum('lmd,lmd->lm', a_q, a_k)
        scale = 1.0 / hd ** 0.5
        logits = (content + rel_k + rel_q + pos_pos) * scale
        attn = jax.nn.softmax(logits, axis=-1)
        out = jnp.einsum('bhlm,bhmd->bhld', attn, v) + jnp.einsum('bhlm,lmd->bhld', attn, a_v)
        return out.transpose(0, 2, 1, 3).reshape(B, S, D)

    def _L0_ffn_ref(x, Wqkv, q_scale, k_scale, Wo, ln_g, ln_b, W1, b1, W2, b2):
        import jax, jax.numpy as jnp
        import numpy as np
        DIM = 128
        DEPTH = 6
        HEADS = 16
        DIM_HEAD = 64
        WINDOW = 32
        INNER = HEADS * DIM_HEAD
        DIM_INNER = int(DIM * 4 * 2 / 3)
        QK_SCALE = 8.0

        def shift_tokens(t):
            a, s = jnp.split(t, 2, -1)
            s = jnp.pad(s, ((0, 0), (1, 0), (0, 0)))[:, :-1]
            return jnp.concatenate([a, s], -1)

        def l2norm(t):
            return t / jnp.maximum(jnp.linalg.norm(t, axis=-1, keepdims=True), 1e-12)

        def rotate_half(x):
            x1, x2 = jnp.split(x, 2, -1)
            return jnp.concatenate([-x2, x1], -1)

        def rotary_tables(n):
            half = jnp.arange(0, DIM_HEAD, 2, dtype=jnp.float32)
            inv_freq = 1.0 / 10000.0 ** (half / DIM_HEAD)
            t = jnp.arange(n, dtype=jnp.float32)
            freqs = t[:, None] * inv_freq[None, :]
            freqs = jnp.concatenate([freqs, freqs], -1)
            base_scale = (half + 0.4 * DIM_HEAD) / (1.4 * DIM_HEAD)
            power = (t - n // 2) / (WINDOW // 2)
            scale = base_scale[None, :] ** power[:, None]
            scale = jnp.concatenate([scale, scale], -1)
            return (freqs, scale)

        def local_attention(q, k, v):
            b, h, n, d = q.shape
            w = WINDOW
            nw = n // w
            bq = q.reshape(b, h, nw, w, d)
            bk = k.reshape(b, h, nw, w, d)
            bv = v.reshape(b, h, nw, w, d)

            def look(t):
                p = jnp.pad(t, ((0, 0), (0, 0), (1, 0), (0, 0), (0, 0)))
                return jnp.concatenate([p[:, :, :nw], p[:, :, 1:]], axis=3)
            bk2, bv2 = (look(bk), look(bv))
            seq = jnp.arange(n).reshape(nw, w)
            seq_p = jnp.pad(seq, ((1, 0), (0, 0)), constant_values=-1)
            jt = jnp.concatenate([seq_p[:nw], seq_p[1:]], axis=1)
            it = seq[:, :, None]
            jb = jt[:, None, :]
            mask = (it < jb) | (it > jb + w) | (jb == -1)
            sim = jnp.einsum('bhwie,bhwje->bhwij', bq, bk2) * QK_SCALE
            sim = jnp.where(mask, -jnp.finfo(sim.dtype).max, sim)
            attn = jax.nn.softmax(sim, -1)
            out = jnp.einsum('bhwij,bhwje->bhwie', attn, bv2)
            return out.reshape(b, h, n, d)

        def attn_layer(x, Wqkv, qs, ksc, Wo):
            b, n, _ = x.shape
            qkv = x @ Wqkv
            q, k, v = jnp.split(qkv, 3, -1)
            sh = lambda t: t.reshape(b, n, HEADS, DIM_HEAD).transpose(0, 2, 1, 3)
            q, k, v = (sh(q), sh(k), sh(v))
            q = l2norm(q) * qs
            k = l2norm(k) * ksc
            freqs, scale = rotary_tables(n)
            cos, sin = (jnp.cos(freqs), jnp.sin(freqs))
            q = q * cos * scale + rotate_half(q) * sin * scale
            inv = 1.0 / scale
            k = k * cos * inv + rotate_half(k) * sin * inv
            out = local_attention(q, k, v)
            out = out.transpose(0, 2, 1, 3).reshape(b, n, INNER)
            return out @ Wo

        def ffn_layer(x, g, bln, W1, b1, W2, b2):
            mu = x.mean(-1, keepdims=True)
            var = ((x - mu) ** 2).mean(-1, keepdims=True)
            xn = (x - mu) / jnp.sqrt(var + 1e-05) * g + bln
            hg = xn @ W1 + b1
            a, gate = jnp.split(hg, 2, -1)
            return a * jax.nn.gelu(gate, approximate=False) @ W2 + b2
        for i in range(DEPTH):
            x = attn_layer(shift_tokens(x), Wqkv[i], q_scale[i], k_scale[i], Wo[i]) + x
            x = ffn_layer(shift_tokens(x), ln_g[i], ln_b[i], W1[i], b1[i], W2[i], b2[i]) + x
        return x

    def _L1_attn_ref(x, Wqkv, bqkv, Wout, bout):
        import jax, jax.numpy as jnp
        import numpy as np
        EMBED_DIM = 128
        NUM_HEADS = 16
        HEAD_DIM = EMBED_DIM // NUM_HEADS
        B, S, E = x.shape
        H, D = (NUM_HEADS, HEAD_DIM)
        qkv = x @ Wqkv + bqkv
        qkv = qkv.reshape(B, S, 3, H, D)
        q, k, v = (qkv[:, :, 0], qkv[:, :, 1], qkv[:, :, 2])
        softmax_scale = 1.0 / np.sqrt(D)
        scores = jnp.einsum('bthd,bshd->bhts', q, k * softmax_scale)
        causal_mask = jnp.triu(jnp.full((S, S), -10000.0, dtype=scores.dtype), 1)
        scores = scores + causal_mask
        attention = jax.nn.softmax(scores, axis=-1)
        context = jnp.einsum('bhts,bshd->bthd', attention, v)
        out = context.reshape(B, S, E) @ Wout + bout
        return out

    def _L1_ffn_ref(x, gate_w, w1, b1, w2, b2):
        import jax, jax.numpy as jnp
        import numpy as np
        NUM_EXPERTS = 8
        TOP_K = 2
        D_MODEL = 128
        EXPERT_CAP = 64
        B, S = (4, 256)
        Bx, Sx, D = x.shape
        xt = x.reshape(-1, D)
        gates = jax.nn.softmax(xt @ gate_w, axis=-1)
        topk_g, topk_i = jax.lax.top_k(gates, TOP_K)
        tok_w = topk_g.sum(axis=-1)
        sel = (topk_i[:, :, None] == jnp.arange(NUM_EXPERTS)[None, None, :]).any(axis=1)
        h = jax.nn.gelu(jnp.einsum('nd,edh->enh', xt, w1) + b1[:, None, :], approximate=False)
        y = jnp.einsum('enh,ehd->end', h, w2) + b2[:, None, :]
        out = jnp.einsum('end,ne,n->nd', y, sel.astype(x.dtype), tok_w)
        return out.reshape(Bx, Sx, D)
    x = L0_attn_x
    x = _layernorm(x + _L0_attn_ref(x, L0_attn_Wq, L0_attn_Wk, L0_attn_Wv, L0_attn_Eq, L0_attn_Ek, L0_attn_Ev), axis=-1)
    x = _layernorm(x + _L0_ffn_ref(x, L0_ffn_Wqkv, L0_ffn_q_scale, L0_ffn_k_scale, L0_ffn_Wo, L0_ffn_ln_g, L0_ffn_ln_b, L0_ffn_W1, L0_ffn_b1, L0_ffn_W2, L0_ffn_b2), axis=-1)
    x = _layernorm(x + _L1_attn_ref(x, L1_attn_Wqkv, L1_attn_bqkv, L1_attn_Wout, L1_attn_bout), axis=-1)
    x = _layernorm(x + _L1_ffn_ref(x, L1_ffn_gate_w, L1_ffn_w1, L1_ffn_b1, L1_ffn_w2, L1_ffn_b2), axis=-1)
    return x

_drawn_inputs = setup_inputs


def setup_inputs(seed=0):
    import zlib

    import numpy as np

    out = dict(_drawn_inputs(seed))
    spreads = {'L0_ffn_q_scale': (1.0, 0.2),
     'L0_ffn_k_scale': (1.0, 0.54),
     'L0_ffn_ln_g': (1.0, 0.544),
     'L0_ffn_ln_b': (0.0, 0.368),
     'L0_ffn_b1': (0.0, 0.1),
     'L0_ffn_b2': (0.0, 0.1),
     'L1_ffn_b1': (0.0, 0.1),
     'L1_ffn_b2': (0.0, 0.1)}
    factors = {'L0_attn_Wq': 3.676, 'L0_attn_Wk': 3.42, 'L0_attn_Eq': 7.821, 'L0_attn_Ek': 22.195}
    for name, (base, spread) in spreads.items():
        noise = np.random.default_rng([zlib.crc32(name.encode()), seed]).standard_normal(out[name].shape)
        drawn = base * np.exp(spread * noise) if base else spread * noise
        out[name] = jnp.asarray(drawn.astype(out[name].dtype))
    for name, factor in factors.items():
        out[name] = (out[name] * factor).astype(out[name].dtype)
    return out
```

```python
from contextlib import ExitStack

import numpy as np

import concourse.bass as bass
from concourse import mybir

F32 = mybir.dt.float32
BF16 = mybir.dt.bfloat16
ALU = mybir.AluOpType
ACT = mybir.ActivationFunctionType
AX = mybir.AxisListType

P = 128
B, S, D = 16, 256, 128
LT = S // P
NT = B * LT
H, HD = 16, 8
SCALE_A = 1.0 / HD ** 0.5
MAXD = 64
NREL = 2 * MAXD + 1
NREX = 2 * S - 1
LB = P // HD
NLB = P // LB
TABW = NREX - LB + 1
DEPTH, BH, BD, WIN = 6, 16, 64, 32
INNER = BH * BD
FF = int(D * 4 * 2 / 3)
FCH = [128, 128, FF - 256]
NEXP, EH = 8, 64
NPR = NEXP // 2
EPS = 1e-5
NEG = -1e30

GMASK, IDENT, SEL24, TRIU, WMASK, PMASK, COS, SIN, SHIFT, ESEL, LOWER = range(11)


def shape_constants():
    f = np.float32
    p = np.arange(P)
    c = {}
    c["group_mask"] = (p[:, None] // HD == np.arange(LB)[None, :]).astype(f)
    c["ident"] = np.eye(P, dtype=f)
    c["flip"] = np.ascontiguousarray(np.eye(P, dtype=f)[::-1])
    heads = p[:, None] // LB == np.arange(8)[None, :]
    toks = p[:, None] % LB == np.arange(LB)[None, :]
    c["own24"] = np.repeat(np.concatenate([heads, toks], 1)[:, :, None], HD, 2).reshape(P, 24 * HD).astype(f)
    c["causal"] = np.where(p[None, :] > p[:, None], f(-125), f(0)).astype(f)
    i, j = p[:, None], p[None, :]
    c["window_own"] = np.where((j > i) | (i > j + WIN), f(NEG), f(0)).astype(f)
    c["window_prev"] = np.where(i > np.arange(WIN)[None, :], f(NEG), f(0)).astype(f)
    half = np.arange(0, BD, 2, dtype=f)
    inv_freq = (f(1) / np.power(f(10000), half / f(BD))).astype(f)
    t = np.arange(S, dtype=f)
    freqs = (t[:, None] * inv_freq[None, :]).astype(f)
    freqs = np.concatenate([freqs, freqs], -1)
    base = ((half + f(0.4 * BD)) / f(1.4 * BD)).astype(f)
    power = ((t - S // 2) / f(WIN // 2)).astype(f)
    scale = np.power(base[None, :], power[:, None]).astype(f)
    scale = np.concatenate([scale, scale], -1)
    sign = np.where(np.arange(BD) < BD // 2, f(-1), f(1))
    inv = (f(1) / scale).astype(f)
    cos, sin = np.cos(freqs), np.sin(freqs) * sign
    lay = lambda q, k: np.stack([q, k], 1).reshape(LT, P, 2, BD).transpose(1, 0, 2, 3).reshape(P, LT * 2 * BD).astype(f)
    c["rot_cos"] = lay(cos * scale * f(8), cos * inv)
    c["rot_sin"] = lay(sin * scale * f(8), sin * inv)
    s1 = np.zeros((P, P), f)
    s1[p[:-1], p[:-1] + 1] = 1
    s2 = np.zeros((P, P), f)
    s2[P - 1, 0] = 1
    c["shift_in"], c["shift_over"] = s1, s2
    e = np.zeros((NEXP, NPR, 2, EH), f)
    for x in range(NEXP):
        e[x, x // 2, x % 2] = 1
    c["expert_rows"] = e.reshape(NEXP, NPR * 2 * EH)
    c["lower"] = np.tile(np.tril(np.ones((NEXP, NEXP), f), -1).reshape(1, -1), (P, 1))
    return c


def build_program(nc, T, out, stop=99):
    ctx = ExitStack()
    with ctx:
        def sb(stack, name, shape, dt=F32):
            return stack.enter_context(nc.sbuf_tensor(name, shape, dt))

        def sem(name):
            return ctx.enter_context(nc.semaphore(name))

        def dram(name, shape):
            return nc.dram_tensor(name, shape, F32, kind="Internal")

        X = sb(ctx, "X", [P, NT, D])
        XR = sb(ctx, "XR", [P, NT, D])
        ident = sb(ctx, "ident", [P, P])
        ident_bf = sb(ctx, "ident_bf", [P, P], BF16)
        gmask = sb(ctx, "gmask", [P, LB])
        ones = sb(ctx, "ones", [P, P])
        neghalf = sb(ctx, "neghalf", [P, LB])
        pause = sb(ctx, "pause", [P, 1])
        xcur = sb(ctx, "xcur", [P, LT, D])
        xT = sb(ctx, "xT", [P, S])
        psum = ctx.enter_context(nc.psum_tensor("psum", [P, 8, 512], F32))
        bank = [psum[:, i, :] for i in range(8)]

        oa = dram("oa", (B, LT, NLB, LB, 2, 8, HD))
        ev_ext = dram("ev_ext", (NREX, HD))
        pp_ext = dram("pp_ext", (1, 512))

        x_in = T["L0_attn_x"].rearrange("b (t p) c -> p (b t) c", p=P)
        out_v = out.rearrange("b (t p) c -> p (b t) c", p=P)

        with ExitStack() as st:
            wq, wk, wv = (sb(st, n, [P, D]) for n in ("a_wq", "a_wk", "a_wv"))
            wq_rep, wk_rep = (sb(st, n, [P, H, P]) for n in ("a_wq_rep", "a_wk_rep"))
            ext = sb(st, "a_ext", [HD, 4, NREX])
            pprow = sb(st, "a_pprow", [1, 512])
            eq_tab, ek_tab = (sb(st, n, [P, TABW]) for n in ("a_eq_tab", "a_ek_tab"))
            ev_tab = sb(st, "a_ev_tab", [P, LT * P + P, HD])
            pp_tab = sb(st, "a_pp_tab", [P, LT, S])
            own24 = sb(st, "a_own24", [P, 24 * HD])
            qT = sb(st, "a_qT", [P, S])
            k_diag = sb(st, "a_k_diag", [P, H, S])
            q_blk, k_blk = (sb(st, n, [P, H, S]) for n in ("a_q_blk", "a_k_blk"))
            relk = sb(st, "a_relk", [P, LT, H, P])
            probs = sb(st, "a_probs", [P, 2, 4, S])
            probsT = sb(st, "a_probsT", [P, LT, NLB, 8, LB])
            vones = sb(st, "a_vones", [P, LT, 2, 1 + 8 * HD])
            nmax, nbias = (sb(st, n, [P, 2, 4]) for n in ("a_nmax", "a_nbias"))
            rsum = sb(st, "a_rsum", [P, 8])
            ymask = sb(st, "a_ymask", [P, 8, 24 * HD])
            ysum = sb(st, "a_ysum", [P, 8, HD])
            yout = sb(st, "a_yout", [P, B * 4, 8 * HD])

            ld_x, ld_c, ld_w, ld_e = sem("a_ld_x"), sem("a_ld_c"), sem("a_ld_w"), sem("a_ld_e")
            ev_wr, pp_wr, tabs, flips = sem("a_ev_wr"), sem("a_pp_wr"), sem("a_tabs"), sem("a_flips")
            ev_turned, pp_turned = sem("a_ev_turned"), sem("a_pp_turned")
            ev_flip = q_blk[:, 0:12, :].rearrange("p h l -> p (h l)")
            pp_flip = k_blk[:, 0:2, :]
            flip = sb(st, "a_flip", [P, P])
            ext_ok, prod_ok, pp_full, pp_ok, set_ok = (sem("a_ext_ok"), sem("a_prod_ok"), sem("a_pp_full"),
                                                       sem("a_pp_ok"), sem("a_set_ok"))

            with nc.Block() as block:
                @block.sync
                def _(sp):
                    for name, t in (("L0_attn_Eq", 0), ("L0_attn_Ek", 2)):
                        sp.dma_start(ext[:, t, S - 1 - MAXD:S + MAXD], T[name].rearrange("r d -> d r"),
                                     allow_slow_non_contiguous=True).then_inc(ld_e, 16)
                    sp.dma_start(ext[:, 1, S - 1 - MAXD:S + MAXD],
                                 bass.AP(T["L0_attn_Ek"].tensor, (NREL - 1) * HD, [[1, HD], [-HD, NREL]]),
                                 allow_slow_non_contiguous=True).then_inc(ld_e, 16)
                    ev = T["L0_attn_Ev"]
                    sp.dma_start(ev_ext[S - 1 - MAXD:S + MAXD, :], ev[:, :]).then_inc(ev_wr, 16)
                    sp.dma_start(ev_ext[0:S - 1 - MAXD, :],
                                 ev[0:1, :].broadcast_to((S - 1 - MAXD, HD))).then_inc(ev_wr, 16)
                    sp.dma_start(ev_ext[S + MAXD:NREX, :],
                                 ev[NREL - 1:NREL, :].broadcast_to((S - 1 - MAXD, HD))).then_inc(ev_wr, 16)
                    sp.wait_ge(ev_wr, 48)
                    sp.dma_start(ev_flip, bass.AP(ev_ext, 0, [[HD, P], [1, (LT * P + P) * HD]])).then_inc(flips, 16)
                    sp.wait_ge(ext_ok, 1)
                    for m in range(LB):
                        for tab, t in ((eq_tab, 0), (ek_tab, 1)):
                            sp.dma_start(tab[HD * m:HD * m + HD, :],
                                         ext[:, t, LB - 1 - m:LB - 1 - m + TABW]).then_inc(tabs, 16)
                    sp.wait_ge(pp_ok, 1)
                    sp.dma_start(pp_ext[:, 0:NREX], pprow[:, 0:NREX]).then_inc(pp_wr, 16)
                    sp.wait_ge(pp_wr, 16)
                    for mt in range(LT):
                        sp.dma_start(pp_flip[:, mt, :],
                                     bass.AP(pp_ext, P - mt * P, [[1, P], [1, S]])).then_inc(flips, 16)
                    sp.wait_ge(tabs, 16 * 2 * LB)
                    sp.wait_ge(ld_x, 16)

                @block.scalar
                def _(act):
                    for name, t in (("L0_attn_Wq", wq), ("L0_attn_Wk", wk), ("L0_attn_Wv", wv)):
                        act.dma_start(t[:, :], T[name]).then_inc(ld_w, 16)
                    for name, t in (("ident", ident), ("group_mask", gmask), ("own24", own24), ("flip", flip)):
                        act.dma_start(t[:, :], T[name]).then_inc(ld_c, 16)
                    act.dma_start(X[:, :, :], x_in).then_inc(ld_x, 16)

                @block.gpsimd
                def _(pool):
                    nc.gpsimd.memset(ones[:, :], 1.0).then_inc(set_ok, 1)
                    nc.gpsimd.memset(neghalf[:, :], -0.5)
                    nc.gpsimd.memset(vones[:, :, :, :], 1.0)
                    pool.wait_ge(ld_w, 48)
                    for w, rep in ((wq, wq_rep), (wk, wk_rep)):
                        for h in range(H):
                            nc.gpsimd.tensor_copy(
                                rep[:, h, :].rearrange("p (l d) -> p l d", d=HD),
                                w[:, None, h * HD:(h + 1) * HD].broadcast_to((P, LB, HD)))

                @block.vector
                def _(dve):
                    dve.wait_ge(ld_e, 48)
                    for t in range(3):
                        a, b = S - 1 - MAXD, S + MAXD
                        nc.vector.tensor_copy(ext[:, t, 0:a], ext[:, t, a:a + 1].broadcast_to((HD, a)))
                        last = nc.vector.tensor_copy(ext[:, t, b:NREX],
                                                     ext[:, t, b - 1:b].broadcast_to((HD, NREX - b)))
                    last.then_inc(ext_ok, 1)
                    dve.wait_ge(ext_ok, 1)
                    nc.vector.tensor_tensor(ext[:, 3, :], ext[:, 0, :], ext[:, 2, :], ALU.mult).then_inc(prod_ok, 1)
                    dve.wait_ge(pp_full, 1)
                    nc.vector.tensor_copy(pprow[0:1, 0:NREX], bank[0][0:1, 0:NREX]).then_inc(pp_ok, 1)
                    dve.wait_ge(ld_c, 64)
                    nc.vector.tensor_copy(ident_bf[:, :], ident[:, :])
                    dve.wait_ge(ev_turned, 1)
                    nc.vector.tensor_copy(ev_tab[:, :, :].rearrange("p u d -> p (u d)"),
                                          psum[:, 1:7, :].rearrange("p a c -> p (a c)"))
                    dve.wait_ge(pp_turned, 1)
                    nc.vector.tensor_copy(pp_tab[:, :, :].rearrange("p t l -> p (t l)"), bank[7])

                @block.tensor
                def _(pe):
                    pe.wait_ge(set_ok, 1)
                    pe.wait_ge(prod_ok, 1)
                    nc.tensor.matmul(bank[0][0:1, 0:NREX], ones[0:HD, 0:1], ext[:, 3, :],
                                     start=True, stop=True).then_inc(pp_full, 1)
                    pe.wait_ge(ld_c, 64)
                    pe.wait_ge(flips, 16 * (1 + LT))
                    for i in range(6):
                        last = nc.tensor.matmul(bank[1 + i], flip[:, :], ev_flip[:, i * 512:(i + 1) * 512],
                                                start=True, stop=True)
                    last.then_inc(ev_turned, 1)
                    nc.tensor.matmul(bank[7], flip[:, :], pp_flip.rearrange("p t l -> p (t l)"),
                                     start=True, stop=True).then_inc(pp_turned, 1)

            FQK, FV, FQB, FKB, FRK, FY = 2, 3, 4, 12, (20, 32), (28, 40, 44, 48)
            order = list(range(28)) + [28, 29, 30, 31] + list(range(32, 52))
            FA = 52
            ring = bank[0:2]
            score = [psum[:, 2:4, :], psum[:, 4:6, :]]
            turned = bank[6:8]
            x_copied, ring_full, ring_free = sem("a_x_copied"), [sem("a_ring_full0"), sem("a_ring_full1")], \
                [sem("a_ring_free0"), sem("a_ring_free1")]
            score_full, row_max, bias_ok, exp_done = (sem("a_score_full"), sem("a_row_max"), sem("a_bias_ok"),
                                                      sem("a_exp_done"))
            turn_full, turn_out = sem("a_turn_full"), sem("a_turn_out")
            ymask_ok, ysum_ok, yout_ok, oa_st = (sem("a_ymask_ok"), sem("a_ysum_ok"), sem("a_yout_ok"),
                                                 sem("a_oa_st"))

            def filled(b, i):
                return b * (FA // 2) + i // 2 + 1

            with nc.Block() as block:
                @block.gpsimd
                def _(pool):
                    with pool.Fori(0, B) as b:
                        nc.gpsimd.tensor_copy(xcur[:, :, :], X[:, bass.ds(b * LT, LT), :]).then_inc(x_copied, 1)
                        pool.wait_ge(ring_full[1], filled(b, 1))

                @block.tensor
                def _(pe):
                    with pe.Fori(0, B) as b:
                        def room(i):
                            if i >= 2:
                                pe.wait_ge(ring_free[i % 2], filled(b, i - 2))
                            return ring[i % 2]

                        def relative_keys(lt):
                            for n in range(8):
                                mt, i = n // 4, FRK[lt] + n
                                r = room(i)
                                for j in range(2):
                                    blk = lt * NLB // 1 + (n % 4) * 2 + j
                                    v = mt * P - blk * LB + S - LB
                                    last = nc.tensor.matmul(r[:, j * S:(j + 1) * S], ek_tab[:, v:v + P],
                                                            q_blk[:, :, blk * LB:(blk + 1) * LB], start=(j == 0), stop=(j == 1), skip_group_check=True)
                                last.then_inc(ring_full[i % 2], 1)

                        def scores(s):
                            lt, hq = s // 4, s % 4
                            if s >= 2:
                                pe.wait_ge(exp_done, b * 8 + s - 1)
                            if hq == 0:
                                for i in (6, 7):
                                    pe.wait_ge(ring_free[i % 2], filled(b, FRK[lt] + i))
                            for mt in range(LT):
                                o = score[s % 2][:, mt, :].rearrange("p (h m) -> p h m", h=4)
                                hs = slice(hq * 4, hq * 4 + 4)
                                nc.tensor.matmul(o, qT[:, lt * P:(lt + 1) * P], k_diag[:, hs, mt * P:(mt + 1) * P],
                                                 start=True, stop=False, skip_group_check=True)
                                for n in range(NLB):
                                    blk = mt * NLB + n
                                    v = lt * P - blk * LB + S - LB
                                    nc.tensor.matmul(o[:, :, n * LB:(n + 1) * LB], eq_tab[:, v:v + P],
                                                     k_blk[:, hs, blk * LB:(blk + 1) * LB], start=False, stop=False,
                                                     skip_group_check=True)
                                for h in range(4):
                                    last = nc.tensor.matmul(o[:, h, :], relk[:, mt, hq * 4 + h, :], ident[:, :],
                                                            start=False, stop=(h == 3), skip_group_check=True)
                            last.then_inc(score_full, 1)

                        def turn(s):
                            pe.wait_ge(exp_done, b * 8 + s + 1)
                            if s >= 1:
                                pe.wait_ge(turn_out, b * 8 + s)
                            for mt in range(LT):
                                for h in range(4):
                                    last = nc.tensor.transpose(turned[mt][:, h * P:(h + 1) * P],
                                                               probs[:, s % 2, h, mt * P:(mt + 1) * P], ident[:, :])
                            last.then_inc(turn_full, 1)

                        def outputs(g):
                            pe.wait_ge(turn_out, b * 8 + 2 * g + 2)
                            lt, hh = g // 2, g % 2
                            for n in range(4):
                                i = FY[g] + n
                                r = room(i)
                                for j in range(2):
                                    blk = lt * NLB + 2 * n + j
                                    for mt in range(LT):
                                        w = probsT[:, mt, 2 * n + j, :, :].rearrange("p h l -> p (h l)")
                                        o = r[:, j * 193:(j + 1) * 193]
                                        u = blk * LB - mt * P + P
                                        nc.tensor.matmul(o[:, 0:65], w, vones[:, mt, hh, :],
                                                         start=(j == 0 and mt == 0), stop=False, skip_group_check=True)
                                        last = nc.tensor.matmul(o[:, 65:193], w, ev_tab[:, u:u + LB, :],
                                                                start=False, stop=(j == 1 and mt == 1),
                                                                skip_group_check=True)
                                last.then_inc(ring_full[i % 2], 1)

                        pe.wait_ge(x_copied, b + 1)
                        for t in range(LT):
                            nc.tensor.transpose(room(t)[:, 0:P], xcur[:, t, :], ident[:, :]).then_inc(ring_full[t], 1)
                        r = room(FQK)
                        pe.wait_ge(ring_free[1], filled(b, 1))
                        nc.tensor.matmul(r[:, 0:S], wq[:, :], xT[:, :], start=True, stop=False, skip_group_check=True)
                        nc.tensor.matmul(r[:, S:2 * S], wk[:, :], xT[:, :], start=False, stop=True,
                                         skip_group_check=True).then_inc(ring_full[FQK % 2], 1)
                        r = room(FV)
                        for t in range(LT):
                            last = nc.tensor.matmul(r[:, t * D:(t + 1) * D], xT[:, t * P:(t + 1) * P], wv[:, :],
                                                    start=(t == 0), stop=(t == 1), skip_group_check=True)
                        last.then_inc(ring_full[FV % 2], 1)
                        for f, rep in ((FQB, wq_rep), (FKB, wk_rep)):
                            for n in range(H // 2):
                                r = room(f + n)
                                for j in range(2):
                                    last = nc.tensor.matmul(r[:, j * S:(j + 1) * S], rep[:, 2 * n + j, :], xT[:, :],
                                                            start=(j == 0), stop=(j == 1), skip_group_check=True)
                                last.then_inc(ring_full[(f + n) % 2], 1)
                        relative_keys(0)
                        scores(0)
                        scores(1)
                        turn(0)
                        scores(2)
                        turn(1)
                        outputs(0)
                        scores(3)
                        turn(2)
                        relative_keys(1)
                        scores(4)
                        turn(3)
                        outputs(1)
                        scores(5)
                        turn(4)
                        scores(6)
                        turn(5)
                        outputs(2)
                        scores(7)
                        turn(6)
                        turn(7)
                        outputs(3)
                        for i in (FA - 2, FA - 1):
                            pe.wait_ge(ring_free[i % 2], filled(b, i))

                @block.scalar
                def _(act):
                    with act.Fori(0, B) as b:
                        def exps(s):
                            act.wait_ge(bias_ok, b * 8 + s + 1)
                            for h in range(4):
                                last = nc.scalar.activation(
                                    probs[:, s % 2, h, :].rearrange("p (t m) -> p t m", t=LT),
                                    score[s % 2][:, :, h * P:(h + 1) * P], ACT.Exp,
                                    bias=nbias[:, s % 2, h:h + 1], scale=SCALE_A)
                            last.then_inc(exp_done, 1)

                        def turns(s):
                            act.wait_ge(turn_full, b * 8 + s + 1)
                            for mt in range(LT):
                                last = nc.scalar.copy(probsT[:, mt, :, (s % 2) * 4:(s % 2) * 4 + 4, :],
                                                      turned[mt].rearrange("p (h k l) -> p k h l", h=4, l=LB))
                            last.then_inc(turn_out, 1)

                        for s in range(8):
                            exps(s)
                            if s:
                                turns(s - 1)
                        turns(7)

                @block.vector
                def _(dve):
                    with dve.Fori(0, B) as b:
                        def take(i):
                            dve.wait_ge(ring_full[i % 2], filled(b, i))
                            return ring[i % 2]

                        def maxima(s):
                            dve.wait_ge(score_full, b * 8 + s + 1)
                            nc.vector.tensor_reduce(nmax[:, s % 2, :],
                                                    score[s % 2].rearrange("p t (h m) -> p h t m", h=4),
                                                    AX.XY, ALU.max).then_inc(row_max, 1)
                            dve.wait_ge(row_max, b * 8 + s + 1)
                            nc.vector.tensor_scalar(nbias[:, s % 2, :], nmax[:, s % 2, :], -SCALE_A, None,
                                                    ALU.mult).then_inc(bias_ok, 1)

                        def relative_keys(lt):
                            for n in range(8):
                                i, mt, lp = FRK[lt] + n, n // 4, n % 4
                                r = take(i)
                                pp = pp_tab[:, mt, lt * P + lp * 32:lt * P + lp * 32 + 32]
                                nc.vector.tensor_tensor(
                                    relk[:, mt, :, lp * 32:lp * 32 + 32].rearrange("p h (j l) -> p j h l", j=2),
                                    r.rearrange("p (j h l) -> p j h l", j=2, h=H),
                                    pp.rearrange("p (j l) -> p j l", j=2)[:, :, None, :].broadcast_to((P, 2, H, LB)),
                                    ALU.add).then_inc(ring_free[i % 2], 1)

                        def outputs(g):
                            for n in range(4):
                                i = FY[g] + n
                                r = take(i)[:, 0:386].rearrange("p (j c) -> p j c", j=2)
                                nc.vector.tensor_tensor(ymask[:, 2 * n:2 * n + 2, :], r[:, :, 1:193],
                                                        own24[:, None, :].broadcast_to((P, 2, 24 * HD)),
                                                        ALU.mult).then_inc(ymask_ok, 1)
                                nc.vector.reciprocal(rsum[:, 2 * n:2 * n + 2], r[:, :, 0]).then_inc(ring_free[i % 2], 1)
                            dve.wait_ge(ymask_ok, b * 16 + 4 * g + 4)
                            nc.vector.tensor_reduce(ysum[:, :, :], ymask[:, :, :].rearrange("p n (g d) -> p n d g", d=HD),
                                                    AX.X, ALU.add).then_inc(ysum_ok, 1)
                            dve.wait_ge(ysum_ok, b * 4 + g + 1)
                            for i in (2, 3):
                                dve.wait_ge(ring_free[i % 2], filled(b, FY[g] + i))
                            nc.vector.tensor_tensor(yout[:, bass.ds(b * 4 + g, 1), :].rearrange("p a (n d) -> p (a n) d", d=HD),
                                                    ysum[:, :, :], rsum[:, :, None].broadcast_to((P, 8, HD)),
                                                    ALU.mult).then_inc(yout_ok, 1)

                        for t in range(LT):
                            r = take(t)
                            nc.vector.tensor_copy(xT[:, t * P:(t + 1) * P], r[:, 0:P]).then_inc(ring_free[t], 1)
                        r = take(FQK)
                        nc.vector.tensor_copy(qT[:, :], r[:, 0:S])
                        nc.vector.tensor_tensor(k_diag[:, :, :], r[:, None, S:2 * S].broadcast_to((P, H, S)),
                                                gmask[:, :, None].broadcast_to((P, H, S)),
                                                ALU.mult).then_inc(ring_free[FQK % 2], 1)
                        r = take(FV)
                        nc.vector.tensor_copy(vones[:, :, :, 1:65],
                                              r[:, 0:LT * D].rearrange("p (t a c) -> p t a c", t=LT, a=2)
                                              ).then_inc(ring_free[FV % 2], 1)
                        for f, blk in ((FQB, q_blk), (FKB, k_blk)):
                            for n in range(H // 2):
                                r = take(f + n)
                                nc.vector.tensor_tensor(
                                    blk[:, 2 * n:2 * n + 2, :].rearrange("p h (n l) -> p (h n) l", l=LB),
                                    r.rearrange("p (n l) -> p n l", l=LB),
                                    gmask[:, None, :].broadcast_to((P, 2 * S // LB, LB)),
                                    ALU.mult).then_inc(ring_free[(f + n) % 2], 1)
                        relative_keys(0)
                        maxima(0)
                        maxima(1)
                        maxima(2)
                        outputs(0)
                        maxima(3)
                        relative_keys(1)
                        maxima(4)
                        outputs(1)
                        maxima(5)
                        maxima(6)
                        outputs(2)
                        maxima(7)
                        outputs(3)

                @block.sync
                def _(sp):
                    with sp.Fori(0, B) as b:
                        for g in range(4):
                            lt, hh = g // 2, g % 2
                            sp.wait_ge(yout_ok, b * 4 + g + 1)
                            for h in range(8):
                                sp.dma_start(
                                    oa[b, lt, :, :, hh, h, :].rearrange("k l d -> l k d"),
                                    yout[LB * h:LB * h + LB, b * 4 + g, :].rearrange("p (k d) -> p k d", d=HD)
                                ).then_inc(oa_st, 16)
                    sp.wait_ge(oa_st, 16 * B * 4 * 8)

        def layer_norm(tag, residual=None, load=None, keep=None, store=None):
            GT = 8
            with ExitStack() as st:
                stats = sb(st, f"{tag}_stats", [P, GT, 6])
                mv = sb(st, f"{tag}_mv", [P, GT, 2])
                var = sb(st, f"{tag}_var", [P, GT])
                rstd = sb(st, f"{tag}_rstd", [P, GT])
                added, stats_ok, mv_ok, var_ok, rstd_ok, normed, kept, loaded, stored = (
                    sem(f"{tag}_{n}") for n in ("added", "stats_ok", "mv_ok", "var_ok", "rstd_ok", "normed", "kept",
                                                "loaded", "stored"))
                with nc.Block() as block:
                    @block.sync
                    def _(sp):
                        if load is not None:
                            sp.dma_start(residual[:, :, :], load).then_inc(loaded, 16)
                        if store is not None:
                            with sp.Fori(0, NT // GT) as g:
                                sp.wait_ge(normed, (g + 1) * GT)
                                sp.dma_start(store[:, bass.ds(g * GT, GT), :],
                                             X[:, bass.ds(g * GT, GT), :]).then_inc(stored, 16)
                            sp.wait_ge(stored, 16 * (NT // GT))

                    @block.vector
                    def _(dve):
                        if load is not None:
                            dve.wait_ge(loaded, 16)
                        with dve.Fori(0, NT // GT) as g:
                            tiles = bass.ds(g * GT, GT)
                            if residual is not None:
                                nc.vector.tensor_tensor(X[:, tiles, :], X[:, tiles, :], residual[:, tiles, :],
                                                        ALU.add).then_inc(added, 1)
                                dve.wait_ge(added, g + 1)
                                nc.vector.memset(pause[:, :], 0.0)
                            for j in range(GT):
                                nc.vector.bn_stats(stats[:, j, :], X[:, bass.ds(g * GT + j, 1), :].rearrange("p a c -> p (a c)")).then_inc(stats_ok, 1)
                            dve.wait_ge(stats_ok, (g + 1) * GT)
                            nc.vector.memset(pause[:, :], 0.0)
                            for j in range(GT):
                                nc.vector.bn_aggr(mv[:, j, :], stats[:, j, :]).then_inc(mv_ok, 1)
                            dve.wait_ge(mv_ok, (g + 1) * GT)
                            nc.vector.tensor_scalar(var[:, :], mv[:, :, 1], EPS, None, ALU.add).then_inc(var_ok, 1)
                            dve.wait_ge(rstd_ok, g + 1)
                            for j in range(GT):
                                t = X[:, bass.ds(g * GT + j, 1), :].rearrange("p a c -> p (a c)")
                                nc.vector.tensor_scalar(t, t, mv[:, j, 0:1], rstd[:, j:j + 1], ALU.subtract,
                                                        ALU.mult).then_inc(normed, 1)

                    @block.gpsimd
                    def _(pool):
                        with pool.Fori(0, NT // GT) as g:
                            pool.wait_ge(var_ok, g + 1)
                            nc.gpsimd.tensor_tensor(rstd[:, :], var[:, :], neghalf[:, 0:GT],
                                                    ALU.pow).then_inc(rstd_ok, 1)

                    if keep is not None:
                        @block.scalar
                        def _(act):
                            with act.Fori(0, NT // GT) as g:
                                tiles = bass.ds(g * GT, GT)
                                act.wait_ge(normed, (g + 1) * GT)
                                nc.scalar.copy(keep[:, tiles, :], X[:, tiles, :]).then_inc(kept, 1)

        def store_stream(tag):
            done = sem(f"{tag}_done")
            with nc.Block() as block:
                @block.sync
                def _(sp):
                    sp.dma_start(out_v, X[:, :, :]).then_inc(done, 16)
                    sp.wait_ge(done, 16)

        oa_tiles = oa.rearrange("b t k l a h d -> (k l) (b t) (a h d)")
        layer_norm("ln1", residual=XR, load=oa_tiles, keep=XR)
        if stop == 1:
            return store_stream("stop")

        with ExitStack() as st:
            wqkv = sb(st, "b_wqkv", [P, 3 * INNER])
            wo = sb(st, "b_wo", [P, INNER // P, D])
            qk_gain = sb(st, "b_qk_gain", [P, 2, BD])
            cos0, sin0, cosg, sing = (sb(st, n, [P, LT, 2, BD]) for n in ("b_cos0", "b_sin0", "b_cosg", "b_sing"))
            w1 = sb(st, "b_w1", [P, 2 * FF])
            w2 = sb(st, "b_w2", [P, 3, D])
            b1 = sb(st, "b_b1", [P, 6])
            b2 = sb(st, "b_b2", [1, D])
            lng, lnb = sb(st, "b_lng", [P, 1]), sb(st, "b_lnb", [P, 1])
            shift_in, shift_over = sb(st, "b_shift_in", [P, P]), sb(st, "b_shift_over", [P, P])
            masks0 = sb(st, "b_masks0", [P, P + WIN])
            own_bf = sb(st, "b_own_bf", [P, P], BF16)
            prev_bf = sb(st, "b_prev_bf", [P, WIN], BF16)
            sq = sb(st, "b_sq", [P, 2 * 8 * BD])
            ss = sb(st, "b_ss", [P, 16])
            rnorm = sb(st, "b_rnorm", [P, 16])
            t1, t2 = sb(st, "b_t1", [P, 16, BD]), sb(st, "b_t2", [P, 16, BD])
            rot, qk = sb(st, "b_rot", [P, 16, BD]), sb(st, "b_qk", [P, 16, BD])
            v = sb(st, "b_v", [P, 4, 8, BD + 1])
            qTs = sb(st, "b_qTs", [P, 4, P])
            kz = sb(st, "b_kz", [P, LT, 4, 2, P])
            m_own, m_prev = sb(st, "b_m_own", [P, 8]), sb(st, "b_m_prev", [WIN, 8])
            pr = sb(st, "b_pr", [P, 8, P])
            pp0 = sb(st, "b_pp0", [WIN, 8, WIN])
            pp = sb(st, "b_pp", [WIN, 8, P])
            prT = sb(st, "b_prT", [P, 8, P])
            ppT = sb(st, "b_ppT", [P, 8, WIN])
            rs = sb(st, "b_rs", [P, 8])
            o = sb(st, "b_o", [P, 8, BD])
            oT = sb(st, "b_oT", [P, 4, P])
            xh = sb(st, "b_xh", [P, 2, LT, D // 2])
            xs = sb(st, "b_xs", [P, 2, LT, D])
            st6 = sb(st, "b_st6", [P, 2, LT, 6])
            mv = sb(st, "b_mv", [P, 2, LT, 2])
            fvar, frstd = sb(st, "b_fvar", [P, 2, LT]), sb(st, "b_frstd", [P, 2, LT])
            xn = sb(st, "b_xn", [P, 2, LT, D])
            xnT = sb(st, "b_xnT", [P, 2, S])
            gel = sb(st, "b_gel", [P, 2, 3, S])
            hid = sb(st, "b_hid", [P, 2, 3, S])

            c_ld, c_set, wa_ld, wf_ld = sem("b_c_ld"), sem("b_c_set"), sem("b_wa_ld"), sem("b_wf_ld")
            gains = sem("b_gains")
            x_copied, xcur_free = sem("b_x_copied"), sem("b_xcur_free")
            qk_full, v_full, sq_done, ss_done = sem("b_qk_full"), sem("b_v_full"), sem("b_sq_done"), sem("b_ss_done")
            floor_done, rn_done, t_done, rot_done, qk_done, v_done = (
                sem("b_floor_done"), sem("b_rn_done"), sem("b_t_done"), sem("b_rot_done"), sem("b_qk_done"),
                sem("b_v_done"))
            sc_full, mo_done, mp_done, mx_done, sub_done, exp_done = (
                sem("b_sc_full"), sem("b_mo_done"), sem("b_mp_done"), sem("b_mx_done"), sem("b_sub_done"),
                sem("b_exp_done"))
            rs_done, o_done, x_attn = sem("b_rs_done"), sem("b_o_done"), sem("b_x_attn")
            ring_full = [sem("b_ring_full0"), sem("b_ring_full1")]
            ring_free = [sem("b_ring_free0"), sem("b_ring_free1")]
            x_ffn, sh_copied, st_done, mv_done, var_done, rstd_done, xn_done = (
                sem("b_x_ffn"), sem("b_sh_copied"), sem("b_st_done"), sem("b_mv_done"), sem("b_var_done"),
                sem("b_rstd_done"), sem("b_xn_done"))
            hg_full, gel_done, hid_done = sem("b_hg_full"), sem("b_gel_done"), sem("b_hid_done")
            fr_full = [sem("b_fr_full0"), sem("b_fr_full1")]
            fr_free = [sem("b_fr_free0"), sem("b_fr_free1")]

            wqkv_d, wo_d = T["L0_ffn_Wqkv"], T["L0_ffn_Wo"]
            N_WA, N_WF = 4, 10
            NS = 4
            names = [("x", 0), ("x", 1)]
            for s in range(NS):
                names += [("q", s), ("k", s), ("p", s, 0), ("p", s, 1)] + ([("pp", s)] if s % 2 else []) + \
                         [("o", s, 0), ("o", s, 1), ("oT", s), ("w", s)]
            FB = len(names)
            assert FB % 2 == 0
            at = {n: i for i, n in enumerate(names)}

            with nc.Block() as block:
                @block.sync
                def _(sp):
                    for name, t in (("rot_cos", cos0), ("rot_sin", sin0)):
                        sp.dma_start(t[:, :, :, :].rearrange("p t a d -> p (t a d)"), T[name]).then_inc(c_ld, 16)
                    sp.dma_start(shift_in[:, :], T["shift_in"]).then_inc(c_ld, 16)
                    sp.dma_start(shift_over[:, :], T["shift_over"]).then_inc(c_ld, 16)
                    sp.dma_start(masks0[:, 0:P], T["window_own"]).then_inc(c_ld, 16)
                    sp.dma_start(masks0[:, P:P + WIN], T["window_prev"]).then_inc(c_ld, 16)
                    sp.wait_ge(c_ld, 96)

                @block.gpsimd
                def _(pool):
                    nc.gpsimd.memset(v[:, :, :, :], 1.0)
                    nc.gpsimd.memset(kz[:, :, :, :, :], 0.0)
                    nc.gpsimd.memset(pp[:, :, :], 0.0)

                @block.vector
                def _(dve):
                    nc.vector.memset(xT[64:128, 0:1], 0.0)
                    dve.wait_ge(c_ld, 96)
                    nc.vector.tensor_copy(own_bf[:, :], masks0[:, 0:P])
                    nc.vector.tensor_copy(prev_bf[:, :], masks0[:, P:P + WIN])

            def filled(n, i):
                return n * (FB // 2) + i // 2 + 1

            FF_FILLS = 8

            def ffilled(n, i):
                return n * (FF_FILLS // 2) + i // 2 + 1

            ring = bank[6:8]
            NP = B // 2
            with nc.Block() as block:
                @block.sync
                def _(sp):
                    with sp.Fori(0, DEPTH) as l:
                        sp.wait_ge(x_attn, l * B * NS + 1)
                        sp.dma_start(wqkv[:, :], wqkv_d[l]).then_inc(wa_ld, 16)
                        sp.dma_start(wo[:, :, :], wo_d[l].rearrange("(k p) c -> p k c", p=P)).then_inc(wa_ld, 16)
                        for i, n in enumerate(("L0_ffn_q_scale", "L0_ffn_k_scale")):
                            sp.dma_start(qk_gain[:, i, :], T[n][bass.ds(l, 1), :].broadcast_to((P, BD))).then_inc(wa_ld, 16)
                        sp.wait_ge(x_ffn, l * B + B)
                        sp.dma_start(w1[:, :], T["L0_ffn_W1"][l]).then_inc(wf_ld, 16)
                        w2_d = T["L0_ffn_W2"][l]
                        sp.dma_start(w2[:, 0:2, :], w2_d[0:256, :].rearrange("(k p) c -> p k c", p=P)).then_inc(wf_ld, 16)
                        sp.dma_start(w2[0:FCH[2], 2, :], w2_d[256:FF, :]).then_inc(wf_ld, 16)
                        for part in range(2):
                            b1_d = T["L0_ffn_b1"][l][part * FF:(part + 1) * FF]
                            sp.dma_start(b1[:, 3 * part:3 * part + 2], b1_d[0:256].rearrange("(k p) -> p k", p=P),
                                         allow_slow_non_contiguous=True).then_inc(wf_ld, 16)
                            sp.dma_start(b1[0:FCH[2], 3 * part + 2:3 * part + 3],
                                         b1_d[256:FF].rearrange("(p k) -> p k", k=1),
                                         allow_slow_non_contiguous=True).then_inc(wf_ld, 16)
                        sp.dma_start(b2[:, :], T["L0_ffn_b2"][bass.ds(l, 1), :]).then_inc(wf_ld, 16)

                @block.gpsimd
                def _(pool):
                    with pool.Fori(0, DEPTH) as l:
                        with pool.Fori(0, B) as b:
                            n = l * B + b
                            pool.wait_ge(x_ffn, n + 1)
                            nc.gpsimd.tensor_copy(xcur[:, :, :], X[:, bass.ds(b * LT, LT), :]).then_inc(x_copied, 1)
                            for s in range(NS):
                                m = n * NS + s + 1
                                pool.wait_ge(floor_done, m)
                                nc.gpsimd.tensor_tensor(rnorm[:, :], ss[:, :], neghalf[:, :], ALU.pow).then_inc(rn_done, 1)
                                pool.wait_ge(t_done, m)
                                nc.gpsimd.tensor_tensor(rot[:, :, :], t1[:, :, :], t2[:, :, :], ALU.add).then_inc(rot_done, 1)
                                pool.wait_ge(rot_done, m)
                                pool.wait_ge(rn_done, m)
                                nc.gpsimd.tensor_tensor(qk[:, :, :], rot[:, :, :],
                                                        rnorm[:, :, None].broadcast_to((P, 16, BD)),
                                                        ALU.mult).then_inc(qk_done, 1)
                            pool.wait_ge(ring_full[1], filled(n, 1))
                        with pool.Fori(0, NP) as i:
                            n = l * NP + i
                            for q in range(2):
                                pool.wait_ge(x_attn, (l * B + i * 2 + q + 1) * NS + 1)
                                t = X[:, bass.ds(i * 4 + q * 2, LT), :]
                                nc.gpsimd.tensor_copy(xh[:, q, :, :], t[:, :, D // 2:D])
                                nc.gpsimd.tensor_copy(xs[:, q, :, 0:D // 2], t[:, :, 0:D // 2]).then_inc(sh_copied, 1)
                            for q in range(2):
                                pool.wait_ge(var_done, n * 2 + q + 1)
                                nc.gpsimd.tensor_tensor(frstd[:, q, :], fvar[:, q, :], neghalf[:, 0:LT],
                                                        ALU.pow).then_inc(rstd_done, 1)
                            pool.wait_ge(xn_done, n * 4 + 4)

                @block.tensor
                def _(pe):
                    with pe.Fori(0, DEPTH) as l:
                        with pe.Fori(0, B) as b:
                            n = l * B + b
                            pe.wait_ge(wa_ld, (l + 1) * 16 * N_WA)

                            def room(name):
                                i = at[name]
                                pe.wait_ge(ring_free[i % 2], filled(n, i))
                                return ring[i % 2], ring_full[i % 2]

                            def out_of(name):
                                i = at[name]
                                pe.wait_ge(ring_free[i % 2], filled(n, i) + 1)

                            def project(s):
                                hg, t = s // 2, s % 2
                                if s:
                                    pe.wait_ge(t_done, n * NS + s)
                                    pe.wait_ge(v_done, n * NS + s)
                                for a in range(3):
                                    c = a * INNER + hg * 512
                                    last = nc.tensor.matmul(bank[a], xT[:, t * P:(t + 1) * P], wqkv[:, c:c + 512],
                                                            start=True, stop=True)
                                    if a == 1:
                                        last.then_inc(qk_full, 1)
                                last.then_inc(v_full, 1)

                            pe.wait_ge(x_copied, n + 1)
                            for t in range(LT):
                                r, full = room(("x", t))
                                nc.tensor.transpose(r[:, 0:P], xcur[:, t, :], ident[:, :]).then_inc(full, 1)
                            out_of(("x", 0))
                            out_of(("x", 1))
                            project(0)
                            for s in range(NS):
                                hg, t = s // 2, s % 2
                                m = n * NS + s + 1
                                pe.wait_ge(qk_done, m)
                                for a, name in enumerate("qk"):
                                    r, full = room((name, s))
                                    for p in range(4):
                                        last = nc.tensor.transpose(
                                            r[:, p * P:(p + 1) * P],
                                            qk[:, a * 8 + 2 * p:a * 8 + 2 * p + 2, :].rearrange("p h d -> p (h d)"),
                                            ident[:, :])
                                    last.then_inc(full, 1)
                                out_of(("q", s))
                                out_of(("k", s))
                                for half in range(2):
                                    sc = bank[3 + half]
                                    nc.tensor.matmul(sc.rearrange("p (h j) -> p h j", h=4), ident_bf[:, :],
                                                     own_bf[:, None, :].broadcast_to((P, 4, P)),
                                                     start=True, stop=False, skip_group_check=True)
                                    for p in range(2):
                                        last = nc.tensor.matmul(
                                            sc[:, p * 2 * P:(p + 1) * 2 * P], qTs[:, 2 * half + p, :],
                                            kz[:, t, 2 * half + p, :, :].rearrange("p h j -> p (h j)"),
                                            start=False, stop=(p == 1), skip_group_check=True)
                                if t:
                                    sc = bank[5][:, 0:8 * WIN]
                                    nc.tensor.matmul(sc.rearrange("p (h j) -> p h j", h=8), ident_bf[:, :],
                                                     prev_bf[:, None, :].broadcast_to((P, 8, WIN)),
                                                     start=True, stop=False, skip_group_check=True)
                                    for p in range(4):
                                        last = nc.tensor.matmul(
                                            sc[:, p * 2 * WIN:(p + 1) * 2 * WIN].rearrange("p (h j) -> p h j", h=2),
                                            qTs[:, p, :], kz[:, 0, p, :, P - WIN:P],
                                            start=False, stop=(p == 3), skip_group_check=True)
                                last.then_inc(sc_full, 1)
                                if s + 1 < NS:
                                    project(s + 1)
                                pe.wait_ge(exp_done, m)
                                for half in range(2):
                                    r, full = room(("p", s, half))
                                    for h in range(4):
                                        last = nc.tensor.transpose(r[:, h * P:(h + 1) * P], pr[:, 4 * half + h, :],
                                                                   ident[:, :])
                                    last.then_inc(full, 1)
                                if t:
                                    r, full = room(("pp", s))
                                    nc.tensor.matmul(r[:, 0:WIN], pp[:, 0, :], ident[0:WIN, 0:WIN], start=True, stop=True)
                                    for h in range(1, 8):
                                        last = nc.tensor.transpose(r[:, h * WIN:(h + 1) * WIN], pp[:, h, :],
                                                                   ident[0:WIN, 0:WIN])
                                    last.then_inc(full, 1)
                                for half in range(2):
                                    out_of(("p", s, half))
                                    if t and not half:
                                        out_of(("pp", s))
                                    if not half:
                                        pe.wait_ge(v_done, m)
                                    r, full = room(("o", s, half))
                                    for h in range(4):
                                        hh = 4 * half + h
                                        c = slice(h * (BD + 1), (h + 1) * (BD + 1))
                                        last = nc.tensor.matmul(r[:, c], prT[:, hh, :], v[:, s, hh, :],
                                                                start=(h == 0), stop=(h == 3 and not t),
                                                                skip_group_check=True)
                                    if t:
                                        for h in range(4):
                                            hh = 4 * half + h
                                            c = slice(h * (BD + 1), (h + 1) * (BD + 1))
                                            last = nc.tensor.matmul(r[0:WIN, c], ppT[:, hh, :], v[:, s - 1, hh, :],
                                                                    start=False, stop=(h == 3), skip_group_check=True)
                                    last.then_inc(full, 1)
                                pe.wait_ge(o_done, 2 * m)
                                r, full = room(("oT", s))
                                for p in range(4):
                                    last = nc.tensor.transpose(
                                        r[:, p * P:(p + 1) * P],
                                        o[:, 2 * p:2 * p + 2, :].rearrange("p h d -> p (h d)"), ident[:, :])
                                last.then_inc(full, 1)
                                out_of(("oT", s))
                                r, full = room(("w", s))
                                for p in range(4):
                                    last = nc.tensor.matmul(r[:, 0:D], oT[:, p, :], wo[:, 4 * hg + p, :],
                                                            start=(p == 0), stop=(p == 3))
                                last.then_inc(full, 1)
                        with pe.Fori(0, NP) as i:
                            n = l * NP + i
                            for j in (FB - 2, FB - 1):
                                pe.wait_ge(ring_free[j % 2], filled(l * B + B - 1, j) + 1)
                            pe.wait_ge(wf_ld, (l + 1) * 16 * N_WF)

                            def room(j):
                                pe.wait_ge(fr_free[j % 2], ffilled(n, j))
                                return ring[j % 2], fr_full[j % 2]

                            def out_of(j):
                                pe.wait_ge(fr_free[j % 2], ffilled(n, j) + 1)

                            for q in range(2):
                                pe.wait_ge(sh_copied, n * 2 + q + 1)
                                r, full = room(q)
                                nc.tensor.matmul(r[:, 0:64], shift_in[:, :], xh[:, q, 0, :], start=True, stop=False,
                                                 skip_group_check=True)
                                nc.tensor.matmul(r[:, 64:128], shift_in[:, :], xh[:, q, 1, :], start=False, stop=False,
                                                 skip_group_check=True)
                                nc.tensor.matmul(r[:, 64:128], shift_over[:, :], xh[:, q, 0, :], start=False, stop=True,
                                                 skip_group_check=True).then_inc(full, 1)
                            for q in range(2):
                                pe.wait_ge(xn_done, n * 4 + 2 * q + 2)
                                r, full = room(2 + q)
                                for t in range(LT):
                                    last = nc.tensor.transpose(r[:, t * P:(t + 1) * P], xn[:, q, t, :], ident[:, :])
                                last.then_inc(full, 1)
                            for q in range(2):
                                out_of(2 + q)
                                for k, (c0, c1) in enumerate(((3, 4), (0, 1), (5, 2))):
                                    r = bank[3 * q + k]
                                    for j, c in enumerate((c0, c1)):
                                        w, f = FCH[c % 3], (c // 3) * FF + 128 * (c % 3)
                                        last = nc.tensor.matmul(r[0:w, j * S:(j + 1) * S], w1[:, f:f + w], xnT[:, q, :],
                                                                start=(j == 0), stop=(j == 1), skip_group_check=True)
                                    last.then_inc(hg_full, 1)
                            for q in range(2):
                                pe.wait_ge(hid_done, n * 2 + q + 1)
                                for t in range(LT):
                                    r, full = room(4 + 2 * q + t)
                                    for c in range(3):
                                        nc.tensor.matmul(r[:, 0:D], hid[0:FCH[c], q, c, t * P:(t + 1) * P],
                                                         w2[0:FCH[c], c, :], start=(c == 0), stop=False)
                                    nc.tensor.matmul(r[:, 0:D], ones[0:1, :], b2[:, :], start=False,
                                                     stop=True).then_inc(full, 1)
                        for i in (FF_FILLS - 2, FF_FILLS - 1):
                            pe.wait_ge(fr_free[i % 2], ffilled(l * NP + NP - 1, i) + 1)

                @block.scalar
                def _(act):
                    with act.Fori(0, DEPTH) as l:
                        act.wait_ge(x_ffn, l * B + B)
                        act.dma_start(lng[:, :], T["L0_ffn_ln_g"][bass.ds(l, 1), :].rearrange("a c -> c a"),
                                      allow_slow_non_contiguous=True).then_inc(wf_ld, 16)
                        act.dma_start(lnb[:, :], T["L0_ffn_ln_b"][bass.ds(l, 1), :].rearrange("a c -> c a"),
                                      allow_slow_non_contiguous=True).then_inc(wf_ld, 16)
                        with act.Fori(0, B) as b:
                            n = l * B + b

                            def take(name):
                                i = at[name]
                                act.wait_ge(ring_full[i % 2], filled(n, i))
                                return ring[i % 2], ring_free[i % 2]

                            def squares(s):
                                m = n * NS + s + 1
                                act.wait_ge(qk_full, m)
                                nc.scalar.activation(sq[:, :], psum[:, 0:2, :].rearrange("p a c -> p (a c)"),
                                                     ACT.Square).then_inc(sq_done, 1)
                                act.wait_ge(v_full, m)
                                nc.scalar.copy(v[:, s, :, 0:BD],
                                               bank[2].rearrange("p (h d) -> p h d", h=8)).then_inc(v_done, 1)

                            r, free = take(("x", 0))
                            nc.scalar.copy(xT[0:64, 0:P], r[0:64, 0:P])
                            nc.scalar.copy(xT[64:128, 1:P + 1], r[64:128, 0:P]).then_inc(free, 1)
                            r, free = take(("x", 1))
                            nc.scalar.copy(xT[0:64, P:S], r[0:64, 0:P])
                            nc.scalar.copy(xT[64:128, P + 1:S], r[64:128, 0:P - 1]).then_inc(free, 1)
                            squares(0)
                            for s in range(NS):
                                t = s % 2
                                m = n * NS + s + 1
                                r, free = take(("q", s))
                                nc.scalar.copy(qTs[:, :, :], r.rearrange("p (a i) -> p a i", a=4)).then_inc(free, 1)
                                r, free = take(("k", s))
                                for j in range(2):
                                    last = nc.scalar.copy(kz[64 * j:64 * j + 64, t, :, j, :],
                                                          r[64 * j:64 * j + 64, :].rearrange("p (a i) -> p a i", a=4))
                                last.then_inc(free, 1)
                                if s + 1 < NS:
                                    squares(s + 1)
                                act.wait_ge(sub_done, m)
                                if t:
                                    nc.scalar.activation(pp[:, :, P - WIN:P], pp0[:, :, :], ACT.Exp)
                                nc.scalar.activation(pr[:, :, :], pr[:, :, :], ACT.Exp).then_inc(exp_done, 1)
                                for half in range(2):
                                    r, free = take(("p", s, half))
                                    nc.scalar.copy(prT[:, 4 * half:4 * half + 4, :],
                                                   r.rearrange("p (h i) -> p h i", h=4)).then_inc(free, 1)
                                if t:
                                    r, free = take(("pp", s))
                                    nc.scalar.copy(ppT[:, :, :], r[:, 0:8 * WIN].rearrange("p (h i) -> p h i", h=8)
                                                   ).then_inc(free, 1)
                                r, free = take(("oT", s))
                                nc.scalar.copy(oT[:, :, :], r.rearrange("p (a i) -> p a i", a=4)).then_inc(free, 1)
                        with act.Fori(0, NP) as i:
                            n = l * NP + i
                            act.wait_ge(wf_ld, (l + 1) * 16 * N_WF)

                            def take(j):
                                act.wait_ge(fr_full[j % 2], ffilled(n, j))
                                return ring[j % 2], fr_free[j % 2]

                            for q in range(2):
                                r, free = take(q)
                                act.wait_ge(sh_copied, n * 2 + q + 1)
                                nc.scalar.copy(xs[:, q, :, D // 2:D],
                                               r[:, 0:P].rearrange("p (t c) -> p t c", t=LT)).then_inc(free, 1)
                            for q in range(2):
                                r, free = take(2 + q)
                                nc.scalar.activation(xnT[:, q, :], r[:, 0:S], ACT.Identity, bias=lnb[:, 0:1],
                                                     scale=lng[:, 0:1]).then_inc(free, 1)
                            for q in range(2):
                                for k, c in ((0, 0), (0, 1), (2, 2)):
                                    act.wait_ge(hg_full, n * 6 + 3 * q + k + 1)
                                    w = FCH[c]
                                    r = bank[3 * q + k][0:w, (c % 2) * S:(c % 2) * S + S]
                                    last = nc.scalar.activation(gel[0:w, q, c, :], r, ACT.Gelu,
                                                                bias=b1[0:w, 3 + c:4 + c])
                                last.then_inc(gel_done, 1)

                @block.vector
                def _(dve):
                    for f in (*ring_free, *fr_free):
                        dve.sem_inc(f, 1)
                    dve.sem_inc(x_ffn, B)
                    dve.sem_inc(x_attn, 1)
                    with dve.Fori(0, DEPTH) as l:
                        dve.wait_ge(wa_ld, (l + 1) * 16 * N_WA)
                        g2 = lambda c: qk_gain[:, None, :, c].broadcast_to((P, LT, 2, BD if c == slice(0, BD) else BD // 2))
                        lo, hi = slice(0, BD // 2), slice(BD // 2, BD)
                        nc.vector.tensor_tensor(cosg[:, :, :, :], cos0[:, :, :, :], g2(slice(0, BD)), ALU.mult).then_inc(gains, 1)
                        nc.vector.tensor_tensor(sing[:, :, :, lo], sin0[:, :, :, lo], g2(hi), ALU.mult).then_inc(gains, 1)
                        nc.vector.tensor_tensor(sing[:, :, :, hi], sin0[:, :, :, hi], g2(lo), ALU.mult).then_inc(gains, 1)
                        with dve.Fori(0, B) as b:
                            n = l * B + b
                            dve.wait_ge(gains, l * 3 + 3)

                            def take(name):
                                i = at[name]
                                dve.wait_ge(ring_full[i % 2], filled(n, i))
                                return ring[i % 2], ring_free[i % 2]

                            def rotate(s):
                                t, m = s % 2, n * NS + s + 1
                                dve.wait_ge(sq_done, m)
                                nc.vector.tensor_reduce(ss[:, :], sq[:, :].rearrange("p (h d) -> p h d", d=BD), AX.X,
                                                        ALU.add).then_inc(ss_done, 1)
                                dve.wait_ge(ss_done, m)
                                nc.vector.tensor_scalar(ss[:, :], ss[:, :], 1e-24, None, ALU.max).then_inc(floor_done, 1)
                                x4 = psum[:, 0:2, :].rearrange("p a (h d) -> p a h d", d=BD)
                                t14 = t1[:, :, :].rearrange("p (a h) d -> p a h d", a=2)
                                t24 = t2[:, :, :].rearrange("p (a h) d -> p a h d", a=2)
                                tab = lambda g, c, w: g[:, t, :, None, c].broadcast_to((P, 2, 8, w))
                                nc.vector.tensor_tensor(t14, x4, tab(cosg, slice(0, BD), BD), ALU.mult)
                                nc.vector.tensor_tensor(t24[:, :, :, lo], x4[:, :, :, hi], tab(sing, lo, BD // 2), ALU.mult)
                                nc.vector.tensor_tensor(t24[:, :, :, hi], x4[:, :, :, lo], tab(sing, hi, BD // 2),
                                                        ALU.mult).then_inc(t_done, 1)

                            rotate(0)
                            for s in range(NS):
                                t, m = s % 2, n * NS + s + 1
                                dve.wait_ge(sc_full, m)
                                own = psum[:, 3:5, :].rearrange("p a (h j) -> p (a h) j", h=4)
                                nc.vector.tensor_reduce(m_own[:, :], own, AX.X, ALU.max).then_inc(mo_done, 1)
                                if t:
                                    prev = bank[5][0:WIN, 0:8 * WIN].rearrange("p (h j) -> p h j", h=8)
                                    nc.vector.tensor_reduce(m_prev[:, :], prev, AX.X, ALU.max).then_inc(mp_done, 1)
                                    dve.wait_ge(mo_done, m)
                                    dve.wait_ge(mp_done, n * 2 + s // 2 + 1)
                                    nc.vector.tensor_tensor(m_own[0:WIN, :], m_own[0:WIN, :], m_prev[:, :],
                                                            ALU.max).then_inc(mx_done, 1)
                                    dve.wait_ge(mx_done, n * 2 + s // 2 + 1)
                                    nc.vector.tensor_tensor(pp0[:, :, :], prev,
                                                            m_own[0:WIN, :, None].broadcast_to((WIN, 8, WIN)),
                                                            ALU.subtract)
                                else:
                                    dve.wait_ge(mo_done, m)
                                nc.vector.tensor_tensor(pr[:, :, :], own, m_own[:, :, None].broadcast_to((P, 8, P)),
                                                        ALU.subtract).then_inc(sub_done, 1)
                                if s + 1 < NS:
                                    rotate(s + 1)
                                for half in range(2):
                                    r, free = take(("o", s, half))
                                    r4 = r[:, 0:4 * (BD + 1)].rearrange("p (h d) -> p h d", h=4)
                                    hs = slice(4 * half, 4 * half + 4)
                                    nc.vector.reciprocal(rs[:, hs], r4[:, :, BD]).then_inc(rs_done, 1)
                                    dve.wait_ge(rs_done, 2 * (m - 1) + half + 1)
                                    nc.vector.tensor_tensor(o[:, hs, :], r4[:, :, 0:BD],
                                                            rs[:, hs, None].broadcast_to((P, 4, BD)),
                                                            ALU.mult).then_inc(o_done, 1)
                                    dve.wait_ge(o_done, 2 * (m - 1) + half + 1)
                                    dve.sem_inc(free, 1)
                                r, free = take(("w", s))
                                xt = X[:, bass.ds(b * LT + t, 1), :].rearrange("p a c -> p (a c)")
                                nc.vector.tensor_tensor(xt, r[:, 0:D], xt, ALU.add).then_inc(x_attn, 1)
                                dve.wait_ge(x_attn, m + 1)
                                dve.sem_inc(free, 1)
                        with dve.Fori(0, NP) as i:
                            n = l * NP + i
                            dve.wait_ge(wf_ld, (l + 1) * 16 * N_WF)
                            for q in range(2):
                                dve.wait_ge(fr_free[q], ffilled(n, q) + 1)
                                dve.wait_ge(sh_copied, n * 2 + q + 1)
                                nc.vector.memset(pause[:, :], 0.0)
                                for t in range(LT):
                                    nc.vector.bn_stats(st6[:, q, t, :], xs[:, q, t, :]).then_inc(st_done, 1)
                                dve.wait_ge(st_done, n * 4 + 2 * q + 2)
                                nc.vector.memset(pause[:, :], 0.0)
                                for t in range(LT):
                                    nc.vector.bn_aggr(mv[:, q, t, :], st6[:, q, t, :]).then_inc(mv_done, 1)
                                dve.wait_ge(mv_done, n * 4 + 2 * q + 2)
                                nc.vector.tensor_scalar(fvar[:, q, :], mv[:, q, :, 1], EPS, None,
                                                        ALU.add).then_inc(var_done, 1)
                            for q in range(2):
                                dve.wait_ge(rstd_done, n * 2 + q + 1)
                                for t in range(LT):
                                    nc.vector.tensor_scalar(xn[:, q, t, :], xs[:, q, t, :], mv[:, q, t, 0:1],
                                                            frstd[:, q, t:t + 1], ALU.subtract,
                                                            ALU.mult).then_inc(xn_done, 1)
                            for q in range(2):
                                dve.wait_ge(hg_full, n * 6 + 3 * q + 3)
                                dve.wait_ge(gel_done, n * 2 + q + 1)
                                for c in range(3):
                                    w = FCH[c]
                                    r = bank[3 * q + (2 if c == 2 else 1)]
                                    r = r[0:w, S:2 * S] if c in (1, 2) else r[0:w, 0:S]
                                    last = nc.vector.scalar_tensor_tensor(
                                        out=hid[0:w, q, c, :], in0=r, scalar=b1[0:w, c:c + 1],
                                        in1=gel[0:w, q, c, :], op0=ALU.add, op1=ALU.mult)
                                last.then_inc(hid_done, 1)
                            for q in range(2):
                                for t in range(LT):
                                    j = 4 + 2 * q + t
                                    dve.wait_ge(fr_full[j % 2], ffilled(n, j))
                                    xt = X[:, bass.ds(i * 4 + q * 2 + t, 1), :].rearrange("p a c -> p (a c)")
                                    last = nc.vector.tensor_tensor(xt, ring[j % 2][:, 0:D], xt, ALU.add)
                                    last.then_inc(fr_free[j % 2], 1)
                                    dve.wait_ge(fr_free[j % 2], ffilled(n, j) + 1)
                                dve.sem_inc(x_ffn, 1)

        layer_norm("ln2", residual=XR)
        if stop == 2:
            return store_stream("stop")

        with ExitStack() as st:
            wqkv_c = sb(st, "c_wqkv", [P, 3 * D])
            bias_q, bias_k = sb(st, "c_bias_q", [P, 1]), sb(st, "c_bias_k", [P, 1])
            bias_v, bias_o = sb(st, "c_bias_v", [1, D]), sb(st, "c_bias_o", [1, D])
            wout = sb(st, "c_wout", [P, D])
            kmask = sb(st, "c_kmask", [P, H])
            mask0 = sb(st, "c_mask0", [P, P])
            mask_in, mask_all = sb(st, "c_mask_in", [P, P], BF16), sb(st, "c_mask_all", [P, P], BF16)
            ident80 = sb(st, "c_ident80", [P, P], BF16)
            qT = sb(st, "c_qT", [P, S])
            k_diag = sb(st, "c_k_diag", [P, H, S])
            vones = sb(st, "c_vones", [P, LT, H, HD + 1])
            probs = sb(st, "c_probs", [P, 2, 4, S])
            probsT = sb(st, "c_probsT", [P, LT, LT, H, P])
            nmax = sb(st, "c_nmax", [P, 2, 4])
            rsum = sb(st, "c_rsum", [P, H])
            o = sb(st, "c_o", [P, H, HD])
            oT = sb(st, "c_oT", [P, P])

            ld, cset = sem("c_ld"), sem("c_set")
            with nc.Block() as block:
                @block.sync
                def _(sp):
                    bq = T["L1_attn_bqkv"]
                    sp.dma_start(wqkv_c[:, :], T["L1_attn_Wqkv"]).then_inc(ld, 16)
                    sp.dma_start(wout[:, :], T["L1_attn_Wout"]).then_inc(ld, 16)
                    sp.dma_start(bias_q[:, :], bq[0:D].rearrange("(p a) -> p a", a=1),
                                 allow_slow_non_contiguous=True).then_inc(ld, 16)
                    sp.dma_start(bias_k[:, :], bq[D:2 * D].rearrange("(p a) -> p a", a=1),
                                 allow_slow_non_contiguous=True).then_inc(ld, 16)
                    sp.dma_start(bias_v[:, :], bq[2 * D:3 * D].rearrange("(a p) -> a p", a=1)).then_inc(ld, 16)
                    sp.dma_start(bias_o[:, :], T["L1_attn_bout"].rearrange("(a p) -> a p", a=1)).then_inc(ld, 16)
                    sp.dma_start(mask0[:, :], T["causal"]).then_inc(ld, 16)
                    sp.wait_ge(ld, 16 * 7)

                @block.gpsimd
                def _(pool):
                    nc.gpsimd.memset(vones[:, :, :, :], 1.0)

                @block.vector
                def _(dve):
                    nc.vector.memset(mask_all[:, :], -125.0)
                    nc.vector.tensor_scalar(ident80[:, :], ident[:, :], 80.0, None, ALU.mult)
                    nc.vector.tensor_scalar(kmask[:, :], gmask[:, :], SCALE_A, None, ALU.mult)
                    dve.wait_ge(ld, 16 * 7)
                    nc.vector.tensor_copy(mask_in[:, :], mask0[:, :])

            names = [("x", 0), ("x", 1), "qk", "v"] + [(k, t) for t in range(LT) for k in ("o", "oT", "w")]
            FC = len(names)
            assert FC % 2 == 0
            at_c = {n: i for i, n in enumerate(names)}
            ring, score, turned = bank[0:2], [psum[:, 2:4, :], psum[:, 4:6, :]], bank[6:8]
            x_copied, ring_full, ring_free = sem("c_x_copied"), [sem("c_ring_full0"), sem("c_ring_full1")], \
                [sem("c_ring_free0"), sem("c_ring_free1")]
            score_full, max_ok, exp_done = sem("c_score_full"), sem("c_max_ok"), sem("c_exp_done")
            turn_full, turn_out, rsum_ok, o_ok = sem("c_turn_full"), sem("c_turn_out"), sem("c_rsum_ok"), sem("c_o_ok")

            def filled_c(b, i):
                return b * (FC // 2) + i // 2 + 1

            with nc.Block() as block:
                @block.gpsimd
                def _(pool):
                    with pool.Fori(0, B) as b:
                        nc.gpsimd.tensor_copy(xcur[:, :, :], X[:, bass.ds(b * LT, LT), :]).then_inc(x_copied, 1)
                        pool.wait_ge(ring_full[1], filled_c(b, 1))

                @block.tensor
                def _(pe):
                    with pe.Fori(0, B) as b:
                        def room(name):
                            i = at_c[name]
                            if i >= 2:
                                pe.wait_ge(ring_free[i % 2], filled_c(b, i - 2))
                            return ring[i % 2], ring_full[i % 2]

                        def out_of(name):
                            i = at_c[name]
                            pe.wait_ge(ring_free[i % 2], filled_c(b, i))

                        def scores(s):
                            lt, hq = s // 4, s % 4
                            if s >= 2:
                                pe.wait_ge(exp_done, b * 8 + s - 1)
                            for mt in range(LT):
                                sc = score[s % 2][:, mt, :]
                                last = nc.tensor.matmul(sc.rearrange("p (h m) -> p h m", h=4),
                                                        qT[:, lt * P:(lt + 1) * P],
                                                        k_diag[:, hq * 4:hq * 4 + 4, mt * P:(mt + 1) * P],
                                                        start=True, stop=(mt < lt), skip_group_check=True)
                                if mt >= lt:
                                    mask = mask_in if mt == lt else mask_all
                                    last = nc.tensor.matmul(sc.rearrange("p (h m) -> p h m", h=4), ident80[:, :],
                                                            mask[:, None, :].broadcast_to((P, 4, P)),
                                                            start=False, stop=True, skip_group_check=True)
                            last.then_inc(score_full, 1)

                        def turn(s):
                            pe.wait_ge(exp_done, b * 8 + s + 1)
                            if s >= 1:
                                pe.wait_ge(turn_out, b * 8 + s)
                            for mt in range(LT):
                                for h in range(4):
                                    last = nc.tensor.transpose(turned[mt][:, h * P:(h + 1) * P],
                                                               probs[:, s % 2, h, mt * P:(mt + 1) * P], ident[:, :])
                            last.then_inc(turn_full, 1)

                        def outputs(lt):
                            pe.wait_ge(turn_out, b * 8 + 4 * lt + 4)
                            r, full = room(("o", lt))
                            for h in range(H):
                                for mt in range(LT):
                                    last = nc.tensor.matmul(r[:, h * (HD + 1):(h + 1) * (HD + 1)],
                                                            probsT[:, lt, mt, h, :], vones[:, mt, h, :],
                                                            start=(h == 0 and mt == 0), stop=(h == H - 1 and mt == 1),
                                                            skip_group_check=True)
                            last.then_inc(full, 1)

                        def turn_outputs(lt):
                            pe.wait_ge(o_ok, b * LT + lt + 1)
                            r, full = room(("oT", lt))
                            nc.tensor.transpose(r[:, 0:P], o[:, :, :].rearrange("p h d -> p (h d)"),
                                                ident[:, :]).then_inc(full, 1)

                        def project(lt):
                            out_of(("oT", lt))
                            r, full = room(("w", lt))
                            nc.tensor.matmul(r[:, 0:D], oT[:, :], wout[:, :], start=True, stop=False)
                            nc.tensor.matmul(r[:, 0:D], ones[0:1, :], bias_o[:, :], start=False,
                                             stop=True).then_inc(full, 1)

                        pe.wait_ge(x_copied, b + 1)
                        for t in range(LT):
                            r, full = room(("x", t))
                            nc.tensor.transpose(r[:, 0:P], xcur[:, t, :], ident[:, :]).then_inc(full, 1)
                        r, full = room("qk")
                        out_of(("x", 1))
                        nc.tensor.matmul(r[:, 0:S], wqkv_c[:, 0:D], xT[:, :], start=True, stop=False,
                                         skip_group_check=True)
                        nc.tensor.matmul(r[:, S:2 * S], wqkv_c[:, D:2 * D], xT[:, :], start=False, stop=True,
                                         skip_group_check=True).then_inc(full, 1)
                        r, full = room("v")
                        for t in range(LT):
                            c = slice(t * D, (t + 1) * D)
                            nc.tensor.matmul(r[:, c], xT[:, t * P:(t + 1) * P], wqkv_c[:, 2 * D:3 * D],
                                             start=(t == 0), stop=False, skip_group_check=True)
                            last = nc.tensor.matmul(r[:, c], ones[0:1, :], bias_v[:, :], start=False, stop=(t == 1),
                                                    skip_group_check=True)
                        last.then_inc(full, 1)
                        out_of("qk")
                        scores(0)
                        scores(1)
                        turn(0)
                        scores(2)
                        turn(1)
                        scores(3)
                        turn(2)
                        scores(4)
                        turn(3)
                        out_of("v")
                        outputs(0)
                        scores(5)
                        turn(4)
                        turn_outputs(0)
                        scores(6)
                        turn(5)
                        project(0)
                        scores(7)
                        turn(6)
                        turn(7)
                        outputs(1)
                        turn_outputs(1)
                        project(1)
                        for i in (FC - 2, FC - 1):
                            pe.wait_ge(ring_free[i % 2], filled_c(b, i))

                @block.scalar
                def _(act):
                    with act.Fori(0, B) as b:
                        def exps(s):
                            act.wait_ge(max_ok, b * 8 + s + 1)
                            for h in range(4):
                                last = nc.scalar.activation(
                                    probs[:, s % 2, h, :].rearrange("p (t m) -> p t m", t=LT),
                                    score[s % 2][:, :, h * P:(h + 1) * P], ACT.Exp, bias=nmax[:, s % 2, h:h + 1])
                            last.then_inc(exp_done, 1)

                        def turns(s):
                            lt, hq = s // 4, s % 4
                            act.wait_ge(turn_full, b * 8 + s + 1)
                            for mt in range(LT):
                                last = nc.scalar.copy(probsT[:, lt, mt, hq * 4:hq * 4 + 4, :],
                                                      turned[mt].rearrange("p (h l) -> p h l", h=4))
                            last.then_inc(turn_out, 1)

                        for s in range(8):
                            exps(s)
                            if s:
                                turns(s - 1)
                        turns(7)

                @block.vector
                def _(dve):
                    with dve.Fori(0, B) as b:
                        def take(name):
                            i = at_c[name]
                            dve.wait_ge(ring_full[i % 2], filled_c(b, i))
                            return ring[i % 2], ring_free[i % 2]

                        def maxima(s):
                            dve.wait_ge(score_full, b * 8 + s + 1)
                            nc.vector.tensor_reduce(nmax[:, s % 2, :],
                                                    score[s % 2].rearrange("p t (h m) -> p h t m", h=4),
                                                    AX.XY, ALU.max, negate=True).then_inc(max_ok, 1)

                        def outputs(lt):
                            r, free = take(("o", lt))
                            r3 = r[:, 0:H * (HD + 1)].rearrange("p (h d) -> p h d", h=H)
                            nc.vector.reciprocal(rsum[:, :], r3[:, :, 0]).then_inc(rsum_ok, 1)
                            dve.wait_ge(rsum_ok, b * LT + lt + 1)
                            nc.vector.tensor_tensor(o[:, :, :], r3[:, :, 1:HD + 1],
                                                    rsum[:, :, None].broadcast_to((P, H, HD)),
                                                    ALU.mult).then_inc(o_ok, 1)
                            dve.wait_ge(o_ok, b * LT + lt + 1)
                            dve.sem_inc(free, 1)

                        def turn_outputs(lt):
                            r, free = take(("oT", lt))
                            nc.vector.tensor_copy(oT[:, :], r[:, 0:P]).then_inc(free, 1)

                        def project(lt):
                            r, free = take(("w", lt))
                            xt = X[:, bass.ds(b * LT + lt, 1), :].rearrange("p a c -> p (a c)")
                            nc.vector.tensor_tensor(xt, r[:, 0:D], xt, ALU.add).then_inc(free, 1)

                        for t in range(LT):
                            r, free = take(("x", t))
                            nc.vector.tensor_copy(xT[:, t * P:(t + 1) * P], r[:, 0:P]).then_inc(free, 1)
                        r, free = take("qk")
                        nc.vector.tensor_scalar(qT[:, :], r[:, 0:S], bias_q[:, 0:1], None, ALU.add)
                        nc.vector.scalar_tensor_tensor(out=k_diag[:, :, :], in0=r[:, None, S:2 * S].broadcast_to((P, H, S)),
                                                       scalar=bias_k[:, 0:1], in1=kmask[:, :, None].broadcast_to((P, H, S)),
                                                       op0=ALU.add, op1=ALU.mult).then_inc(free, 1)
                        r, free = take("v")
                        nc.vector.tensor_copy(vones[:, :, :, 1:HD + 1],
                                              r[:, 0:LT * D].rearrange("p (t h d) -> p t h d", t=LT, h=H)
                                              ).then_inc(free, 1)
                        for s in range(5):
                            maxima(s)
                        outputs(0)
                        maxima(5)
                        turn_outputs(0)
                        maxima(6)
                        project(0)
                        maxima(7)
                        outputs(1)
                        turn_outputs(1)
                        project(1)

        layer_norm("ln3")
        if stop == 3:
            return store_stream("stop")

        with ExitStack() as st:
            gate_w = sb(st, "d_gate_w", [P, NEXP])
            w1 = sb(st, "d_w1", [P, NEXP, EH])
            b1 = sb(st, "d_b1", [P, NPR])
            w2 = sb(st, "d_w2", [P, NPR, D])
            b2 = sb(st, "d_b2", [NEXP, D])
            rows = sb(st, "d_rows", [NEXP, NPR, P])
            lower = sb(st, "d_lower", [P, NEXP, NEXP])
            xT_all = sb(st, "d_xT_all", [P, B * S])
            gmax, gsum, grec, tokw = (sb(st, n, [P, 1]) for n in ("d_gmax", "d_gsum", "d_grec", "d_tokw"))
            gexp, gate, rank, sel = (sb(st, n, [P, NEXP]) for n in ("d_gexp", "d_gate", "d_rank", "d_sel"))
            above, equal = (sb(st, n, [P, NEXP, NEXP]) for n in ("d_above", "d_equal"))
            coef = sb(st, "d_coef", [P, LT, NEXP])
            coefT_all = sb(st, "d_coefT_all", [NEXP, B * S])
            coefT = sb(st, "d_coefT", [NEXP, S])
            hid = sb(st, "d_hid", [P, NPR, S])
            hidw = sb(st, "d_hidw", [P, NPR, S])

            ld = sem("d_ld")
            x_copied, xT_full, xT_ok, lg_full, ct_full, ct_ok = (
                sem(f"d_{n}") for n in ("x_copied", "xT_full", "xT_ok", "lg_full", "ct_full", "ct_ok"))
            max_ok, exp_ok, rec_ok, gate_ok, cmp_ok, rank_ok, sel_ok, tokw_ok, coef_ok, kept_ok = (
                sem(f"d_{n}") for n in ("max_ok", "exp_ok", "rec_ok", "gate_ok", "cmp_ok", "rank_ok", "sel_ok",
                                        "tokw_ok", "coef_ok", "kept_ok"))
            with nc.Block() as block:
                @block.sync
                def _(sp):
                    sp.dma_start(gate_w[:, :], T["L1_ffn_gate_w"]).then_inc(ld, 16)
                    sp.dma_start(lower[:, :, :].rearrange("p a c -> p (a c)"), T["lower"]).then_inc(ld, 16)
                    sp.dma_start(w1[:, :, :], T["L1_ffn_w1"].rearrange("e d h -> d e h")).then_inc(ld, 16)
                    sp.dma_start(b1[:, :], T["L1_ffn_b1"].rearrange("(a e) h -> (e h) a", e=2),
                                 allow_slow_non_contiguous=True).then_inc(ld, 16)
                    sp.dma_start(w2[:, :, :], T["L1_ffn_w2"].rearrange("(a e) h d -> (e h) a d", e=2)).then_inc(ld, 16)
                    sp.dma_start(b2[:, :], T["L1_ffn_b2"]).then_inc(ld, 16)
                    sp.dma_start(rows[:, :, :].rearrange("p a c -> p (a c)"), T["expert_rows"]).then_inc(ld, 16)
                    sp.wait_ge(ld, 16 * 7)

            xT_b, lg_b, ct_b = bank[0], bank[1], bank[2]
            with nc.Block() as block:
                @block.gpsimd
                def _(pool):
                    with pool.Fori(0, B) as b:
                        nc.gpsimd.tensor_copy(xcur[:, :, :], X[:, bass.ds(b * LT, LT), :]).then_inc(x_copied, 1)
                        pool.wait_ge(xT_full, b + 1)

                @block.tensor
                def _(pe):
                    with pe.Fori(0, B) as b:
                        pe.wait_ge(x_copied, b + 1)
                        for t in range(LT):
                            last = nc.tensor.transpose(xT_b[:, t * P:(t + 1) * P], xcur[:, t, :], ident[:, :])
                        last.then_inc(xT_full, 1)
                        pe.wait_ge(xT_ok, b + 1)
                        for t in range(LT):
                            last = nc.tensor.matmul(lg_b[:, t * NEXP:(t + 1) * NEXP], xT[:, t * P:(t + 1) * P],
                                                    gate_w[:, :], start=(t == 0), stop=(t == 1), skip_group_check=True)
                        last.then_inc(lg_full, 1)
                        pe.wait_ge(coef_ok, b * LT + LT)
                        for t in range(LT):
                            last = nc.tensor.transpose(ct_b[0:NEXP, t * P:(t + 1) * P], coef[:, t, :], ident[:, :])
                        last.then_inc(ct_full, 1)

                @block.scalar
                def _(act):
                    with act.Fori(0, B) as b:
                        act.wait_ge(xT_full, b + 1)
                        nc.scalar.copy(xT[:, :], xT_b[:, 0:S])
                        nc.scalar.copy(xT_all[:, bass.ds(b * S, S)], xT_b[:, 0:S]).then_inc(xT_ok, 1)
                        for t in range(LT):
                            act.wait_ge(max_ok, b * LT + t + 1)
                            nc.scalar.activation(gexp[:, :], lg_b[:, t * NEXP:(t + 1) * NEXP], ACT.Exp,
                                                 bias=gmax[:, 0:1], accum_out=gsum[:, 0:1]).then_inc(exp_ok, 1)
                        act.wait_ge(ct_full, b + 1)
                        nc.scalar.copy(coefT_all[:, bass.ds(b * S, S)], ct_b[0:NEXP, 0:S]).then_inc(ct_ok, 1)

                @block.vector
                def _(dve):
                    with dve.Fori(0, B) as b:
                        dve.wait_ge(lg_full, b + 1)
                        for t in range(LT):
                            m = b * LT + t + 1
                            nc.vector.tensor_reduce(gmax[:, :], lg_b[:, t * NEXP:(t + 1) * NEXP], AX.X, ALU.max,
                                                    negate=True).then_inc(max_ok, 1)
                            dve.wait_ge(exp_ok, m)
                            nc.vector.reciprocal(grec[:, :], gsum[:, :]).then_inc(rec_ok, 1)
                            dve.wait_ge(rec_ok, m)
                            nc.vector.tensor_scalar(gate[:, :], gexp[:, :], grec[:, 0:1], None, ALU.mult).then_inc(gate_ok, 1)
                            dve.wait_ge(gate_ok, m)
                            mine = gate[:, :, None].broadcast_to((P, NEXP, NEXP))
                            other = gate[:, None, :].broadcast_to((P, NEXP, NEXP))
                            nc.vector.tensor_tensor(above[:, :, :], other, mine, ALU.is_gt).then_inc(cmp_ok, 1)
                            nc.vector.tensor_tensor(equal[:, :, :], other, mine, ALU.is_equal).then_inc(cmp_ok, 1)
                            dve.wait_ge(cmp_ok, 4 * m - 2)
                            nc.vector.tensor_tensor(equal[:, :, :], equal[:, :, :], lower[:, :, :], ALU.mult).then_inc(cmp_ok, 1)
                            dve.wait_ge(cmp_ok, 4 * m - 1)
                            nc.vector.tensor_tensor(above[:, :, :], above[:, :, :], equal[:, :, :], ALU.add).then_inc(cmp_ok, 1)
                            dve.wait_ge(cmp_ok, 4 * m)
                            nc.vector.tensor_reduce(rank[:, :], above[:, :, :], AX.X, ALU.add).then_inc(rank_ok, 1)
                            dve.wait_ge(rank_ok, m)
                            nc.vector.tensor_scalar(sel[:, :], rank[:, :], 2.0, None, ALU.is_lt).then_inc(sel_ok, 1)
                            dve.wait_ge(sel_ok, m)
                            nc.vector.tensor_tensor(rank[:, :], sel[:, :], gate[:, :], ALU.mult).then_inc(kept_ok, 1)
                            dve.wait_ge(kept_ok, m)
                            nc.vector.tensor_reduce(tokw[:, :], rank[:, :], AX.X, ALU.add).then_inc(tokw_ok, 1)
                            dve.wait_ge(tokw_ok, m)
                            nc.vector.tensor_scalar(coef[:, t, :], sel[:, :], tokw[:, 0:1], None, ALU.mult).then_inc(coef_ok, 1)

            c_copied, h_full, h_ok, cb_full, hw_ok, o_full, o_out, c_used = (
                sem(f"d2_{n}") for n in ("c_copied", "h_full", "h_ok", "cb_full", "hw_ok", "o_full", "o_out", "c_used"))
            h_b, cb_b, o_b = psum[:, 0:2, :], psum[:, 2:4, :], psum[:, 4:6, :]
            with nc.Block() as block:
                @block.gpsimd
                def _(pool):
                    with pool.Fori(0, B) as b:
                        nc.gpsimd.tensor_copy(coefT[:, :], coefT_all[:, bass.ds(b * S, S)]).then_inc(c_copied, 1)
                        pool.wait_ge(o_full, b * LT + LT)

                @block.tensor
                def _(pe):
                    with pe.Fori(0, B) as b:
                        for a in range(NPR):
                            last = nc.tensor.matmul(h_b[:, a // 2, (a % 2) * S:(a % 2) * S + S],
                                                    w1[:, 2 * a:2 * a + 2, :].rearrange("p e h -> p (e h)"),
                                                    xT_all[:, bass.ds(b * S, S)], start=(a % 2 == 0), stop=(a % 2 == 1),
                                                    skip_group_check=True)
                        last.then_inc(h_full, 1)
                        pe.wait_ge(c_copied, b + 1)
                        for a in range(NPR):
                            last = nc.tensor.matmul(cb_b[:, a // 2, (a % 2) * S:(a % 2) * S + S], rows[:, a, :],
                                                    coefT[:, :], start=(a % 2 == 0), stop=(a % 2 == 1),
                                                    skip_group_check=True)
                        last.then_inc(cb_full, 1)
                        pe.wait_ge(hw_ok, b + 1)
                        for t in range(LT):
                            c = slice(t * P, (t + 1) * P)
                            for a in range(NPR):
                                nc.tensor.matmul(o_b[:, t, 0:D], hidw[:, a, c], w2[:, a, :], start=(a == 0), stop=False)
                            nc.tensor.matmul(o_b[:, t, 0:D], coefT[:, c], b2[:, :], start=False,
                                             stop=True).then_inc(o_full, 1)
                        pe.wait_ge(o_out, b * LT + LT)

                @block.scalar
                def _(act):
                    with act.Fori(0, B) as b:
                        act.wait_ge(h_full, b + 1)
                        for a in range(NPR):
                            last = nc.scalar.activation(hid[:, a, :], h_b[:, a // 2, (a % 2) * S:(a % 2) * S + S],
                                                        ACT.Gelu, bias=b1[:, a:a + 1])
                        last.then_inc(h_ok, 1)

                @block.vector
                def _(dve):
                    with dve.Fori(0, B) as b:
                        dve.wait_ge(h_ok, b + 1)
                        dve.wait_ge(cb_full, b + 1)
                        nc.vector.tensor_tensor(hidw[:, :, :].rearrange("p a s -> p (a s)"),
                                                cb_b.rearrange("p a s -> p (a s)"),
                                                hid[:, :, :].rearrange("p a s -> p (a s)"), ALU.mult).then_inc(hw_ok, 1)
                        for t in range(LT):
                            dve.wait_ge(o_full, b * LT + t + 1)
                            xt = X[:, bass.ds(b * LT + t, 1), :].rearrange("p a c -> p (a c)")
                            nc.vector.tensor_tensor(xt, o_b[:, t, 0:D], xt, ALU.add).then_inc(o_out, 1)

        layer_norm("ln4", store=out_v)


_INS = ['L0_attn_x', 'L0_attn_Wq', 'L0_attn_Wk', 'L0_attn_Wv', 'L0_attn_Eq', 'L0_attn_Ek', 'L0_attn_Ev',
        'L0_ffn_Wqkv', 'L0_ffn_q_scale', 'L0_ffn_k_scale', 'L0_ffn_Wo', 'L0_ffn_ln_g', 'L0_ffn_ln_b', 'L0_ffn_W1',
        'L0_ffn_b1', 'L0_ffn_W2', 'L0_ffn_b2', 'L1_attn_Wqkv', 'L1_attn_bqkv', 'L1_attn_Wout', 'L1_attn_bout',
        'L1_ffn_gate_w', 'L1_ffn_w1', 'L1_ffn_b1', 'L1_ffn_w2', 'L1_ffn_b2']
_STOP = 99


def kernel(**inputs):
    import numpy as _np
    import concourse.bacc as _bacc
    from concourse import mybir as _mybir
    from concourse.bass_utils import run_bass_kernel_spmd as _run

    nc = _bacc.Bacc("TRN2", target_bir_lowering=False, num_devices=1)
    arrays, args = {}, {}
    for name in _INS:
        a = _np.ascontiguousarray(inputs[name])
        arrays[f"in_{name}_dram"] = a
        args[name] = nc.dram_tensor(f"in_{name}_dram", a.shape, _mybir.dt.from_np(a.dtype), kind="ExternalInput").ap()
    for name, a in shape_constants().items():
        arrays[f"const_{name}_dram"] = a
        args[name] = nc.dram_tensor(f"const_{name}_dram", a.shape, _mybir.dt.from_np(a.dtype),
                                    kind="ExternalInput").ap()
    out = nc.dram_tensor("out_0_dram", (B, S, D), _mybir.dt.float32, kind="ExternalOutput").ap()
    build_program(nc, args, out, _STOP)
    r = _run(nc, [arrays], core_ids=[0])
    return r.results[0]["out_0_dram"]
```

```python
from contextlib import ExitStack

import numpy as np

import concourse.bass as bass
from concourse import mybir

F32 = mybir.dt.float32
BF16 = mybir.dt.bfloat16
ALU = mybir.AluOpType
ACT = mybir.ActivationFunctionType
AX = mybir.AxisListType

P = 128
B, S, D = 16, 256, 128
LT = S // P
NT = B * LT
H, HD = 16, 8
SCALE_A = 1.0 / HD ** 0.5
MAXD = 64
NREL = 2 * MAXD + 1
NREX = 2 * S - 1
LB = P // HD
NLB = P // LB
TABW = NREX - LB + 1
DEPTH, BH, BD, WIN = 6, 16, 64, 32
INNER = BH * BD
FF = int(D * 4 * 2 / 3)
FCH = [128, 128, FF - 256]
NEXP, EH = 8, 64
NPR = NEXP // 2
EPS = 1e-5
NEG = -1e30

GMASK, IDENT, SEL24, TRIU, WMASK, PMASK, COS, SIN, SHIFT, ESEL, LOWER = range(11)


def shape_constants():
    f = np.float32
    p = np.arange(P)
    c = {}
    c["group_mask"] = (p[:, None] // HD == np.arange(LB)[None, :]).astype(f)
    c["ident"] = np.eye(P, dtype=f)
    c["flip"] = np.ascontiguousarray(np.eye(P, dtype=f)[::-1])
    heads = p[:, None] // LB == np.arange(8)[None, :]
    toks = p[:, None] % LB == np.arange(LB)[None, :]
    c["own24"] = np.repeat(np.concatenate([heads, toks], 1)[:, :, None], HD, 2).reshape(P, 24 * HD).astype(f)
    c["causal"] = np.where(p[None, :] > p[:, None], f(-125), f(0)).astype(f)
    i, j = p[:, None], p[None, :]
    c["window_own"] = np.where((j > i) | (i > j + WIN), f(NEG), f(0)).astype(f)
    c["window_prev"] = np.where(i > np.arange(WIN)[None, :], f(NEG), f(0)).astype(f)
    half = np.arange(0, BD, 2, dtype=f)
    inv_freq = (f(1) / np.power(f(10000), half / f(BD))).astype(f)
    t = np.arange(S, dtype=f)
    freqs = (t[:, None] * inv_freq[None, :]).astype(f)
    freqs = np.concatenate([freqs, freqs], -1)
    base = ((half + f(0.4 * BD)) / f(1.4 * BD)).astype(f)
    power = ((t - S // 2) / f(WIN // 2)).astype(f)
    scale = np.power(base[None, :], power[:, None]).astype(f)
    scale = np.concatenate([scale, scale], -1)
    sign = np.where(np.arange(BD) < BD // 2, f(-1), f(1))
    inv = (f(1) / scale).astype(f)
    cos, sin = np.cos(freqs), np.sin(freqs) * sign
    lay = lambda q, k: np.stack([q, k], 1).reshape(LT, P, 2, BD).transpose(1, 0, 2, 3).reshape(P, LT * 2 * BD).astype(f)
    c["rot_cos"] = lay(cos * scale * f(8), cos * inv)
    c["rot_sin"] = lay(sin * scale * f(8), sin * inv)
    s1 = np.zeros((P, P), f)
    s1[p[:-1], p[:-1] + 1] = 1
    s2 = np.zeros((P, P), f)
    s2[P - 1, 0] = 1
    c["shift_in"], c["shift_over"] = s1, s2
    e = np.zeros((NEXP, NPR, 2, EH), f)
    for x in range(NEXP):
        e[x, x // 2, x % 2] = 1
    c["expert_rows"] = e.reshape(NEXP, NPR * 2 * EH)
    c["lower"] = np.tile(np.tril(np.ones((NEXP, NEXP), f), -1).reshape(1, -1), (P, 1))
    return c


def build_program(nc, T, out, stop=99):
    ctx = ExitStack()
    with ctx:
        def sb(stack, name, shape, dt=F32):
            return stack.enter_context(nc.sbuf_tensor(name, shape, dt))

        def sem(name):
            return ctx.enter_context(nc.semaphore(name))

        def dram(name, shape):
            return nc.dram_tensor(name, shape, F32, kind="Internal")

        X = sb(ctx, "X", [P, NT, D])
        XR = sb(ctx, "XR", [P, NT, D])
        ident = sb(ctx, "ident", [P, P])
        ident_bf = sb(ctx, "ident_bf", [P, P], BF16)
        gmask = sb(ctx, "gmask", [P, LB])
        ones = sb(ctx, "ones", [P, P])
        neghalf = sb(ctx, "neghalf", [P, LB])
        pause = sb(ctx, "pause", [P, 1])
        xcur = sb(ctx, "xcur", [P, LT, D])
        xT = sb(ctx, "xT", [P, S])
        psum = ctx.enter_context(nc.psum_tensor("psum", [P, 8, 512], F32))
        bank = [psum[:, i, :] for i in range(8)]

        oa = dram("oa", (B, LT, NLB, LB, 2, 8, HD))
        ev_ext = dram("ev_ext", (NREX, HD))
        pp_ext = dram("pp_ext", (1, 512))

        x_in = T["L0_attn_x"].rearrange("b (t p) c -> p (b t) c", p=P)
        out_v = out.rearrange("b (t p) c -> p (b t) c", p=P)

        with ExitStack() as st:
            wq, wk, wv = (sb(st, n, [P, D]) for n in ("a_wq", "a_wk", "a_wv"))
            wq_rep, wk_rep = (sb(st, n, [P, H, P]) for n in ("a_wq_rep", "a_wk_rep"))
            ext = sb(st, "a_ext", [HD, 4, NREX])
            pprow = sb(st, "a_pprow", [1, 512])
            eq_tab, ek_tab = (sb(st, n, [P, TABW]) for n in ("a_eq_tab", "a_ek_tab"))
            ev_tab = sb(st, "a_ev_tab", [P, LT * P + P, HD])
            pp_tab = sb(st, "a_pp_tab", [P, LT, S])
            own24 = sb(st, "a_own24", [P, 24 * HD])
            qT = sb(st, "a_qT", [P, S])
            k_diag = sb(st, "a_k_diag", [P, H, S])
            q_blk, k_blk = (sb(st, n, [P, H, S]) for n in ("a_q_blk", "a_k_blk"))
            relk = sb(st, "a_relk", [P, LT, H, P])
            probs = sb(st, "a_probs", [P, 2, 4, S])
            probsT = sb(st, "a_probsT", [P, LT, NLB, 8, LB])
            vones = sb(st, "a_vones", [P, LT, 2, 1 + 8 * HD])
            nmax, nbias = (sb(st, n, [P, 2, 4]) for n in ("a_nmax", "a_nbias"))
            rsum = sb(st, "a_rsum", [P, 8])
            ymask = sb(st, "a_ymask", [P, 8, 24 * HD])
            ysum = sb(st, "a_ysum", [P, 8, HD])
            yout = sb(st, "a_yout", [P, B * 4, 8 * HD])

            ld_x, ld_c, ld_w, ld_e = sem("a_ld_x"), sem("a_ld_c"), sem("a_ld_w"), sem("a_ld_e")
            ev_wr, pp_wr, tabs, flips = sem("a_ev_wr"), sem("a_pp_wr"), sem("a_tabs"), sem("a_flips")
            ev_turned, pp_turned = sem("a_ev_turned"), sem("a_pp_turned")
            ev_flip = q_blk[:, 0:12, :].rearrange("p h l -> p (h l)")
            pp_flip = k_blk[:, 0:2, :]
            flip = sb(st, "a_flip", [P, P])
            ext_ok, prod_ok, pp_full, pp_ok, set_ok = (sem("a_ext_ok"), sem("a_prod_ok"), sem("a_pp_full"),
                                                       sem("a_pp_ok"), sem("a_set_ok"))

            with nc.Block() as block:
                @block.sync
                def _(sp):
                    for name, t in (("L0_attn_Eq", 0), ("L0_attn_Ek", 2)):
                        sp.dma_start(ext[:, t, S - 1 - MAXD:S + MAXD], T[name].rearrange("r d -> d r"),
                                     allow_slow_non_contiguous=True).then_inc(ld_e, 16)
                    sp.dma_start(ext[:, 1, S - 1 - MAXD:S + MAXD],
                                 bass.AP(T["L0_attn_Ek"].tensor, (NREL - 1) * HD, [[1, HD], [-HD, NREL]]),
                                 allow_slow_non_contiguous=True).then_inc(ld_e, 16)
                    ev = T["L0_attn_Ev"]
                    sp.dma_start(ev_ext[S - 1 - MAXD:S + MAXD, :], ev[:, :]).then_inc(ev_wr, 16)
                    sp.dma_start(ev_ext[0:S - 1 - MAXD, :],
                                 ev[0:1, :].broadcast_to((S - 1 - MAXD, HD))).then_inc(ev_wr, 16)
                    sp.dma_start(ev_ext[S + MAXD:NREX, :],
                                 ev[NREL - 1:NREL, :].broadcast_to((S - 1 - MAXD, HD))).then_inc(ev_wr, 16)
                    sp.wait_ge(ev_wr, 48)
                    sp.dma_start(ev_flip, bass.AP(ev_ext, 0, [[HD, P], [1, (LT * P + P) * HD]])).then_inc(flips, 16)
                    sp.wait_ge(ext_ok, 1)
                    for m in range(LB):
                        for tab, t in ((eq_tab, 0), (ek_tab, 1)):
                            sp.dma_start(tab[HD * m:HD * m + HD, :],
                                         ext[:, t, LB - 1 - m:LB - 1 - m + TABW]).then_inc(tabs, 16)
                    sp.wait_ge(pp_ok, 1)
                    sp.dma_start(pp_ext[:, 0:NREX], pprow[:, 0:NREX]).then_inc(pp_wr, 16)
                    sp.wait_ge(pp_wr, 16)
                    for mt in range(LT):
                        sp.dma_start(pp_flip[:, mt, :],
                                     bass.AP(pp_ext, P - mt * P, [[1, P], [1, S]])).then_inc(flips, 16)
                    sp.wait_ge(tabs, 16 * 2 * LB)
                    sp.wait_ge(ld_x, 16)

                @block.scalar
                def _(act):
                    for name, t in (("L0_attn_Wq", wq), ("L0_attn_Wk", wk), ("L0_attn_Wv", wv)):
                        act.dma_start(t[:, :], T[name]).then_inc(ld_w, 16)
                    for name, t in (("ident", ident), ("group_mask", gmask), ("own24", own24), ("flip", flip)):
                        act.dma_start(t[:, :], T[name]).then_inc(ld_c, 16)
                    act.dma_start(X[:, :, :], x_in).then_inc(ld_x, 16)

                @block.gpsimd
                def _(pool):
                    nc.gpsimd.memset(ones[:, :], 1.0).then_inc(set_ok, 1)
                    nc.gpsimd.memset(neghalf[:, :], -0.5)
                    nc.gpsimd.memset(vones[:, :, :, :], 1.0)
                    pool.wait_ge(ld_w, 48)
                    for w, rep in ((wq, wq_rep), (wk, wk_rep)):
                        for h in range(H):
                            nc.gpsimd.tensor_copy(
                                rep[:, h, :].rearrange("p (l d) -> p l d", d=HD),
                                w[:, None, h * HD:(h + 1) * HD].broadcast_to((P, LB, HD)))

                @block.vector
                def _(dve):
                    dve.wait_ge(ld_e, 48)
                    for t in range(3):
                        a, b = S - 1 - MAXD, S + MAXD
                        nc.vector.tensor_copy(ext[:, t, 0:a], ext[:, t, a:a + 1].broadcast_to((HD, a)))
                        last = nc.vector.tensor_copy(ext[:, t, b:NREX],
                                                     ext[:, t, b - 1:b].broadcast_to((HD, NREX - b)))
                    last.then_inc(ext_ok, 1)
                    dve.wait_ge(ext_ok, 1)
                    nc.vector.tensor_tensor(ext[:, 3, :], ext[:, 0, :], ext[:, 2, :], ALU.mult).then_inc(prod_ok, 1)
                    dve.wait_ge(pp_full, 1)
                    nc.vector.tensor_copy(pprow[0:1, 0:NREX], bank[0][0:1, 0:NREX]).then_inc(pp_ok, 1)
                    dve.wait_ge(ld_c, 64)
                    nc.vector.tensor_copy(ident_bf[:, :], ident[:, :])
                    dve.wait_ge(ev_turned, 1)
                    nc.vector.tensor_copy(ev_tab[:, :, :].rearrange("p u d -> p (u d)"),
                                          psum[:, 1:7, :].rearrange("p a c -> p (a c)"))
                    dve.wait_ge(pp_turned, 1)
                    nc.vector.tensor_copy(pp_tab[:, :, :].rearrange("p t l -> p (t l)"), bank[7])

                @block.tensor
                def _(pe):
                    pe.wait_ge(set_ok, 1)
                    pe.wait_ge(prod_ok, 1)
                    nc.tensor.matmul(bank[0][0:1, 0:NREX], ones[0:HD, 0:1], ext[:, 3, :],
                                     start=True, stop=True).then_inc(pp_full, 1)
                    pe.wait_ge(ld_c, 64)
                    pe.wait_ge(flips, 16 * (1 + LT))
                    for i in range(6):
                        last = nc.tensor.matmul(bank[1 + i], flip[:, :], ev_flip[:, i * 512:(i + 1) * 512],
                                                start=True, stop=True)
                    last.then_inc(ev_turned, 1)
                    nc.tensor.matmul(bank[7], flip[:, :], pp_flip.rearrange("p t l -> p (t l)"),
                                     start=True, stop=True).then_inc(pp_turned, 1)

            FQK, FV, FQB, FKB, FRK, FY = 2, 3, 4, 12, (20, 32), (28, 40, 44, 48)
            order = list(range(28)) + [28, 29, 30, 31] + list(range(32, 52))
            FA = 52
            ring = bank[0:2]
            score = [psum[:, 2:4, :], psum[:, 4:6, :]]
            turned = bank[6:8]
            x_copied, ring_full, ring_free = sem("a_x_copied"), [sem("a_ring_full0"), sem("a_ring_full1")], \
                [sem("a_ring_free0"), sem("a_ring_free1")]
            score_full, row_max, bias_ok, exp_done = (sem("a_score_full"), sem("a_row_max"), sem("a_bias_ok"),
                                                      sem("a_exp_done"))
            turn_full, turn_out = sem("a_turn_full"), sem("a_turn_out")
            ymask_ok, ysum_ok, yout_ok, oa_st = (sem("a_ymask_ok"), sem("a_ysum_ok"), sem("a_yout_ok"),
                                                 sem("a_oa_st"))

            def filled(b, i):
                return b * (FA // 2) + i // 2 + 1

            with nc.Block() as block:
                @block.gpsimd
                def _(pool):
                    with pool.Fori(0, B) as b:
                        nc.gpsimd.tensor_copy(xcur[:, :, :], X[:, bass.ds(b * LT, LT), :]).then_inc(x_copied, 1)
                        pool.wait_ge(ring_full[1], filled(b, 1))

                @block.tensor
                def _(pe):
                    with pe.Fori(0, B) as b:
                        def room(i):
                            if i >= 2:
                                pe.wait_ge(ring_free[i % 2], filled(b, i - 2))
                            return ring[i % 2]

                        def relative_keys(lt):
                            for n in range(8):
                                mt, i = n // 4, FRK[lt] + n
                                r = room(i)
                                for j in range(2):
                                    blk = lt * NLB // 1 + (n % 4) * 2 + j
                                    v = mt * P - blk * LB + S - LB
                                    last = nc.tensor.matmul(r[:, j * S:(j + 1) * S], ek_tab[:, v:v + P],
                                                            q_blk[:, :, blk * LB:(blk + 1) * LB], start=(j == 0), stop=(j == 1), skip_group_check=True)
                                last.then_inc(ring_full[i % 2], 1)

                        def scores(s):
                            lt, hq = s // 4, s % 4
                            if s >= 2:
                                pe.wait_ge(exp_done, b * 8 + s - 1)
                            if hq == 0:
                                for i in (6, 7):
                                    pe.wait_ge(ring_free[i % 2], filled(b, FRK[lt] + i))
                            for mt in range(LT):
                                o = score[s % 2][:, mt, :].rearrange("p (h m) -> p h m", h=4)
                                hs = slice(hq * 4, hq * 4 + 4)
                                nc.tensor.matmul(o, qT[:, lt * P:(lt + 1) * P], k_diag[:, hs, mt * P:(mt + 1) * P],
                                                 start=True, stop=False, skip_group_check=True)
                                for n in range(NLB):
                                    blk = mt * NLB + n
                                    v = lt * P - blk * LB + S - LB
                                    nc.tensor.matmul(o[:, :, n * LB:(n + 1) * LB], eq_tab[:, v:v + P],
                                                     k_blk[:, hs, blk * LB:(blk + 1) * LB], start=False, stop=False,
                                                     skip_group_check=True)
                                for h in range(4):
                                    last = nc.tensor.matmul(o[:, h, :], relk[:, mt, hq * 4 + h, :], ident[:, :],
                                                            start=False, stop=(h == 3), skip_group_check=True)
                            last.then_inc(score_full, 1)

                        def turn(s):
                            pe.wait_ge(exp_done, b * 8 + s + 1)
                            if s >= 1:
                                pe.wait_ge(turn_out, b * 8 + s)
                            for mt in range(LT):
                                for h in range(4):
                                    last = nc.tensor.transpose(turned[mt][:, h * P:(h + 1) * P],
                                                               probs[:, s % 2, h, mt * P:(mt + 1) * P], ident[:, :])
                            last.then_inc(turn_full, 1)

                        def outputs(g):
                            pe.wait_ge(turn_out, b * 8 + 2 * g + 2)
                            lt, hh = g // 2, g % 2
                            for n in range(4):
                                i = FY[g] + n
                                r = room(i)
                                for j in range(2):
                                    blk = lt * NLB + 2 * n + j
                                    for mt in range(LT):
                                        w = probsT[:, mt, 2 * n + j, :, :].rearrange("p h l -> p (h l)")
                                        o = r[:, j * 193:(j + 1) * 193]
                                        u = blk * LB - mt * P + P
                                        nc.tensor.matmul(o[:, 0:65], w, vones[:, mt, hh, :],
                                                         start=(j == 0 and mt == 0), stop=False, skip_group_check=True)
                                        last = nc.tensor.matmul(o[:, 65:193], w, ev_tab[:, u:u + LB, :],
                                                                start=False, stop=(j == 1 and mt == 1),
                                                                skip_group_check=True)
                                last.then_inc(ring_full[i % 2], 1)

                        pe.wait_ge(x_copied, b + 1)
                        for t in range(LT):
                            nc.tensor.transpose(room(t)[:, 0:P], xcur[:, t, :], ident[:, :]).then_inc(ring_full[t], 1)
                        r = room(FQK)
                        pe.wait_ge(ring_free[1], filled(b, 1))
                        nc.tensor.matmul(r[:, 0:S], wq[:, :], xT[:, :], start=True, stop=False, skip_group_check=True)
                        nc.tensor.matmul(r[:, S:2 * S], wk[:, :], xT[:, :], start=False, stop=True,
                                         skip_group_check=True).then_inc(ring_full[FQK % 2], 1)
                        r = room(FV)
                        for t in range(LT):
                            last = nc.tensor.matmul(r[:, t * D:(t + 1) * D], xT[:, t * P:(t + 1) * P], wv[:, :],
                                                    start=(t == 0), stop=(t == 1), skip_group_check=True)
                        last.then_inc(ring_full[FV % 2], 1)
                        for f, rep in ((FQB, wq_rep), (FKB, wk_rep)):
                            for n in range(H // 2):
                                r = room(f + n)
                                for j in range(2):
                                    last = nc.tensor.matmul(r[:, j * S:(j + 1) * S], rep[:, 2 * n + j, :], xT[:, :],
                                                            start=(j == 0), stop=(j == 1), skip_group_check=True)
                                last.then_inc(ring_full[(f + n) % 2], 1)
                        relative_keys(0)
                        scores(0)
                        scores(1)
                        turn(0)
                        scores(2)
                        turn(1)
                        outputs(0)
                        scores(3)
                        turn(2)
                        relative_keys(1)
                        scores(4)
                        turn(3)
                        outputs(1)
                        scores(5)
                        turn(4)
                        scores(6)
                        turn(5)
                        outputs(2)
                        scores(7)
                        turn(6)
                        turn(7)
                        outputs(3)
                        for i in (FA - 2, FA - 1):
                            pe.wait_ge(ring_free[i % 2], filled(b, i))

                @block.scalar
                def _(act):
                    with act.Fori(0, B) as b:
                        def exps(s):
                            act.wait_ge(bias_ok, b * 8 + s + 1)
                            for h in range(4):
                                last = nc.scalar.activation(
                                    probs[:, s % 2, h, :].rearrange("p (t m) -> p t m", t=LT),
                                    score[s % 2][:, :, h * P:(h + 1) * P], ACT.Exp,
                                    bias=nbias[:, s % 2, h:h + 1], scale=SCALE_A)
                            last.then_inc(exp_done, 1)

                        def turns(s):
                            act.wait_ge(turn_full, b * 8 + s + 1)
                            for mt in range(LT):
                                last = nc.scalar.copy(probsT[:, mt, :, (s % 2) * 4:(s % 2) * 4 + 4, :],
                                                      turned[mt].rearrange("p (h k l) -> p k h l", h=4, l=LB))
                            last.then_inc(turn_out, 1)

                        for s in range(8):
                            exps(s)
                            if s:
                                turns(s - 1)
                        turns(7)

                @block.vector
                def _(dve):
                    with dve.Fori(0, B) as b:
                        def take(i):
                            dve.wait_ge(ring_full[i % 2], filled(b, i))
                            return ring[i % 2]

                        def maxima(s):
                            dve.wait_ge(score_full, b * 8 + s + 1)
                            nc.vector.tensor_reduce(nmax[:, s % 2, :],
                                                    score[s % 2].rearrange("p t (h m) -> p h t m", h=4),
                                                    AX.XY, ALU.max).then_inc(row_max, 1)
                            dve.wait_ge(row_max, b * 8 + s + 1)
                            nc.vector.tensor_scalar(nbias[:, s % 2, :], nmax[:, s % 2, :], -SCALE_A, None,
                                                    ALU.mult).then_inc(bias_ok, 1)

                        def relative_keys(lt):
                            for n in range(8):
                                i, mt, lp = FRK[lt] + n, n // 4, n % 4
                                r = take(i)
                                pp = pp_tab[:, mt, lt * P + lp * 32:lt * P + lp * 32 + 32]
                                nc.vector.tensor_tensor(
                                    relk[:, mt, :, lp * 32:lp * 32 + 32].rearrange("p h (j l) -> p j h l", j=2),
                                    r.rearrange("p (j h l) -> p j h l", j=2, h=H),
                                    pp.rearrange("p (j l) -> p j l", j=2)[:, :, None, :].broadcast_to((P, 2, H, LB)),
                                    ALU.add).then_inc(ring_free[i % 2], 1)

                        def outputs(g):
                            for n in range(4):
                                i = FY[g] + n
                                r = take(i)[:, 0:386].rearrange("p (j c) -> p j c", j=2)
                                nc.vector.tensor_tensor(ymask[:, 2 * n:2 * n + 2, :], r[:, :, 1:193],
                                                        own24[:, None, :].broadcast_to((P, 2, 24 * HD)),
                                                        ALU.mult).then_inc(ymask_ok, 1)
                                nc.vector.reciprocal(rsum[:, 2 * n:2 * n + 2], r[:, :, 0]).then_inc(ring_free[i % 2], 1)
                            dve.wait_ge(ymask_ok, b * 16 + 4 * g + 4)
                            nc.vector.tensor_reduce(ysum[:, :, :], ymask[:, :, :].rearrange("p n (g d) -> p n d g", d=HD),
                                                    AX.X, ALU.add).then_inc(ysum_ok, 1)
                            dve.wait_ge(ysum_ok, b * 4 + g + 1)
                            for i in (2, 3):
                                dve.wait_ge(ring_free[i % 2], filled(b, FY[g] + i))
                            nc.vector.tensor_tensor(yout[:, bass.ds(b * 4 + g, 1), :].rearrange("p a (n d) -> p (a n) d", d=HD),
                                                    ysum[:, :, :], rsum[:, :, None].broadcast_to((P, 8, HD)),
                                                    ALU.mult).then_inc(yout_ok, 1)

                        for t in range(LT):
                            r = take(t)
                            nc.vector.tensor_copy(xT[:, t * P:(t + 1) * P], r[:, 0:P]).then_inc(ring_free[t], 1)
                        r = take(FQK)
                        nc.vector.tensor_copy(qT[:, :], r[:, 0:S])
                        nc.vector.tensor_tensor(k_diag[:, :, :], r[:, None, S:2 * S].broadcast_to((P, H, S)),
                                                gmask[:, :, None].broadcast_to((P, H, S)),
                                                ALU.mult).then_inc(ring_free[FQK % 2], 1)
                        r = take(FV)
                        nc.vector.tensor_copy(vones[:, :, :, 1:65],
                                              r[:, 0:LT * D].rearrange("p (t a c) -> p t a c", t=LT, a=2)
                                              ).then_inc(ring_free[FV % 2], 1)
                        for f, blk in ((FQB, q_blk), (FKB, k_blk)):
                            for n in range(H // 2):
                                r = take(f + n)
                                nc.vector.tensor_tensor(
                                    blk[:, 2 * n:2 * n + 2, :].rearrange("p h (n l) -> p (h n) l", l=LB),
                                    r.rearrange("p (n l) -> p n l", l=LB),
                                    gmask[:, None, :].broadcast_to((P, 2 * S // LB, LB)),
                                    ALU.mult).then_inc(ring_free[(f + n) % 2], 1)
                        relative_keys(0)
                        maxima(0)
                        maxima(1)
                        maxima(2)
                        outputs(0)
                        maxima(3)
                        relative_keys(1)
                        maxima(4)
                        outputs(1)
                        maxima(5)
                        maxima(6)
                        outputs(2)
                        maxima(7)
                        outputs(3)

                @block.sync
                def _(sp):
                    with sp.Fori(0, B) as b:
                        for g in range(4):
                            lt, hh = g // 2, g % 2
                            sp.wait_ge(yout_ok, b * 4 + g + 1)
                            for h in range(8):
                                sp.dma_start(
                                    oa[b, lt, :, :, hh, h, :].rearrange("k l d -> l k d"),
                                    yout[LB * h:LB * h + LB, b * 4 + g, :].rearrange("p (k d) -> p k d", d=HD)
                                ).then_inc(oa_st, 16)
                    sp.wait_ge(oa_st, 16 * B * 4 * 8)

        def layer_norm(tag, residual=None, load=None, keep=None, store=None):
            GT = 8
            with ExitStack() as st:
                stats = sb(st, f"{tag}_stats", [P, GT, 6])
                mv = sb(st, f"{tag}_mv", [P, GT, 2])
                var = sb(st, f"{tag}_var", [P, GT])
                rstd = sb(st, f"{tag}_rstd", [P, GT])
                added, stats_ok, mv_ok, var_ok, rstd_ok, normed, kept, loaded, stored = (
                    sem(f"{tag}_{n}") for n in ("added", "stats_ok", "mv_ok", "var_ok", "rstd_ok", "normed", "kept",
                                                "loaded", "stored"))
                with nc.Block() as block:
                    @block.sync
                    def _(sp):
                        if load is not None:
                            sp.dma_start(residual[:, :, :], load).then_inc(loaded, 16)
                        if store is not None:
                            with sp.Fori(0, NT // GT) as g:
                                sp.wait_ge(normed, (g + 1) * GT)
                                sp.dma_start(store[:, bass.ds(g * GT, GT), :],
                                             X[:, bass.ds(g * GT, GT), :]).then_inc(stored, 16)
                            sp.wait_ge(stored, 16 * (NT // GT))

                    @block.vector
                    def _(dve):
                        if load is not None:
                            dve.wait_ge(loaded, 16)
                        with dve.Fori(0, NT // GT) as g:
                            tiles = bass.ds(g * GT, GT)
                            if residual is not None:
                                nc.vector.tensor_tensor(X[:, tiles, :], X[:, tiles, :], residual[:, tiles, :],
                                                        ALU.add).then_inc(added, 1)
                                dve.wait_ge(added, g + 1)
                                nc.vector.memset(pause[:, :], 0.0)
                            for j in range(GT):
                                nc.vector.bn_stats(stats[:, j, :], X[:, bass.ds(g * GT + j, 1), :].rearrange("p a c -> p (a c)")).then_inc(stats_ok, 1)
                            dve.wait_ge(stats_ok, (g + 1) * GT)
                            nc.vector.memset(pause[:, :], 0.0)
                            for j in range(GT):
                                nc.vector.bn_aggr(mv[:, j, :], stats[:, j, :]).then_inc(mv_ok, 1)
                            dve.wait_ge(mv_ok, (g + 1) * GT)
                            nc.vector.tensor_scalar(var[:, :], mv[:, :, 1], EPS, None, ALU.add).then_inc(var_ok, 1)
                            dve.wait_ge(rstd_ok, g + 1)
                            for j in range(GT):
                                t = X[:, bass.ds(g * GT + j, 1), :].rearrange("p a c -> p (a c)")
                                nc.vector.tensor_scalar(t, t, mv[:, j, 0:1], rstd[:, j:j + 1], ALU.subtract,
                                                        ALU.mult).then_inc(normed, 1)

                    @block.gpsimd
                    def _(pool):
                        with pool.Fori(0, NT // GT) as g:
                            pool.wait_ge(var_ok, g + 1)
                            nc.gpsimd.tensor_tensor(rstd[:, :], var[:, :], neghalf[:, 0:GT],
                                                    ALU.pow).then_inc(rstd_ok, 1)

                    if keep is not None:
                        @block.scalar
                        def _(act):
                            with act.Fori(0, NT // GT) as g:
                                tiles = bass.ds(g * GT, GT)
                                act.wait_ge(normed, (g + 1) * GT)
                                nc.scalar.copy(keep[:, tiles, :], X[:, tiles, :]).then_inc(kept, 1)

        def store_stream(tag):
            done = sem(f"{tag}_done")
            with nc.Block() as block:
                @block.sync
                def _(sp):
                    sp.dma_start(out_v, X[:, :, :]).then_inc(done, 16)
                    sp.wait_ge(done, 16)

        oa_tiles = oa.rearrange("b t k l a h d -> (k l) (b t) (a h d)")
        layer_norm("ln1", residual=XR, load=oa_tiles, keep=XR)
        if stop == 1:
            return store_stream("stop")

        with ExitStack() as st:
            wqkv = sb(st, "b_wqkv", [P, 3 * INNER])
            wo = sb(st, "b_wo", [P, INNER // P, D])
            qk_gain = sb(st, "b_qk_gain", [P, 2, BD])
            cos0, sin0, cosg, sing = (sb(st, n, [P, LT, 2, BD]) for n in ("b_cos0", "b_sin0", "b_cosg", "b_sing"))
            w1 = sb(st, "b_w1", [P, 2 * FF])
            w2 = sb(st, "b_w2", [P, 3, D])
            b1 = sb(st, "b_b1", [P, 6])
            b2 = sb(st, "b_b2", [1, D])
            lng, lnb = sb(st, "b_lng", [P, 1]), sb(st, "b_lnb", [P, 1])
            shift_in, shift_over = sb(st, "b_shift_in", [P, P]), sb(st, "b_shift_over", [P, P])
            masks0 = sb(st, "b_masks0", [P, P + WIN])
            own_bf = sb(st, "b_own_bf", [P, P], BF16)
            prev_bf = sb(st, "b_prev_bf", [P, WIN], BF16)
            sq = sb(st, "b_sq", [P, 2 * 8 * BD])
            ss = sb(st, "b_ss", [P, 2, 16])
            rnorm = sb(st, "b_rnorm", [P, 2, 16])
            t1, t2 = sb(st, "b_t1", [P, 2, 16, BD]), sb(st, "b_t2", [P, 2, 16, BD])
            rot, qk = sb(st, "b_rot", [P, 2, 16, BD]), sb(st, "b_qk", [P, 2, 16, BD])
            v = sb(st, "b_v", [P, 4, 8, BD + 1])
            qTs = sb(st, "b_qTs", [P, 4, P])
            kz = sb(st, "b_kz", [P, LT, 4, 2, P])
            m_own, m_prev = sb(st, "b_m_own", [P, 8]), sb(st, "b_m_prev", [WIN, 8])
            pr = sb(st, "b_pr", [P, 2, 8, P])
            pp0 = sb(st, "b_pp0", [WIN, 8, WIN])
            pp = sb(st, "b_pp", [WIN, 8, P])
            prT = sb(st, "b_prT", [P, 8, P])
            ppT = sb(st, "b_ppT", [P, 8, WIN])
            rs = sb(st, "b_rs", [P, 8])
            o = sb(st, "b_o", [P, 8, BD])
            oT = sb(st, "b_oT", [P, 4, P])
            st6 = sb(st, "b_st6", [P, 2, LT, 6])
            mv = sb(st, "b_mv", [P, 2, LT, 2])
            fvar, frstd = sb(st, "b_fvar", [P, 2, LT]), sb(st, "b_frstd", [P, 2, LT])
            xn = sb(st, "b_xn", [P, 2, LT, D])
            xnT = sb(st, "b_xnT", [P, 2, S])
            gel = sb(st, "b_gel", [P, 2, 3, S])
            hid = sb(st, "b_hid", [P, 2, 3, S])

            c_ld, c_set, wa_ld, wf_ld = sem("b_c_ld"), sem("b_c_set"), sem("b_wa_ld"), sem("b_wf_ld")
            gains = sem("b_gains")
            x_copied, x_full, xT_done = sem("b_x_copied"), sem("b_x_full"), sem("b_xT_done")
            qk_full, v_full, sq_done, ss_done = sem("b_qk_full"), sem("b_v_full"), sem("b_sq_done"), sem("b_ss_done")
            floor_done, rn_done, t_done, rot_done, qk_done, v_done = (
                sem("b_floor_done"), sem("b_rn_done"), sem("b_t_done"), sem("b_rot_done"), sem("b_qk_done"),
                sem("b_v_done"))
            sc_full, mo_done, mp_done, mx_done, sub_done, exp_done = (
                sem("b_sc_full"), sem("b_mo_done"), sem("b_mp_done"), sem("b_mx_done"), sem("b_sub_done"),
                sem("b_exp_done"))
            rs_done, o_done, x_attn = sem("b_rs_done"), sem("b_o_done"), sem("b_x_attn")
            ring_full = [sem(f"b_ring_full{i}") for i in range(3)]
            ring_free = [sem(f"b_ring_free{i}") for i in range(3)]
            x_ffn, st_done, mv_done, var_done, rstd_done, xn_done = (
                sem("b_x_ffn"), sem("b_st_done"), sem("b_mv_done"), sem("b_var_done"), sem("b_rstd_done"),
                sem("b_xn_done"))
            hg_full, gel_done, hid_done = sem("b_hg_full"), sem("b_gel_done"), sem("b_hid_done")
            fr_full = [sem("b_fr_full0"), sem("b_fr_full1")]
            fr_free = [sem("b_fr_free0"), sem("b_fr_free1")]

            wqkv_d, wo_d = T["L0_ffn_Wqkv"], T["L0_ffn_Wo"]
            N_WA, N_WF = 4, 10
            NS = 4

            SLOTS = {"first": range(-4, 0), "loop": range(NS), "last": range(NS)}

            def valid(part, step):
                return {"first": step >= 0, "loop": True, "last": step < NS}[part]

            def slot_fills(part, j):
                fills = [("q", j + 2), ("k", j + 2), ("p0", j + 1), ("p1", j + 1)]
                fills += [("oT", j), ("prev", j + 2)] if j % 2 else [("pp", j + 1), ("oT", j)]
                fills += [("w", j), ("o0", j + 1), ("o1", j + 1)]
                return [f if valid(part, f[1]) else None for f in fills]

            ring_at = {part: {} for part in SLOTS}
            ring_count = {part: [0, 0, 0] for part in SLOTS}
            for part in SLOTS:
                for j in SLOTS[part]:
                    for i, f in enumerate(slot_fills(part, j)):
                        if f is not None:
                            ring_at[part][f] = (i % 3, ring_count[part][i % 3])
                            ring_count[part][i % 3] += 1
            RF, RL = ring_count["first"][0], ring_count["loop"][0]
            assert all(ring_count[p] == [c] * 3 for p, c in (("first", RF), ("loop", RL), ("last", RL - RF)))

            def ring_fill(part, l, b, name):
                back = 0
                if part != "first" and name not in ring_at[part]:
                    name, back = (name[0], name[1] + NS), RL
                    i, number = ring_at["loop"][name]
                else:
                    i, number = ring_at[part][name]
                return i, l * (B * RL) + (0 if part == "first" else b * RL + RF) + (number - back + 1)

            with nc.Block() as block:
                @block.sync
                def _(sp):
                    for name, t in (("rot_cos", cos0), ("rot_sin", sin0)):
                        sp.dma_start(t[:, :, :, :].rearrange("p t a d -> p (t a d)"), T[name]).then_inc(c_ld, 16)
                    sp.dma_start(shift_in[:, :], T["shift_in"]).then_inc(c_ld, 16)
                    sp.dma_start(shift_over[:, :], T["shift_over"]).then_inc(c_ld, 16)
                    sp.dma_start(masks0[:, 0:P], T["window_own"]).then_inc(c_ld, 16)
                    sp.dma_start(masks0[:, P:P + WIN], T["window_prev"]).then_inc(c_ld, 16)
                    sp.wait_ge(c_ld, 96)

                @block.gpsimd
                def _(pool):
                    nc.gpsimd.memset(v[:, :, :, :], 1.0)
                    nc.gpsimd.memset(kz[:, :, :, :, :], 0.0)
                    nc.gpsimd.memset(pp[:, :, :], 0.0)

                @block.vector
                def _(dve):
                    nc.vector.memset(xT[64:128, 0:1], 0.0)
                    dve.wait_ge(c_ld, 96)
                    nc.vector.tensor_copy(own_bf[:, :], masks0[:, 0:P])
                    nc.vector.tensor_copy(prev_bf[:, :], masks0[:, P:P + WIN])

            def pair_fill(part, l, i, kind):
                in_part = {"first": {"x": 1, "xT": 2}, "loop": {"x": 3, "xT": 4, "out": 5}, "last": {"out": 3}}[part]
                return l * (3 * (B // 2)) + (0 if part == "first" else i * 3) + in_part[kind]

            ring = bank[5:8]
            fring = bank[6:8]
            NP = B // 2
            with nc.Block() as block:
                @block.sync
                def _(sp):
                    with sp.Fori(0, DEPTH) as l:
                        sp.wait_ge(x_attn, l * B * NS + 1)
                        sp.dma_start(wqkv[:, :], wqkv_d[l]).then_inc(wa_ld, 16)
                        sp.dma_start(wo[:, :, :], wo_d[l].rearrange("(k p) c -> p k c", p=P)).then_inc(wa_ld, 16)
                        for i, n in enumerate(("L0_ffn_q_scale", "L0_ffn_k_scale")):
                            sp.dma_start(qk_gain[:, i, :], T[n][bass.ds(l, 1), :].broadcast_to((P, BD))).then_inc(wa_ld, 16)
                        sp.wait_ge(x_ffn, l * B + B)
                        sp.dma_start(w1[:, :], T["L0_ffn_W1"][l]).then_inc(wf_ld, 16)
                        w2_d = T["L0_ffn_W2"][l]
                        sp.dma_start(w2[:, 0:2, :], w2_d[0:256, :].rearrange("(k p) c -> p k c", p=P)).then_inc(wf_ld, 16)
                        sp.dma_start(w2[0:FCH[2], 2, :], w2_d[256:FF, :]).then_inc(wf_ld, 16)
                        for part in range(2):
                            b1_d = T["L0_ffn_b1"][l][part * FF:(part + 1) * FF]
                            sp.dma_start(b1[:, 3 * part:3 * part + 2], b1_d[0:256].rearrange("(k p) -> p k", p=P),
                                         allow_slow_non_contiguous=True).then_inc(wf_ld, 16)
                            sp.dma_start(b1[0:FCH[2], 3 * part + 2:3 * part + 3],
                                         b1_d[256:FF].rearrange("(p k) -> p k", k=1),
                                         allow_slow_non_contiguous=True).then_inc(wf_ld, 16)
                        sp.dma_start(b2[:, :], T["L0_ffn_b2"][bass.ds(l, 1), :]).then_inc(wf_ld, 16)

                @block.gpsimd
                def _(pool):
                    with pool.Fori(0, DEPTH) as l:
                        with pool.Fori(0, B) as b:
                            for s in range(NS):
                                m, i = (l * B + b) * NS + s + 1, s % 2
                                pool.wait_ge(floor_done, m)
                                nc.gpsimd.tensor_tensor(rnorm[:, i, :], ss[:, i, :], neghalf[:, :], ALU.pow).then_inc(rn_done, 1)
                                pool.wait_ge(t_done, m)
                                nc.gpsimd.tensor_tensor(rot[:, i, :, :], t1[:, i, :, :], t2[:, i, :, :], ALU.add).then_inc(rot_done, 1)
                                pool.wait_ge(rot_done, m)
                                pool.wait_ge(rn_done, m)
                                nc.gpsimd.tensor_tensor(qk[:, i, :, :], rot[:, i, :, :],
                                                        rnorm[:, i, :, None].broadcast_to((P, 16, BD)),
                                                        ALU.mult).then_inc(qk_done, 1)
                        with pool.Fori(0, NP) as i:
                            n = l * NP + i
                            for q in range(2):
                                pool.wait_ge(var_done, n * 2 + q + 1)
                                nc.gpsimd.tensor_tensor(frstd[:, q, :], fvar[:, q, :], neghalf[:, 0:LT],
                                                        ALU.pow).then_inc(rstd_done, 1)

                @block.tensor
                def _(pe):
                    with pe.Fori(0, DEPTH) as l:
                        def room(part, b, name):
                            i, number = ring_fill(part, l, b, name)
                            pe.wait_ge(ring_free[i], number)
                            return ring[i], ring_full[i]

                        def out_of(part, b, name):
                            i, number = ring_fill(part, l, b, name)
                            pe.wait_ge(ring_free[i], number + 1)

                        def turn_x(seq):
                            pe.wait_ge(x_copied, seq + 1)
                            for t in range(LT):
                                last = nc.tensor.transpose(bank[0][:, t * P:(t + 1) * P], xcur[:, t, :], ident[:, :])
                            last.then_inc(x_full, 1)

                        def turn_qk(part, b, s, m):
                            pe.wait_ge(qk_done, m)
                            for a, name in enumerate("qk"):
                                r, full = room(part, b, (name, s))
                                for p in range(4):
                                    last = nc.tensor.transpose(
                                        r[:, p * P:(p + 1) * P],
                                        qk[:, s % 2, a * 8 + 2 * p:a * 8 + 2 * p + 2, :].rearrange("p h d -> p (h d)"),
                                        ident[:, :])
                                last.then_inc(full, 1)

                        def project(s, m, before):
                            hg, t = s % NS // 2, s % 2
                            if before:
                                pe.wait_ge(t_done, m - 1)
                            for a in range(3):
                                if a == 2 and before:
                                    pe.wait_ge(v_done, m - 1)
                                c = a * INNER + hg * 512
                                last = nc.tensor.matmul(bank[a], xT[:, t * P:(t + 1) * P], wqkv[:, c:c + 512],
                                                        start=True, stop=True)
                                if a == 1:
                                    last.then_inc(qk_full, 1)
                            last.then_inc(v_full, 1)

                        def turn_probs(part, b, s, m):
                            pe.wait_ge(exp_done, m)
                            for half in range(2):
                                r, full = room(part, b, (f"p{half}", s))
                                for h in range(4):
                                    last = nc.tensor.transpose(r[:, h * P:(h + 1) * P], pr[:, s % 2, 4 * half + h, :],
                                                               ident[:, :])
                                last.then_inc(full, 1)
                            if s % 2:
                                r, full = room(part, b, ("pp", s))
                                nc.tensor.matmul(r[:, 0:WIN], pp[:, 0, :], ident[0:WIN, 0:WIN], start=True, stop=True)
                                for h in range(1, 8):
                                    last = nc.tensor.transpose(r[:, h * WIN:(h + 1) * WIN], pp[:, h, :],
                                                               ident[0:WIN, 0:WIN])
                                last.then_inc(full, 1)

                        def scores(part, b, s):
                            t = s % 2
                            out_of(part, b, ("q", s))
                            out_of(part, b, ("k", s))
                            for half in range(2):
                                sc = bank[3 + half]
                                nc.tensor.matmul(sc.rearrange("p (h j) -> p h j", h=4), ident_bf[:, :],
                                                 own_bf[:, None, :].broadcast_to((P, 4, P)),
                                                 start=True, stop=False, skip_group_check=True)
                                for p in range(2):
                                    last = nc.tensor.matmul(
                                        sc[:, p * 2 * P:(p + 1) * 2 * P], qTs[:, 2 * half + p, :],
                                        kz[:, t, 2 * half + p, :, :].rearrange("p h j -> p (h j)"),
                                        start=False, stop=(p == 1), skip_group_check=True)
                            last.then_inc(sc_full, 1)
                            if t:
                                r, full = room(part, b, ("prev", s))
                                sc = r[:, 0:8 * WIN]
                                nc.tensor.matmul(sc.rearrange("p (h j) -> p h j", h=8), ident_bf[:, :],
                                                 prev_bf[:, None, :].broadcast_to((P, 8, WIN)),
                                                 start=True, stop=False, skip_group_check=True)
                                for p in range(4):
                                    last = nc.tensor.matmul(
                                        sc[:, p * 2 * WIN:(p + 1) * 2 * WIN].rearrange("p (h j) -> p h j", h=2),
                                        qTs[:, p, :], kz[:, 0, p, :, P - WIN:P],
                                        start=False, stop=(p == 3), skip_group_check=True)
                                last.then_inc(full, 1)

                        def outputs(part, b, s, m):
                            t = s % 2
                            for half in range(2):
                                out_of(part, b, (f"p{half}", s))
                                if t and not half:
                                    out_of(part, b, ("pp", s))
                                if not half:
                                    pe.wait_ge(v_done, m)
                                r, full = room(part, b, (f"o{half}", s))
                                for h in range(4):
                                    hh = 4 * half + h
                                    c = slice(h * (BD + 1), (h + 1) * (BD + 1))
                                    last = nc.tensor.matmul(r[:, c], prT[:, hh, :], v[:, s % NS, hh, :],
                                                            start=(h == 0), stop=(h == 3 and not t),
                                                            skip_group_check=True)
                                if t:
                                    for h in range(4):
                                        hh = 4 * half + h
                                        c = slice(h * (BD + 1), (h + 1) * (BD + 1))
                                        last = nc.tensor.matmul(r[0:WIN, c], ppT[:, hh, :], v[:, (s - 1) % NS, hh, :],
                                                                start=False, stop=(h == 3), skip_group_check=True)
                                last.then_inc(full, 1)

                        def turn_outputs(part, b, s, m):
                            pe.wait_ge(o_done, 2 * m)
                            r, full = room(part, b, ("oT", s))
                            for p in range(4):
                                last = nc.tensor.transpose(
                                    r[:, p * P:(p + 1) * P],
                                    o[:, 2 * p:2 * p + 2, :].rearrange("p h d -> p (h d)"), ident[:, :])
                            last.then_inc(full, 1)

                        def through_wo(part, b, s):
                            out_of(part, b, ("oT", s))
                            r, full = room(part, b, ("w", s))
                            for p in range(4):
                                last = nc.tensor.matmul(r[:, 0:D], oT[:, p, :], wo[:, 4 * (s // 2) + p, :],
                                                        start=(p == 0), stop=(p == 3))
                            last.then_inc(full, 1)

                        def slots(part, b):
                            ok = lambda step: valid(part, step)
                            for j in SLOTS[part]:
                                m = (l * B + b) * NS + j + 1
                                if j % NS == 0 and ok(j + 4):
                                    if part == "loop":
                                        pe.wait_ge(t_done, m + 3)
                                    turn_x(l * B + b + (j + 4) // NS)
                                if ok(j + 2):
                                    turn_qk(part, b, j + 2, m + 2)
                                if ok(j + 4):
                                    if j % NS == 0:
                                        pe.wait_ge(xT_done, l * B + b + (j + 4) // NS + 1)
                                    project(j + 4, m + 4, before=ok(j + 3))
                                if ok(j + 1):
                                    turn_probs(part, b, j + 1, m + 1)
                                if ok(j):
                                    turn_outputs(part, b, j, m)
                                if ok(j + 2):
                                    scores(part, b, j + 2)
                                if ok(j):
                                    through_wo(part, b, j)
                                if ok(j + 1):
                                    outputs(part, b, j + 1, m + 1)

                        pe.wait_ge(wa_ld, (l + 1) * 16 * N_WA)
                        slots("first", 0)
                        with pe.Fori(0, B - 1) as b:
                            slots("loop", b)
                        slots("last", B - 1)
                        def pair_room(part, i, q, kind):
                            pe.wait_ge(fr_free[q], pair_fill(part, l, i, kind))
                            return fring[q], fr_full[q]

                        def shift_x(part, i, pair, q):
                            r, full = pair_room(part, i, q, "x")
                            r3 = r[:, 0:S].rearrange("p (t c) -> p t c", t=LT)
                            first = pair * 2 * LT + q * LT
                            half = D // 2
                            nc.tensor.matmul(r3[:, :, half:D], shift_in[:, :], X[:, bass.ds(first, LT), half:D],
                                             start=True, stop=False, skip_group_check=True)
                            nc.tensor.matmul(r3[:, 1:2, half:D], shift_over[:, :], X[:, bass.ds(first, 1), half:D],
                                             start=False, stop=False, skip_group_check=True)
                            nc.tensor.matmul(r3[:, :, 0:half], ident[:, :], X[:, bass.ds(first, LT), 0:half],
                                             start=False, stop=True, skip_group_check=True).then_inc(full, 1)

                        def turn_xn(part, i, pair, q):
                            pe.wait_ge(xn_done, (l * NP + pair) * 4 + 2 * q + 2)
                            r, full = pair_room(part, i, q, "xT")
                            for t in range(LT):
                                last = nc.tensor.transpose(r[:, t * P:(t + 1) * P], xn[:, q, t, :], ident[:, :])
                            last.then_inc(full, 1)

                        def hidden(i, q):
                            for k, (c0, c1) in enumerate(((3, 4), (0, 1), (5, 2))):
                                r = bank[3 * q + k]
                                for j, c in enumerate((c0, c1)):
                                    w, f = FCH[c % 3], (c // 3) * FF + 128 * (c % 3)
                                    last = nc.tensor.matmul(r[0:w, j * S:(j + 1) * S], w1[:, f:f + w], xnT[:, q, :],
                                                            start=(j == 0), stop=(j == 1), skip_group_check=True)
                                last.then_inc(hg_full, 1)

                        def pair_outputs(part, i, q):
                            pe.wait_ge(hid_done, (l * NP + i) * 2 + q + 1)
                            r, full = pair_room(part, i, q, "out")
                            nc.tensor.matmul(r[:, 0:S].rearrange("p (t c) -> p t c", t=LT), ones[0:1, :],
                                             b2[:, None, :].broadcast_to((1, LT, D)), start=True, stop=False,
                                             skip_group_check=True)
                            for t in range(LT):
                                for c in range(3):
                                    last = nc.tensor.matmul(r[:, t * D:(t + 1) * D],
                                                            hid[0:FCH[c], q, c, t * P:(t + 1) * P], w2[0:FCH[c], c, :],
                                                            start=False, stop=(t == 1 and c == 2),
                                                            skip_group_check=True)
                            last.then_inc(full, 1)

                        def pair_slot(part, i):
                            ahead = {"first": 0, "loop": i + 1, "last": None}[part]
                            if part != "last":
                                for q in range(2):
                                    shift_x(part, i, ahead, q)
                            if part != "first":
                                for q in range(2):
                                    if part == "loop":
                                        pe.wait_ge(fr_free[q], pair_fill(part, l, i, "x"))
                                    else:
                                        pe.wait_ge(fr_free[q], pair_fill(part, l, i, "out"))
                                    hidden(i, q)
                            if part != "last":
                                for q in range(2):
                                    turn_xn(part, i, ahead, q)
                            if part != "first":
                                for q in range(2):
                                    pair_outputs(part, i, q)

                        for f in ring_free:
                            pe.wait_ge(f, (l + 1) * (B * RL) + 1)
                        pe.wait_ge(wf_ld, (l + 1) * 16 * N_WF)
                        pair_slot("first", 0)
                        with pe.Fori(0, NP - 1) as i:
                            pair_slot("loop", i)
                        pair_slot("last", NP - 1)
                        for f in fr_free:
                            pe.wait_ge(f, (l + 1) * (3 * NP) + 1)

                @block.scalar
                def _(act):
                    with act.Fori(0, DEPTH) as l:
                        act.wait_ge(x_ffn, l * B + B)
                        act.dma_start(lng[:, :], T["L0_ffn_ln_g"][bass.ds(l, 1), :].rearrange("a c -> c a"),
                                      allow_slow_non_contiguous=True).then_inc(wf_ld, 16)
                        act.dma_start(lnb[:, :], T["L0_ffn_ln_b"][bass.ds(l, 1), :].rearrange("a c -> c a"),
                                      allow_slow_non_contiguous=True).then_inc(wf_ld, 16)
                        def take(part, b, name):
                            i, number = ring_fill(part, l, b, name)
                            act.wait_ge(ring_full[i], number)
                            return ring[i], ring_free[i]

                        def copy_x(seq, b):
                            act.wait_ge(x_ffn, seq + 1)
                            nc.scalar.copy(xcur[:, :, :], X[:, bass.ds(b * LT, LT), :]).then_inc(x_copied, 1)

                        def turned_x(seq):
                            act.wait_ge(x_full, seq + 1)
                            r = bank[0]
                            nc.scalar.copy(xT[0:64, 0:S], r[0:64, 0:S])
                            nc.scalar.copy(xT[64:128, 1:S], r[64:128, 0:S - 1]).then_inc(xT_done, 1)

                        def values(part, b, s, m):
                            act.wait_ge(v_full, m)
                            if valid(part, s - 3):
                                i, number = ring_fill(part, l, b, ("o1", s - 3))
                                act.wait_ge(ring_full[i], number)
                            nc.scalar.copy(v[:, s % NS, :, 0:BD],
                                           bank[2].rearrange("p (h d) -> p h d", h=8)).then_inc(v_done, 1)

                        def turned_qk(part, b, s):
                            r, free = take(part, b, ("q", s))
                            nc.scalar.copy(qTs[:, :, :], r.rearrange("p (a i) -> p a i", a=4)).then_inc(free, 1)
                            r, free = take(part, b, ("k", s))
                            for j in range(2):
                                last = nc.scalar.copy(kz[64 * j:64 * j + 64, s % 2, :, j, :],
                                                      r[64 * j:64 * j + 64, :].rearrange("p (a i) -> p a i", a=4))
                            last.then_inc(free, 1)

                        def squares(m, before):
                            act.wait_ge(qk_full, m)
                            if before:
                                act.wait_ge(ss_done, m - 1)
                            nc.scalar.activation(sq[:, :], psum[:, 0:2, :].rearrange("p a c -> p (a c)"),
                                                 ACT.Square).then_inc(sq_done, 1)

                        def turned_probs(part, b, s):
                            for half in range(2):
                                r, free = take(part, b, (f"p{half}", s))
                                nc.scalar.copy(prT[:, 4 * half:4 * half + 4, :],
                                               r.rearrange("p (h i) -> p h i", h=4)).then_inc(free, 1)
                            if s % 2:
                                r, free = take(part, b, ("pp", s))
                                nc.scalar.copy(ppT[:, :, :], r[:, 0:8 * WIN].rearrange("p (h i) -> p h i", h=8)
                                               ).then_inc(free, 1)

                        def turned_outputs(part, b, s):
                            r, free = take(part, b, ("oT", s))
                            nc.scalar.copy(oT[:, :, :], r.rearrange("p (a i) -> p a i", a=4)).then_inc(free, 1)

                        def exps(s, m):
                            act.wait_ge(sub_done, m)
                            if s % 2:
                                nc.scalar.activation(pp[:, :, P - WIN:P], pp0[:, :, :], ACT.Exp)
                            nc.scalar.activation(pr[:, s % 2, :, :], pr[:, s % 2, :, :], ACT.Exp).then_inc(exp_done, 1)

                        def slots(part, b):
                            ok = lambda step: valid(part, step)
                            for j in SLOTS[part]:
                                m = (l * B + b) * NS + j + 1
                                seq = l * B + b + (j + 4) // NS
                                if j % NS == 0 and ok(j + 4):
                                    copy_x(seq, b + (j + 4) // NS)
                                if ok(j + 3):
                                    values(part, b, j + 3, m + 3)
                                if j % NS == 0 and ok(j + 4):
                                    turned_x(seq)
                                if ok(j + 2):
                                    turned_qk(part, b, j + 2)
                                if ok(j + 4):
                                    squares(m + 4, before=ok(j + 3))
                                if ok(j + 1):
                                    turned_probs(part, b, j + 1)
                                if ok(j):
                                    turned_outputs(part, b, j)
                                if ok(j + 2):
                                    exps(j + 2, m + 2)

                        slots("first", 0)
                        with act.Fori(0, B - 1) as b:
                            slots("loop", b)
                        slots("last", B - 1)
                        def gates(i, q):
                            for k, c in ((0, 0), (0, 1), (2, 2)):
                                act.wait_ge(hg_full, (l * NP + i) * 6 + 3 * q + k + 1)
                                w = FCH[c]
                                r = bank[3 * q + k][0:w, (c % 2) * S:(c % 2) * S + S]
                                last = nc.scalar.activation(gel[0:w, q, c, :], r, ACT.Gelu,
                                                            bias=b1[0:w, 3 + c:4 + c])
                            last.then_inc(gel_done, 1)

                        def turned_xn(part, i, q):
                            act.wait_ge(fr_full[q], pair_fill(part, l, i, "xT"))
                            nc.scalar.activation(xnT[:, q, :], fring[q][:, 0:S], ACT.Identity, bias=lnb[:, 0:1],
                                                 scale=lng[:, 0:1]).then_inc(fr_free[q], 1)

                        def pair_slot(part, i):
                            if part != "first":
                                for q in range(2):
                                    gates(i, q)
                            if part != "last":
                                for q in range(2):
                                    turned_xn(part, i, q)

                        act.wait_ge(wf_ld, (l + 1) * 16 * N_WF)
                        pair_slot("first", 0)
                        with act.Fori(0, NP - 1) as i:
                            pair_slot("loop", i)
                        pair_slot("last", NP - 1)

                @block.vector
                def _(dve):
                    for f in (*ring_free, *fr_free):
                        dve.sem_inc(f, 1)
                    dve.sem_inc(x_ffn, B)
                    dve.sem_inc(x_attn, 1)
                    with dve.Fori(0, DEPTH) as l:
                        dve.wait_ge(wa_ld, (l + 1) * 16 * N_WA)
                        g2 = lambda c: qk_gain[:, None, :, c].broadcast_to((P, LT, 2, BD if c == slice(0, BD) else BD // 2))
                        lo, hi = slice(0, BD // 2), slice(BD // 2, BD)
                        nc.vector.tensor_tensor(cosg[:, :, :, :], cos0[:, :, :, :], g2(slice(0, BD)), ALU.mult).then_inc(gains, 1)
                        nc.vector.tensor_tensor(sing[:, :, :, lo], sin0[:, :, :, lo], g2(hi), ALU.mult).then_inc(gains, 1)
                        nc.vector.tensor_tensor(sing[:, :, :, hi], sin0[:, :, :, hi], g2(lo), ALU.mult).then_inc(gains, 1)
                        def take(part, b, name):
                            i, number = ring_fill(part, l, b, name)
                            dve.wait_ge(ring_full[i], number)
                            return ring[i], ring_free[i]

                        def rotate(part, s, m):
                            t, two_back = s % 2, valid(part, s - 2)
                            dve.wait_ge(sq_done, m)
                            if two_back:
                                dve.wait_ge(rn_done, m - 2)
                            nc.vector.tensor_reduce(ss[:, t, :], sq[:, :].rearrange("p (h d) -> p h d", d=BD), AX.X,
                                                    ALU.add).then_inc(ss_done, 1)
                            dve.wait_ge(ss_done, m)
                            nc.vector.tensor_scalar(ss[:, t, :], ss[:, t, :], 1e-24, None, ALU.max).then_inc(floor_done, 1)
                            x4 = psum[:, 0:2, :].rearrange("p a (h d) -> p a h d", d=BD)
                            t14 = t1[:, t, :, :].rearrange("p (a h) d -> p a h d", a=2)
                            t24 = t2[:, t, :, :].rearrange("p (a h) d -> p a h d", a=2)
                            tab = lambda g, c, w: g[:, t, :, None, c].broadcast_to((P, 2, 8, w))
                            if two_back:
                                dve.wait_ge(rot_done, m - 2)
                            nc.vector.tensor_tensor(t14, x4, tab(cosg, slice(0, BD), BD), ALU.mult)
                            nc.vector.tensor_tensor(t24[:, :, :, lo], x4[:, :, :, hi], tab(sing, lo, BD // 2), ALU.mult)
                            nc.vector.tensor_tensor(t24[:, :, :, hi], x4[:, :, :, lo], tab(sing, hi, BD // 2),
                                                    ALU.mult).then_inc(t_done, 1)

                        def less_maxima(part, b, s, m):
                            t = s % 2
                            odd = (l * B + b) * (NS // 2) + s // 2 + 1
                            dve.wait_ge(sc_full, m)
                            own = psum[:, 3:5, :].rearrange("p a (h j) -> p (a h) j", h=4)
                            nc.vector.tensor_reduce(m_own[:, :], own, AX.X, ALU.max).then_inc(mo_done, 1)
                            if t:
                                r, free = take(part, b, ("prev", s))
                                prev = r[0:WIN, 0:8 * WIN].rearrange("p (h j) -> p h j", h=8)
                                nc.vector.tensor_reduce(m_prev[:, :], prev, AX.X, ALU.max).then_inc(mp_done, 1)
                                dve.wait_ge(mo_done, m)
                                dve.wait_ge(mp_done, odd)
                                nc.vector.tensor_tensor(m_own[0:WIN, :], m_own[0:WIN, :], m_prev[:, :],
                                                        ALU.max).then_inc(mx_done, 1)
                                dve.wait_ge(mx_done, odd)
                                nc.vector.tensor_tensor(pp0[:, :, :], prev,
                                                        m_own[0:WIN, :, None].broadcast_to((WIN, 8, WIN)),
                                                        ALU.subtract).then_inc(free, 1)
                            else:
                                dve.wait_ge(mo_done, m)
                            nc.vector.tensor_tensor(pr[:, t, :, :], own, m_own[:, :, None].broadcast_to((P, 8, P)),
                                                    ALU.subtract).then_inc(sub_done, 1)

                        def residual(part, b, s, m):
                            r, free = take(part, b, ("w", s))
                            xt = X[:, bass.ds(b * LT + s % 2, 1), :].rearrange("p a c -> p (a c)")
                            nc.vector.tensor_tensor(xt, r[:, 0:D], xt, ALU.add).then_inc(x_attn, 1)
                            dve.wait_ge(x_attn, m + 1)
                            dve.sem_inc(free, 1)

                        def normalise(part, b, s, m):
                            for half in range(2):
                                r, free = take(part, b, (f"o{half}", s))
                                r4 = r[:, 0:4 * (BD + 1)].rearrange("p (h d) -> p h d", h=4)
                                hs = slice(4 * half, 4 * half + 4)
                                nc.vector.reciprocal(rs[:, hs], r4[:, :, BD]).then_inc(rs_done, 1)
                                dve.wait_ge(rs_done, 2 * (m - 1) + half + 1)
                                nc.vector.tensor_tensor(o[:, hs, :], r4[:, :, 0:BD],
                                                        rs[:, hs, None].broadcast_to((P, 4, BD)),
                                                        ALU.mult).then_inc(o_done, 1)
                                dve.wait_ge(o_done, 2 * (m - 1) + half + 1)
                                dve.sem_inc(free, 1)

                        def slots(part, b):
                            ok = lambda step: valid(part, step)
                            for j in SLOTS[part]:
                                m = (l * B + b) * NS + j + 1
                                if ok(j + 4):
                                    rotate(part, j + 4, m + 4)
                                if ok(j + 2):
                                    less_maxima(part, b, j + 2, m + 2)
                                if ok(j):
                                    residual(part, b, j, m)
                                if ok(j + 1):
                                    normalise(part, b, j + 1, m + 1)

                        dve.wait_ge(gains, l * 3 + 3)
                        slots("first", 0)
                        with dve.Fori(0, B - 1) as b:
                            slots("loop", b)
                        slots("last", B - 1)
                        def norm_x(part, i, pair, q):
                            n = l * NP + pair
                            xs = fring[q][:, 0:S].rearrange("p (t c) -> p t c", t=LT)
                            dve.wait_ge(fr_full[q], pair_fill(part, l, i, "x"))
                            nc.vector.memset(pause[:, :], 0.0)
                            for t in range(LT):
                                nc.vector.bn_stats(st6[:, q, t, :], xs[:, t, :]).then_inc(st_done, 1)
                            dve.wait_ge(st_done, n * 4 + 2 * q + 2)
                            nc.vector.memset(pause[:, :], 0.0)
                            for t in range(LT):
                                nc.vector.bn_aggr(mv[:, q, t, :], st6[:, q, t, :]).then_inc(mv_done, 1)
                            dve.wait_ge(mv_done, n * 4 + 2 * q + 2)
                            nc.vector.tensor_scalar(fvar[:, q, :], mv[:, q, :, 1], EPS, None,
                                                    ALU.add).then_inc(var_done, 1)

                        def scale_x(part, i, pair, q):
                            n = l * NP + pair
                            xs = fring[q][:, 0:S].rearrange("p (t c) -> p t c", t=LT)
                            dve.wait_ge(rstd_done, n * 2 + q + 1)
                            for t in range(LT):
                                nc.vector.tensor_scalar(xn[:, q, t, :], xs[:, t, :], mv[:, q, t, 0:1],
                                                        frstd[:, q, t:t + 1], ALU.subtract,
                                                        ALU.mult).then_inc(xn_done, 1)
                            dve.wait_ge(xn_done, n * 4 + 2 * q + 2)
                            dve.sem_inc(fr_free[q], 1)

                        def gated(i, q):
                            n = l * NP + i
                            dve.wait_ge(hg_full, n * 6 + 3 * q + 3)
                            dve.wait_ge(gel_done, n * 2 + q + 1)
                            for c in range(3):
                                w = FCH[c]
                                r = bank[3 * q + (2 if c == 2 else 1)]
                                r = r[0:w, S:2 * S] if c in (1, 2) else r[0:w, 0:S]
                                last = nc.vector.scalar_tensor_tensor(
                                    out=hid[0:w, q, c, :], in0=r, scalar=b1[0:w, c:c + 1],
                                    in1=gel[0:w, q, c, :], op0=ALU.add, op1=ALU.mult)
                            last.then_inc(hid_done, 1)

                        def pair_residual(part, i, q):
                            dve.wait_ge(fr_full[q], pair_fill(part, l, i, "out"))
                            xt = X[:, bass.ds(i * 2 * LT + q * LT, LT), :]
                            nc.vector.tensor_tensor(xt, fring[q][:, 0:S].rearrange("p (t c) -> p t c", t=LT), xt,
                                                    ALU.add).then_inc(x_ffn, 1)
                            dve.wait_ge(x_ffn, B + (l * NP + i) * 2 + q + 1)
                            dve.sem_inc(fr_free[q], 1)

                        def pair_slot(part, i):
                            ahead = {"first": 0, "loop": i + 1, "last": None}[part]
                            if part != "last":
                                for q in range(2):
                                    norm_x(part, i, ahead, q)
                                for q in range(2):
                                    scale_x(part, i, ahead, q)
                            if part != "first":
                                for q in range(2):
                                    gated(i, q)
                                for q in range(2):
                                    pair_residual(part, i, q)

                        dve.wait_ge(wf_ld, (l + 1) * 16 * N_WF)
                        pair_slot("first", 0)
                        with dve.Fori(0, NP - 1) as i:
                            pair_slot("loop", i)
                        pair_slot("last", NP - 1)

        layer_norm("ln2", residual=XR)
        if stop == 2:
            return store_stream("stop")

        with ExitStack() as st:
            wqkv_c = sb(st, "c_wqkv", [P, 3 * D])
            bias_q, bias_k = sb(st, "c_bias_q", [P, 1]), sb(st, "c_bias_k", [P, 1])
            bias_v, bias_o = sb(st, "c_bias_v", [1, D]), sb(st, "c_bias_o", [1, D])
            wout = sb(st, "c_wout", [P, D])
            kmask = sb(st, "c_kmask", [P, H])
            mask0 = sb(st, "c_mask0", [P, P])
            mask_in, mask_all = sb(st, "c_mask_in", [P, P], BF16), sb(st, "c_mask_all", [P, P], BF16)
            ident80 = sb(st, "c_ident80", [P, P], BF16)
            qT = sb(st, "c_qT", [P, S])
            k_diag = sb(st, "c_k_diag", [P, H, S])
            vones = sb(st, "c_vones", [P, LT, H, HD + 1])
            probs = sb(st, "c_probs", [P, 2, 4, S])
            probsT = sb(st, "c_probsT", [P, LT, LT, H, P])
            nmax = sb(st, "c_nmax", [P, 2, 4])
            rsum = sb(st, "c_rsum", [P, H])
            o = sb(st, "c_o", [P, H, HD])
            oT = sb(st, "c_oT", [P, P])

            ld, cset = sem("c_ld"), sem("c_set")
            with nc.Block() as block:
                @block.sync
                def _(sp):
                    bq = T["L1_attn_bqkv"]
                    sp.dma_start(wqkv_c[:, :], T["L1_attn_Wqkv"]).then_inc(ld, 16)
                    sp.dma_start(wout[:, :], T["L1_attn_Wout"]).then_inc(ld, 16)
                    sp.dma_start(bias_q[:, :], bq[0:D].rearrange("(p a) -> p a", a=1),
                                 allow_slow_non_contiguous=True).then_inc(ld, 16)
                    sp.dma_start(bias_k[:, :], bq[D:2 * D].rearrange("(p a) -> p a", a=1),
                                 allow_slow_non_contiguous=True).then_inc(ld, 16)
                    sp.dma_start(bias_v[:, :], bq[2 * D:3 * D].rearrange("(a p) -> a p", a=1)).then_inc(ld, 16)
                    sp.dma_start(bias_o[:, :], T["L1_attn_bout"].rearrange("(a p) -> a p", a=1)).then_inc(ld, 16)
                    sp.dma_start(mask0[:, :], T["causal"]).then_inc(ld, 16)
                    sp.wait_ge(ld, 16 * 7)

                @block.gpsimd
                def _(pool):
                    nc.gpsimd.memset(vones[:, :, :, :], 1.0)

                @block.vector
                def _(dve):
                    nc.vector.memset(mask_all[:, :], -125.0)
                    nc.vector.tensor_scalar(ident80[:, :], ident[:, :], 80.0, None, ALU.mult)
                    nc.vector.tensor_scalar(kmask[:, :], gmask[:, :], SCALE_A, None, ALU.mult)
                    dve.wait_ge(ld, 16 * 7)
                    nc.vector.tensor_copy(mask_in[:, :], mask0[:, :])

            names = [("x", 0), ("x", 1), "qk", "v"] + [(k, t) for t in range(LT) for k in ("o", "oT", "w")]
            FC = len(names)
            assert FC % 2 == 0
            at_c = {n: i for i, n in enumerate(names)}
            ring, score, turned = bank[0:2], [psum[:, 2:4, :], psum[:, 4:6, :]], bank[6:8]
            x_copied, ring_full, ring_free = sem("c_x_copied"), [sem("c_ring_full0"), sem("c_ring_full1")], \
                [sem("c_ring_free0"), sem("c_ring_free1")]
            score_full, max_ok, exp_done = sem("c_score_full"), sem("c_max_ok"), sem("c_exp_done")
            turn_full, turn_out, rsum_ok, o_ok = sem("c_turn_full"), sem("c_turn_out"), sem("c_rsum_ok"), sem("c_o_ok")

            def filled_c(b, i):
                return b * (FC // 2) + i // 2 + 1

            with nc.Block() as block:
                @block.gpsimd
                def _(pool):
                    with pool.Fori(0, B) as b:
                        nc.gpsimd.tensor_copy(xcur[:, :, :], X[:, bass.ds(b * LT, LT), :]).then_inc(x_copied, 1)
                        pool.wait_ge(ring_full[1], filled_c(b, 1))

                @block.tensor
                def _(pe):
                    with pe.Fori(0, B) as b:
                        def room(name):
                            i = at_c[name]
                            if i >= 2:
                                pe.wait_ge(ring_free[i % 2], filled_c(b, i - 2))
                            return ring[i % 2], ring_full[i % 2]

                        def out_of(name):
                            i = at_c[name]
                            pe.wait_ge(ring_free[i % 2], filled_c(b, i))

                        def scores(s):
                            lt, hq = s // 4, s % 4
                            if s >= 2:
                                pe.wait_ge(exp_done, b * 8 + s - 1)
                            for mt in range(LT):
                                sc = score[s % 2][:, mt, :]
                                last = nc.tensor.matmul(sc.rearrange("p (h m) -> p h m", h=4),
                                                        qT[:, lt * P:(lt + 1) * P],
                                                        k_diag[:, hq * 4:hq * 4 + 4, mt * P:(mt + 1) * P],
                                                        start=True, stop=(mt < lt), skip_group_check=True)
                                if mt >= lt:
                                    mask = mask_in if mt == lt else mask_all
                                    last = nc.tensor.matmul(sc.rearrange("p (h m) -> p h m", h=4), ident80[:, :],
                                                            mask[:, None, :].broadcast_to((P, 4, P)),
                                                            start=False, stop=True, skip_group_check=True)
                            last.then_inc(score_full, 1)

                        def turn(s):
                            pe.wait_ge(exp_done, b * 8 + s + 1)
                            if s >= 1:
                                pe.wait_ge(turn_out, b * 8 + s)
                            for mt in range(LT):
                                for h in range(4):
                                    last = nc.tensor.transpose(turned[mt][:, h * P:(h + 1) * P],
                                                               probs[:, s % 2, h, mt * P:(mt + 1) * P], ident[:, :])
                            last.then_inc(turn_full, 1)

                        def outputs(lt):
                            pe.wait_ge(turn_out, b * 8 + 4 * lt + 4)
                            r, full = room(("o", lt))
                            for h in range(H):
                                for mt in range(LT):
                                    last = nc.tensor.matmul(r[:, h * (HD + 1):(h + 1) * (HD + 1)],
                                                            probsT[:, lt, mt, h, :], vones[:, mt, h, :],
                                                            start=(h == 0 and mt == 0), stop=(h == H - 1 and mt == 1),
                                                            skip_group_check=True)
                            last.then_inc(full, 1)

                        def turn_outputs(lt):
                            pe.wait_ge(o_ok, b * LT + lt + 1)
                            r, full = room(("oT", lt))
                            nc.tensor.transpose(r[:, 0:P], o[:, :, :].rearrange("p h d -> p (h d)"),
                                                ident[:, :]).then_inc(full, 1)

                        def project(lt):
                            out_of(("oT", lt))
                            r, full = room(("w", lt))
                            nc.tensor.matmul(r[:, 0:D], oT[:, :], wout[:, :], start=True, stop=False)
                            nc.tensor.matmul(r[:, 0:D], ones[0:1, :], bias_o[:, :], start=False,
                                             stop=True).then_inc(full, 1)

                        pe.wait_ge(x_copied, b + 1)
                        for t in range(LT):
                            r, full = room(("x", t))
                            nc.tensor.transpose(r[:, 0:P], xcur[:, t, :], ident[:, :]).then_inc(full, 1)
                        r, full = room("qk")
                        out_of(("x", 1))
                        nc.tensor.matmul(r[:, 0:S], wqkv_c[:, 0:D], xT[:, :], start=True, stop=False,
                                         skip_group_check=True)
                        nc.tensor.matmul(r[:, S:2 * S], wqkv_c[:, D:2 * D], xT[:, :], start=False, stop=True,
                                         skip_group_check=True).then_inc(full, 1)
                        r, full = room("v")
                        for t in range(LT):
                            c = slice(t * D, (t + 1) * D)
                            nc.tensor.matmul(r[:, c], xT[:, t * P:(t + 1) * P], wqkv_c[:, 2 * D:3 * D],
                                             start=(t == 0), stop=False, skip_group_check=True)
                            last = nc.tensor.matmul(r[:, c], ones[0:1, :], bias_v[:, :], start=False, stop=(t == 1),
                                                    skip_group_check=True)
                        last.then_inc(full, 1)
                        out_of("qk")
                        scores(0)
                        scores(1)
                        turn(0)
                        scores(2)
                        turn(1)
                        scores(3)
                        turn(2)
                        scores(4)
                        turn(3)
                        out_of("v")
                        outputs(0)
                        scores(5)
                        turn(4)
                        turn_outputs(0)
                        scores(6)
                        turn(5)
                        project(0)
                        scores(7)
                        turn(6)
                        turn(7)
                        outputs(1)
                        turn_outputs(1)
                        project(1)
                        for i in (FC - 2, FC - 1):
                            pe.wait_ge(ring_free[i % 2], filled_c(b, i))

                @block.scalar
                def _(act):
                    with act.Fori(0, B) as b:
                        def exps(s):
                            act.wait_ge(max_ok, b * 8 + s + 1)
                            for h in range(4):
                                last = nc.scalar.activation(
                                    probs[:, s % 2, h, :].rearrange("p (t m) -> p t m", t=LT),
                                    score[s % 2][:, :, h * P:(h + 1) * P], ACT.Exp, bias=nmax[:, s % 2, h:h + 1])
                            last.then_inc(exp_done, 1)

                        def turns(s):
                            lt, hq = s // 4, s % 4
                            act.wait_ge(turn_full, b * 8 + s + 1)
                            for mt in range(LT):
                                last = nc.scalar.copy(probsT[:, lt, mt, hq * 4:hq * 4 + 4, :],
                                                      turned[mt].rearrange("p (h l) -> p h l", h=4))
                            last.then_inc(turn_out, 1)

                        for s in range(8):
                            exps(s)
                            if s:
                                turns(s - 1)
                        turns(7)

                @block.vector
                def _(dve):
                    with dve.Fori(0, B) as b:
                        def take(name):
                            i = at_c[name]
                            dve.wait_ge(ring_full[i % 2], filled_c(b, i))
                            return ring[i % 2], ring_free[i % 2]

                        def maxima(s):
                            dve.wait_ge(score_full, b * 8 + s + 1)
                            nc.vector.tensor_reduce(nmax[:, s % 2, :],
                                                    score[s % 2].rearrange("p t (h m) -> p h t m", h=4),
                                                    AX.XY, ALU.max, negate=True).then_inc(max_ok, 1)

                        def outputs(lt):
                            r, free = take(("o", lt))
                            r3 = r[:, 0:H * (HD + 1)].rearrange("p (h d) -> p h d", h=H)
                            nc.vector.reciprocal(rsum[:, :], r3[:, :, 0]).then_inc(rsum_ok, 1)
                            dve.wait_ge(rsum_ok, b * LT + lt + 1)
                            nc.vector.tensor_tensor(o[:, :, :], r3[:, :, 1:HD + 1],
                                                    rsum[:, :, None].broadcast_to((P, H, HD)),
                                                    ALU.mult).then_inc(o_ok, 1)
                            dve.wait_ge(o_ok, b * LT + lt + 1)
                            dve.sem_inc(free, 1)

                        def turn_outputs(lt):
                            r, free = take(("oT", lt))
                            nc.vector.tensor_copy(oT[:, :], r[:, 0:P]).then_inc(free, 1)

                        def project(lt):
                            r, free = take(("w", lt))
                            xt = X[:, bass.ds(b * LT + lt, 1), :].rearrange("p a c -> p (a c)")
                            nc.vector.tensor_tensor(xt, r[:, 0:D], xt, ALU.add).then_inc(free, 1)

                        for t in range(LT):
                            r, free = take(("x", t))
                            nc.vector.tensor_copy(xT[:, t * P:(t + 1) * P], r[:, 0:P]).then_inc(free, 1)
                        r, free = take("qk")
                        nc.vector.tensor_scalar(qT[:, :], r[:, 0:S], bias_q[:, 0:1], None, ALU.add)
                        nc.vector.scalar_tensor_tensor(out=k_diag[:, :, :], in0=r[:, None, S:2 * S].broadcast_to((P, H, S)),
                                                       scalar=bias_k[:, 0:1], in1=kmask[:, :, None].broadcast_to((P, H, S)),
                                                       op0=ALU.add, op1=ALU.mult).then_inc(free, 1)
                        r, free = take("v")
                        nc.vector.tensor_copy(vones[:, :, :, 1:HD + 1],
                                              r[:, 0:LT * D].rearrange("p (t h d) -> p t h d", t=LT, h=H)
                                              ).then_inc(free, 1)
                        for s in range(5):
                            maxima(s)
                        outputs(0)
                        maxima(5)
                        turn_outputs(0)
                        maxima(6)
                        project(0)
                        maxima(7)
                        outputs(1)
                        turn_outputs(1)
                        project(1)

        layer_norm("ln3")
        if stop == 3:
            return store_stream("stop")

        with ExitStack() as st:
            gate_w = sb(st, "d_gate_w", [P, NEXP])
            w1 = sb(st, "d_w1", [P, NEXP, EH])
            b1 = sb(st, "d_b1", [P, NPR])
            w2 = sb(st, "d_w2", [P, NPR, D])
            b2 = sb(st, "d_b2", [NEXP, D])
            rows = sb(st, "d_rows", [NEXP, NPR, P])
            lower = sb(st, "d_lower", [P, NEXP, NEXP])
            xT_all = sb(st, "d_xT_all", [P, B * S])
            gmax, gsum, grec, tokw = (sb(st, n, [P, 1]) for n in ("d_gmax", "d_gsum", "d_grec", "d_tokw"))
            gexp, gate, rank, sel = (sb(st, n, [P, NEXP]) for n in ("d_gexp", "d_gate", "d_rank", "d_sel"))
            above, equal = (sb(st, n, [P, NEXP, NEXP]) for n in ("d_above", "d_equal"))
            coef = sb(st, "d_coef", [P, LT, NEXP])
            coefT_all = sb(st, "d_coefT_all", [NEXP, B * S])
            coefT = sb(st, "d_coefT", [NEXP, S])
            hid = sb(st, "d_hid", [P, NPR, S])
            hidw = sb(st, "d_hidw", [P, NPR, S])

            ld = sem("d_ld")
            x_copied, xT_full, xT_ok, lg_full, ct_full, ct_ok = (
                sem(f"d_{n}") for n in ("x_copied", "xT_full", "xT_ok", "lg_full", "ct_full", "ct_ok"))
            max_ok, exp_ok, rec_ok, gate_ok, cmp_ok, rank_ok, sel_ok, tokw_ok, coef_ok, kept_ok = (
                sem(f"d_{n}") for n in ("max_ok", "exp_ok", "rec_ok", "gate_ok", "cmp_ok", "rank_ok", "sel_ok",
                                        "tokw_ok", "coef_ok", "kept_ok"))
            with nc.Block() as block:
                @block.sync
                def _(sp):
                    sp.dma_start(gate_w[:, :], T["L1_ffn_gate_w"]).then_inc(ld, 16)
                    sp.dma_start(lower[:, :, :].rearrange("p a c -> p (a c)"), T["lower"]).then_inc(ld, 16)
                    sp.dma_start(w1[:, :, :], T["L1_ffn_w1"].rearrange("e d h -> d e h")).then_inc(ld, 16)
                    sp.dma_start(b1[:, :], T["L1_ffn_b1"].rearrange("(a e) h -> (e h) a", e=2),
                                 allow_slow_non_contiguous=True).then_inc(ld, 16)
                    sp.dma_start(w2[:, :, :], T["L1_ffn_w2"].rearrange("(a e) h d -> (e h) a d", e=2)).then_inc(ld, 16)
                    sp.dma_start(b2[:, :], T["L1_ffn_b2"]).then_inc(ld, 16)
                    sp.dma_start(rows[:, :, :].rearrange("p a c -> p (a c)"), T["expert_rows"]).then_inc(ld, 16)
                    sp.wait_ge(ld, 16 * 7)

            xT_b, lg_b, ct_b = bank[0], bank[1], bank[2]
            with nc.Block() as block:
                @block.gpsimd
                def _(pool):
                    with pool.Fori(0, B) as b:
                        nc.gpsimd.tensor_copy(xcur[:, :, :], X[:, bass.ds(b * LT, LT), :]).then_inc(x_copied, 1)
                        pool.wait_ge(xT_full, b + 1)

                @block.tensor
                def _(pe):
                    with pe.Fori(0, B) as b:
                        pe.wait_ge(x_copied, b + 1)
                        for t in range(LT):
                            last = nc.tensor.transpose(xT_b[:, t * P:(t + 1) * P], xcur[:, t, :], ident[:, :])
                        last.then_inc(xT_full, 1)
                        pe.wait_ge(xT_ok, b + 1)
                        for t in range(LT):
                            last = nc.tensor.matmul(lg_b[:, t * NEXP:(t + 1) * NEXP], xT[:, t * P:(t + 1) * P],
                                                    gate_w[:, :], start=(t == 0), stop=(t == 1), skip_group_check=True)
                        last.then_inc(lg_full, 1)
                        pe.wait_ge(coef_ok, b * LT + LT)
                        for t in range(LT):
                            last = nc.tensor.transpose(ct_b[0:NEXP, t * P:(t + 1) * P], coef[:, t, :], ident[:, :])
                        last.then_inc(ct_full, 1)

                @block.scalar
                def _(act):
                    with act.Fori(0, B) as b:
                        act.wait_ge(xT_full, b + 1)
                        nc.scalar.copy(xT[:, :], xT_b[:, 0:S])
                        nc.scalar.copy(xT_all[:, bass.ds(b * S, S)], xT_b[:, 0:S]).then_inc(xT_ok, 1)
                        for t in range(LT):
                            act.wait_ge(max_ok, b * LT + t + 1)
                            nc.scalar.activation(gexp[:, :], lg_b[:, t * NEXP:(t + 1) * NEXP], ACT.Exp,
                                                 bias=gmax[:, 0:1], accum_out=gsum[:, 0:1]).then_inc(exp_ok, 1)
                        act.wait_ge(ct_full, b + 1)
                        nc.scalar.copy(coefT_all[:, bass.ds(b * S, S)], ct_b[0:NEXP, 0:S]).then_inc(ct_ok, 1)

                @block.vector
                def _(dve):
                    with dve.Fori(0, B) as b:
                        dve.wait_ge(lg_full, b + 1)
                        for t in range(LT):
                            m = b * LT + t + 1
                            nc.vector.tensor_reduce(gmax[:, :], lg_b[:, t * NEXP:(t + 1) * NEXP], AX.X, ALU.max,
                                                    negate=True).then_inc(max_ok, 1)
                            dve.wait_ge(exp_ok, m)
                            nc.vector.reciprocal(grec[:, :], gsum[:, :]).then_inc(rec_ok, 1)
                            dve.wait_ge(rec_ok, m)
                            nc.vector.tensor_scalar(gate[:, :], gexp[:, :], grec[:, 0:1], None, ALU.mult).then_inc(gate_ok, 1)
                            dve.wait_ge(gate_ok, m)
                            mine = gate[:, :, None].broadcast_to((P, NEXP, NEXP))
                            other = gate[:, None, :].broadcast_to((P, NEXP, NEXP))
                            nc.vector.tensor_tensor(above[:, :, :], other, mine, ALU.is_gt).then_inc(cmp_ok, 1)
                            nc.vector.tensor_tensor(equal[:, :, :], other, mine, ALU.is_equal).then_inc(cmp_ok, 1)
                            dve.wait_ge(cmp_ok, 4 * m - 2)
                            nc.vector.tensor_tensor(equal[:, :, :], equal[:, :, :], lower[:, :, :], ALU.mult).then_inc(cmp_ok, 1)
                            dve.wait_ge(cmp_ok, 4 * m - 1)
                            nc.vector.tensor_tensor(above[:, :, :], above[:, :, :], equal[:, :, :], ALU.add).then_inc(cmp_ok, 1)
                            dve.wait_ge(cmp_ok, 4 * m)
                            nc.vector.tensor_reduce(rank[:, :], above[:, :, :], AX.X, ALU.add).then_inc(rank_ok, 1)
                            dve.wait_ge(rank_ok, m)
                            nc.vector.tensor_scalar(sel[:, :], rank[:, :], 2.0, None, ALU.is_lt).then_inc(sel_ok, 1)
                            dve.wait_ge(sel_ok, m)
                            nc.vector.tensor_tensor(rank[:, :], sel[:, :], gate[:, :], ALU.mult).then_inc(kept_ok, 1)
                            dve.wait_ge(kept_ok, m)
                            nc.vector.tensor_reduce(tokw[:, :], rank[:, :], AX.X, ALU.add).then_inc(tokw_ok, 1)
                            dve.wait_ge(tokw_ok, m)
                            nc.vector.tensor_scalar(coef[:, t, :], sel[:, :], tokw[:, 0:1], None, ALU.mult).then_inc(coef_ok, 1)

            c_copied, h_full, h_ok, cb_full, hw_ok, o_full, o_out, c_used = (
                sem(f"d2_{n}") for n in ("c_copied", "h_full", "h_ok", "cb_full", "hw_ok", "o_full", "o_out", "c_used"))
            h_b, cb_b, o_b = psum[:, 0:2, :], psum[:, 2:4, :], psum[:, 4:6, :]
            with nc.Block() as block:
                @block.gpsimd
                def _(pool):
                    with pool.Fori(0, B) as b:
                        nc.gpsimd.tensor_copy(coefT[:, :], coefT_all[:, bass.ds(b * S, S)]).then_inc(c_copied, 1)
                        pool.wait_ge(o_full, b * LT + LT)

                @block.tensor
                def _(pe):
                    with pe.Fori(0, B) as b:
                        for a in range(NPR):
                            last = nc.tensor.matmul(h_b[:, a // 2, (a % 2) * S:(a % 2) * S + S],
                                                    w1[:, 2 * a:2 * a + 2, :].rearrange("p e h -> p (e h)"),
                                                    xT_all[:, bass.ds(b * S, S)], start=(a % 2 == 0), stop=(a % 2 == 1),
                                                    skip_group_check=True)
                        last.then_inc(h_full, 1)
                        pe.wait_ge(c_copied, b + 1)
                        for a in range(NPR):
                            last = nc.tensor.matmul(cb_b[:, a // 2, (a % 2) * S:(a % 2) * S + S], rows[:, a, :],
                                                    coefT[:, :], start=(a % 2 == 0), stop=(a % 2 == 1),
                                                    skip_group_check=True)
                        last.then_inc(cb_full, 1)
                        pe.wait_ge(hw_ok, b + 1)
                        for t in range(LT):
                            c = slice(t * P, (t + 1) * P)
                            for a in range(NPR):
                                nc.tensor.matmul(o_b[:, t, 0:D], hidw[:, a, c], w2[:, a, :], start=(a == 0), stop=False)
                            nc.tensor.matmul(o_b[:, t, 0:D], coefT[:, c], b2[:, :], start=False,
                                             stop=True).then_inc(o_full, 1)
                        pe.wait_ge(o_out, b * LT + LT)

                @block.scalar
                def _(act):
                    with act.Fori(0, B) as b:
                        act.wait_ge(h_full, b + 1)
                        for a in range(NPR):
                            last = nc.scalar.activation(hid[:, a, :], h_b[:, a // 2, (a % 2) * S:(a % 2) * S + S],
                                                        ACT.Gelu, bias=b1[:, a:a + 1])
                        last.then_inc(h_ok, 1)

                @block.vector
                def _(dve):
                    with dve.Fori(0, B) as b:
                        dve.wait_ge(h_ok, b + 1)
                        dve.wait_ge(cb_full, b + 1)
                        nc.vector.tensor_tensor(hidw[:, :, :].rearrange("p a s -> p (a s)"),
                                                cb_b.rearrange("p a s -> p (a s)"),
                                                hid[:, :, :].rearrange("p a s -> p (a s)"), ALU.mult).then_inc(hw_ok, 1)
                        for t in range(LT):
                            dve.wait_ge(o_full, b * LT + t + 1)
                            xt = X[:, bass.ds(b * LT + t, 1), :].rearrange("p a c -> p (a c)")
                            nc.vector.tensor_tensor(xt, o_b[:, t, 0:D], xt, ALU.add).then_inc(o_out, 1)

        layer_norm("ln4", store=out_v)


_INS = ['L0_attn_x', 'L0_attn_Wq', 'L0_attn_Wk', 'L0_attn_Wv', 'L0_attn_Eq', 'L0_attn_Ek', 'L0_attn_Ev',
        'L0_ffn_Wqkv', 'L0_ffn_q_scale', 'L0_ffn_k_scale', 'L0_ffn_Wo', 'L0_ffn_ln_g', 'L0_ffn_ln_b', 'L0_ffn_W1',
        'L0_ffn_b1', 'L0_ffn_W2', 'L0_ffn_b2', 'L1_attn_Wqkv', 'L1_attn_bqkv', 'L1_attn_Wout', 'L1_attn_bout',
        'L1_ffn_gate_w', 'L1_ffn_w1', 'L1_ffn_b1', 'L1_ffn_w2', 'L1_ffn_b2']
_STOP = 99


def kernel(**inputs):
    import numpy as _np
    import concourse.bacc as _bacc
    from concourse import mybir as _mybir
    from concourse.bass_utils import run_bass_kernel_spmd as _run

    nc = _bacc.Bacc("TRN2", target_bir_lowering=False, num_devices=1)
    arrays, args = {}, {}
    for name in _INS:
        a = _np.ascontiguousarray(inputs[name])
        arrays[f"in_{name}_dram"] = a
        args[name] = nc.dram_tensor(f"in_{name}_dram", a.shape, _mybir.dt.from_np(a.dtype), kind="ExternalInput").ap()
    for name, a in shape_constants().items():
        arrays[f"const_{name}_dram"] = a
        args[name] = nc.dram_tensor(f"const_{name}_dram", a.shape, _mybir.dt.from_np(a.dtype),
                                    kind="ExternalInput").ap()
    out = nc.dram_tensor("out_0_dram", (B, S, D), _mybir.dt.float32, kind="ExternalOutput").ap()
    build_program(nc, args, out, _STOP)
    r = _run(nc, [arrays], core_ids=[0])
    return r.results[0]["out_0_dram"]
```

```python
from contextlib import ExitStack

import numpy as np

import concourse.bass as bass
from concourse import mybir

F32 = mybir.dt.float32
BF16 = mybir.dt.bfloat16
F32R = mybir.dt.float32r
ALU = mybir.AluOpType
ACT = mybir.ActivationFunctionType
AX = mybir.AxisListType

P = 128
B, S, D = 16, 256, 128
LT = S // P
NT = B * LT
H, HD = 16, 8
SCALE_A = 1.0 / HD ** 0.5
MAXD = 64
NREL = 2 * MAXD + 1
NREX = 2 * S - 1
LB = P // HD
NLB = P // LB
NG, GC = 4, P // 4
TABW = NREX - LB + 1
DEPTH, BH, BD, WIN = 6, 16, 64, 32
INNER = BH * BD
FF = int(D * 4 * 2 / 3)
FCH = [128, 128, FF - 256]
NEXP, EH = 8, 64
NPR = NEXP // 2
EPS = 1e-5
NEG = -1e30


def shape_constants():
    f = np.float32
    p = np.arange(P)
    c = {}
    c["group_mask"] = (p[:, None] // HD == np.arange(LB)[None, :]).astype(f)
    c["ident"] = np.eye(P, dtype=f)
    c["flip"] = np.ascontiguousarray(np.eye(P, dtype=f)[::-1])
    heads = p[:, None] // LB == np.arange(8)[None, :]
    toks = p[:, None] % LB == np.arange(LB)[None, :]
    c["own"] = np.repeat(np.concatenate([heads, toks, heads], 1)[:, :, None], HD, 2).reshape(P, 32 * HD).astype(f)
    c["head_rows"] = (p[:, None] % GC // HD == np.arange(4)[None, :]).astype(f)
    part, channel = p[:, None, None] // GC, p[:, None, None] % GC
    spread = channel == np.arange(4)[None, :, None] * HD + p[None, None, :] % HD
    c["sum_q"] = (spread & (part % 2 == 0)).reshape(P, 4 * P).astype(f)
    c["sum_k"] = (spread & (part < 2)).reshape(P, 4 * P).astype(f)
    c["causal"] = np.where(p[None, :] > p[:, None], f(-125), f(0)).astype(f)
    i, j = p[:, None], p[None, :]
    c["window_own"] = np.where((j > i) | (i > j + WIN), f(NEG), f(0)).astype(f)
    c["window_prev"] = np.where(i > np.arange(WIN)[None, :], f(NEG), f(0)).astype(f)
    half = np.arange(0, BD, 2, dtype=f)
    inv_freq = (f(1) / np.power(f(10000), half / f(BD))).astype(f)
    t = np.arange(S, dtype=f)
    freqs = (t[:, None] * inv_freq[None, :]).astype(f)
    freqs = np.concatenate([freqs, freqs], -1)
    base = ((half + f(0.4 * BD)) / f(1.4 * BD)).astype(f)
    power = ((t - S // 2) / f(WIN // 2)).astype(f)
    scale = np.power(base[None, :], power[:, None]).astype(f)
    scale = np.concatenate([scale, scale], -1)
    sign = np.where(np.arange(BD) < BD // 2, f(-1), f(1))
    inv = (f(1) / scale).astype(f)
    cos, sin = np.cos(freqs), np.sin(freqs) * sign
    lay = lambda q, k: np.stack([q, k], 1).reshape(LT, P, 2, BD).transpose(1, 0, 2, 3).reshape(P, LT * 2 * BD).astype(f)
    c["rot_cos"] = lay(cos * scale * f(8), cos * inv)
    c["rot_sin"] = lay(sin * scale * f(8), sin * inv)
    s1 = np.zeros((P, P), f)
    s1[p[:-1], p[:-1] + 1] = 1
    s2 = np.zeros((P, P), f)
    s2[P - 1, 0] = 1
    c["shift_in"], c["shift_over"] = s1, s2
    e = np.zeros((NEXP, NPR, 2, EH), f)
    for x in range(NEXP):
        e[x, x // 2, x % 2] = 1
    c["expert_rows"] = e.reshape(NEXP, NPR * 2 * EH)
    c["lower"] = np.tile(np.tril(np.ones((NEXP, NEXP), f), -1).reshape(1, -1), (P, 1))
    return c


def ring_plan(orders, banks):
    at, count = {}, {}
    bank_of = {name: k % banks for k, name in enumerate(orders["loop"])}
    for part, order in orders.items():
        at[part], count[part] = {}, [0] * banks
        for name in order:
            if name is not None:
                r = bank_of[name]
                at[part][name] = (r, count[part][r])
                count[part][r] += 1
    first, loop = count["first"], count["loop"]
    assert all(count["last"][r] == loop[r] - first[r] for r in range(banks))

    def fill(part, i, name):
        r, number = at[part][name]
        return r, (0 if part == "first" else i * loop[r] + first[r]) + number + 1

    return fill, lambda n: [n * c for c in loop]


def build_program(nc, T, out):
    ctx = ExitStack()
    with ctx:
        def sb(stack, name, shape, dt=F32):
            return stack.enter_context(nc.sbuf_tensor(name, shape, dt))

        def sem(name):
            return ctx.enter_context(nc.semaphore(name))

        def dram(name, shape):
            return nc.dram_tensor(name, shape, F32, kind="Internal")

        X = sb(ctx, "X", [P, NT, D])
        XR = sb(ctx, "XR", [P, NT, D])
        ident = sb(ctx, "ident", [P, P])
        ident_bf = sb(ctx, "ident_bf", [P, P], BF16)
        gmask = sb(ctx, "gmask", [P, LB])
        ones = sb(ctx, "ones", [P, P])
        neghalf = sb(ctx, "neghalf", [P, LB])
        pause = sb(ctx, "pause", [P, 1])
        xcur = sb(ctx, "xcur", [P, LT, D])
        xT = sb(ctx, "xT", [P, S])
        psum = ctx.enter_context(nc.psum_tensor("psum", [P, 8, 512], F32))
        bank = [psum[:, i, :] for i in range(8)]

        oa = dram("oa", (B, LT, NLB, LB, 2, 8, HD))
        ev_ext = dram("ev_ext", (NREX, HD))
        pp_ext = dram("pp_ext", (1, 512))

        x_in = T["L0_attn_x"].rearrange("b (t p) c -> p (b t) c", p=P)
        out_v = out.rearrange("b (t p) c -> p (b t) c", p=P)

        with ExitStack() as st:
            wq, wk, wv = (sb(st, n, [P, D]) for n in ("a_wq", "a_wk", "a_wv"))
            wq_rep, wk_rep = (sb(st, n, [P, NG, 4, GC]) for n in ("a_wq_rep", "a_wk_rep"))
            sum_in = sb(st, "a_sum_in", [P, 2, 4 * P])
            sum_q, sum_k = (sb(st, n, [P, 4, P], F32R) for n in ("a_sum_q", "a_sum_k"))
            head_rows = sb(st, "a_head_rows", [P, 4])
            ext = sb(st, "a_ext", [HD, 4, NREX])
            pprow = sb(st, "a_pprow", [1, 512])
            eq_tab, ek_tab = (sb(st, n, [P, TABW]) for n in ("a_eq_tab", "a_ek_tab"))
            VW, YW = 8 * HD, 1 + 24 * HD
            values = sb(st, "a_values", [P, LT, LT * NLB, 2 + 2 * VW + P])
            pp_tab = sb(st, "a_pp_tab", [P, LT, S])
            own = sb(st, "a_own", [P, 32 * HD])
            q_next, q_parts, k_parts = (sb(st, n, [P, NG, S], F32R) for n in ("a_q_next", "a_q_parts", "a_k_parts"))
            v_next = sb(st, "a_v_next", [P, LT, D])
            k_diag = sb(st, "a_k_diag", [P, H, S], F32R)
            q_blk, k_blk = (sb(st, n, [P, H, S]) for n in ("a_q_blk", "a_k_blk"))
            relk = sb(st, "a_relk", [P, LT, H, P])
            probs = sb(st, "a_probs", [P, 2, 4, S])
            probsT = sb(st, "a_probsT", [P, LT, NLB, 8, LB])
            nmax, nbias = (sb(st, n, [P, 2, 4]) for n in ("a_nmax", "a_nbias"))
            rsum = sb(st, "a_rsum", [P, 2, 8])
            ymask = sb(st, "a_ymask", [P, 8, 24 * HD])
            ysum = sb(st, "a_ysum", [P, 8, HD])
            yout = XR[:, :, :].rearrange("p t (a c) -> p (t a) c", a=2)

            ld_x, ld_c, ld_w, ld_e = sem("a_ld_x"), sem("a_ld_c"), sem("a_ld_w"), sem("a_ld_e")
            ev_wr, pp_wr, tabs, flips = sem("a_ev_wr"), sem("a_pp_wr"), sem("a_tabs"), sem("a_flips")
            ev_turned, pp_turned = sem("a_ev_turned"), sem("a_pp_turned")
            ev_flip = q_blk[:, 0:12, :].rearrange("p h l -> p (h l)")
            pp_flip = k_blk[:, 0:2, :]
            flip = sb(st, "a_flip", [P, P])
            ext_ok, prod_ok, pp_full, pp_ok, set_ok = (sem("a_ext_ok"), sem("a_prod_ok"), sem("a_pp_full"),
                                                       sem("a_pp_ok"), sem("a_set_ok"))

            with nc.Block() as block:
                @block.sync
                def _(sp):
                    for name, t in (("L0_attn_Eq", 0), ("L0_attn_Ek", 2)):
                        sp.dma_start(ext[:, t, S - 1 - MAXD:S + MAXD], T[name].rearrange("r d -> d r"),
                                     allow_slow_non_contiguous=True).then_inc(ld_e, 16)
                    sp.dma_start(ext[:, 1, S - 1 - MAXD:S + MAXD],
                                 bass.AP(T["L0_attn_Ek"].tensor, (NREL - 1) * HD, [[1, HD], [-HD, NREL]]),
                                 allow_slow_non_contiguous=True).then_inc(ld_e, 16)
                    ev = T["L0_attn_Ev"]
                    sp.dma_start(ev_ext[S - 1 - MAXD:S + MAXD, :], ev[:, :]).then_inc(ev_wr, 16)
                    sp.dma_start(ev_ext[0:S - 1 - MAXD, :],
                                 ev[0:1, :].broadcast_to((S - 1 - MAXD, HD))).then_inc(ev_wr, 16)
                    sp.dma_start(ev_ext[S + MAXD:NREX, :],
                                 ev[NREL - 1:NREL, :].broadcast_to((S - 1 - MAXD, HD))).then_inc(ev_wr, 16)
                    sp.wait_ge(ev_wr, 48)
                    sp.dma_start(ev_flip, bass.AP(ev_ext, 0, [[HD, P], [1, (LT * P + P) * HD]])).then_inc(flips, 16)
                    sp.wait_ge(ext_ok, 1)
                    for m in range(LB):
                        for tab, t in ((eq_tab, 0), (ek_tab, 1)):
                            sp.dma_start(tab[HD * m:HD * m + HD, :],
                                         ext[:, t, LB - 1 - m:LB - 1 - m + TABW]).then_inc(tabs, 16)
                    sp.wait_ge(pp_ok, 1)
                    sp.dma_start(pp_ext[:, 0:NREX], pprow[:, 0:NREX]).then_inc(pp_wr, 16)
                    sp.wait_ge(pp_wr, 16)
                    for mt in range(LT):
                        sp.dma_start(pp_flip[:, mt, :],
                                     bass.AP(pp_ext, P - mt * P, [[1, P], [1, S]])).then_inc(flips, 16)
                    sp.wait_ge(tabs, 16 * 2 * LB)
                    sp.wait_ge(ld_x, 16)

                @block.scalar
                def _(act):
                    for name, t in (("L0_attn_Wq", wq), ("L0_attn_Wk", wk), ("L0_attn_Wv", wv)):
                        act.dma_start(t[:, :], T[name]).then_inc(ld_w, 16)
                    for name, t in (("ident", ident), ("group_mask", gmask), ("own", own), ("flip", flip),
                                    ("head_rows", head_rows), ("sum_q", sum_in[:, 0, :]), ("sum_k", sum_in[:, 1, :])):
                        act.dma_start(t[:, :], T[name]).then_inc(ld_c, 16)
                    act.dma_start(X[:, :, :], x_in).then_inc(ld_x, 16)

                @block.gpsimd
                def _(pool):
                    nc.gpsimd.memset(ones[:, :], 1.0).then_inc(set_ok, 1)
                    nc.gpsimd.memset(neghalf[:, :], -0.5)
                    nc.gpsimd.memset(values[:, :, :, 0:1], 1.0)
                    nc.gpsimd.memset(values[:, :, :, YW + VW:YW + VW + 1], 1.0)
                    pool.wait_ge(ld_w, 48)
                    for w, rep in ((wq, wq_rep), (wk, wk_rep)):
                        nc.gpsimd.tensor_copy(rep[:, :, :, :],
                                              w[:, :].rearrange("p (g c) -> p g c", g=NG)[:, :, None, :]
                                              .broadcast_to((P, NG, 4, GC)))

                @block.vector
                def _(dve):
                    dve.wait_ge(ld_e, 48)
                    for t in range(3):
                        a, b = S - 1 - MAXD, S + MAXD
                        nc.vector.tensor_copy(ext[:, t, 0:a], ext[:, t, a:a + 1].broadcast_to((HD, a)))
                        last = nc.vector.tensor_copy(ext[:, t, b:NREX],
                                                     ext[:, t, b - 1:b].broadcast_to((HD, NREX - b)))
                    last.then_inc(ext_ok, 1)
                    dve.wait_ge(ext_ok, 1)
                    nc.vector.tensor_tensor(ext[:, 3, :], ext[:, 0, :], ext[:, 2, :], ALU.mult).then_inc(prod_ok, 1)
                    dve.wait_ge(pp_full, 1)
                    nc.vector.tensor_copy(pprow[0:1, 0:NREX], bank[0][0:1, 0:NREX]).then_inc(pp_ok, 1)
                    dve.wait_ge(ld_c, 16 * 7)
                    nc.vector.tensor_copy(ident_bf[:, :], ident[:, :])
                    for part, t in ((sum_q, 0), (sum_k, 1)):
                        nc.vector.tensor_copy(part[:, :, :].rearrange("p a c -> p (a c)"), sum_in[:, t, :])
                    dve.wait_ge(ev_turned, 1)
                    windows = psum[:, 1:7, :].rearrange("p a c -> p (a c)").rearrange("p (u c) -> p u c", c=P)
                    for mt in range(LT):
                        u = (1 - mt) * NLB
                        nc.vector.tensor_copy(values[:, mt, :, 1 + VW:1 + VW + P], windows[:, u:u + LT * NLB, :])
                    dve.wait_ge(pp_turned, 1)
                    nc.vector.tensor_copy(pp_tab[:, :, :].rearrange("p t l -> p (t l)"), bank[7])

                @block.tensor
                def _(pe):
                    pe.wait_ge(set_ok, 1)
                    pe.wait_ge(prod_ok, 1)
                    nc.tensor.matmul(bank[0][0:1, 0:NREX], ones[0:HD, 0:1], ext[:, 3, :],
                                     start=True, stop=True).then_inc(pp_full, 1)
                    pe.wait_ge(ld_c, 16 * 7)
                    pe.wait_ge(flips, 16 * (1 + LT))
                    for i in range(6):
                        last = nc.tensor.matmul(bank[1 + i], flip[:, :], ev_flip[:, i * 512:(i + 1) * 512],
                                                start=True, stop=True)
                    last.then_inc(ev_turned, 1)
                    nc.tensor.matmul(bank[7], flip[:, :], pp_flip.rearrange("p t l -> p (t l)"),
                                     start=True, stop=True).then_inc(pp_turned, 1)

            rk = lambda lt: [("rk", lt, n) for n in range(8)]
            y = lambda g: [("y", g, n) for n in range(4)]
            qb = [("qb", n) for n in range(8)]
            kb = [("kb", n) for n in range(8)]
            qs, ks = [("qs", 0), ("qs", 1)], [("ks", 0), ("ks", 1)]
            orders = {"first": ["x"] + qs + ks + ["v"] + qb + kb,
                      "loop": (rk(0) + ["x"] + qs + ks + y(0) + ["v"] + rk(1) + qb[:6] + y(1) + qb[6:] + kb[:4] + y(2)
                               + kb[4:] + y(3)),
                      "last": rk(0) + y(0) + rk(1) + y(1) + y(2) + y(3)}
            ring_fill, ring_fills = ring_plan(orders, 2)
            ring = bank[0:2]
            score = [psum[:, 2:4, :], psum[:, 4:6, :]]
            turned = bank[6:8]
            x_copied, ring_full, ring_free = sem("a_x_copied"), [sem("a_ring_full0"), sem("a_ring_full1")], \
                [sem("a_ring_free0"), sem("a_ring_free1")]
            score_full, row_max, bias_ok, exp_done = (sem("a_score_full"), sem("a_row_max"), sem("a_bias_ok"),
                                                      sem("a_exp_done"))
            turn_full, turn_out, diag_ok, high_ok, queries_ok, values_ok = (
                sem("a_turn_full"), sem("a_turn_out"), sem("a_diag_ok"), sem("a_high_ok"), sem("a_queries_ok"),
                sem("a_values_ok"))
            ymask_ok, ysum_ok, yout_ok, oa_st = (sem("a_ymask_ok"), sem("a_ysum_ok"), sem("a_yout_ok"),
                                                 sem("a_oa_st"))

            with nc.Block() as block:
                @block.gpsimd
                def _(pool):
                    def sequence(part, b):
                        i = 0 if part == "first" else b + 1
                        nc.gpsimd.tensor_copy(xcur[:, :, :], X[:, bass.ds(i * LT, LT), :]).then_inc(x_copied, 1)
                        for hq in range(NG):
                            r, number = ring_fill(part, b, ks[hq // 2])
                            pool.wait_ge(ring_free[r], number + 1)
                            if part == "loop":
                                pool.wait_ge(score_full, b * 8 + 5 + hq)
                            nc.gpsimd.tensor_tensor(k_diag[:, hq * 4:hq * 4 + 4, :],
                                                    k_parts[:, hq:hq + 1, :].bitcast(F32).broadcast_to((P, 4, S)),
                                                    head_rows[:, :, None].broadcast_to((P, 4, S)),
                                                    ALU.mult).then_inc(diag_ok, 1)

                    sequence("first", 0)
                    with pool.Fori(0, B - 1) as b:
                        sequence("loop", b)

                @block.tensor
                def _(pe):
                    def sequence(part, b):
                        def room(name):
                            r, number = ring_fill(part, b, name)
                            pe.wait_ge(ring_free[r], number)
                            return ring[r], ring_full[r]

                        def out_of(name):
                            r, number = ring_fill(part, b, name)
                            pe.wait_ge(ring_free[r], number + 1)

                        def turn_x():
                            pe.wait_ge(x_copied, 1 if part == "first" else b + 2)
                            r, full = room("x")
                            for t in range(LT):
                                last = nc.tensor.transpose(r[:, t * P:(t + 1) * P], xcur[:, t, :], ident[:, :])
                            last.then_inc(full, 1)

                        def project_groups(names, rep):
                            for name in names:
                                r, full = room(name)
                                for j in range(2):
                                    last = nc.tensor.matmul(r[:, j * S:(j + 1) * S],
                                                            rep[:, 2 * name[1] + j, :, :].rearrange("p a c -> p (a c)"),
                                                            xT[:, :], start=(j == 0), stop=(j == 1), skip_group_check=True)
                                last.then_inc(full, 1)

                        def project_v():
                            r, full = room("v")
                            for t in range(LT):
                                last = nc.tensor.matmul(r[:, t * D:(t + 1) * D], xT[:, t * P:(t + 1) * P], wv[:, :],
                                                        start=(t == 0), stop=(t == 1), skip_group_check=True)
                            last.then_inc(full, 1)

                        def spread_block(name):
                            if name is None:
                                return
                            sums, parts, of = (sum_q, q_next, qs) if name[0] == "qb" else (sum_k, k_parts, ks)
                            out_of(of[name[1] // 4])
                            r, full = room(name)
                            for j in range(2):
                                h = 2 * name[1] + j
                                last = nc.tensor.matmul(r[:, j * S:(j + 1) * S], sums[:, h % 4, :], parts[:, h // 4, :],
                                                        start=(j == 0), stop=(j == 1), skip_group_check=True)
                            last.then_inc(full, 1)

                        def relative_keys(lt):
                            for name in rk(lt):
                                mt, n = name[2] // 4, name[2] % 4
                                r, full = room(name)
                                for j in range(2):
                                    blk = lt * NLB + n * 2 + j
                                    v = mt * P - blk * LB + S - LB
                                    last = nc.tensor.matmul(r[:, j * S:(j + 1) * S], ek_tab[:, v:v + P],
                                                            q_blk[:, :, blk * LB:(blk + 1) * LB], start=(j == 0),
                                                            stop=(j == 1), skip_group_check=True)
                                last.then_inc(full, 1)

                        def scores(s, blocks=()):
                            lt, hq = s // 4, s % 4
                            if s >= 2:
                                pe.wait_ge(exp_done, b * 8 + s - 1)
                            if s == 0:
                                pe.wait_ge(queries_ok, b + 1)
                            if lt == 0:
                                pe.wait_ge(diag_ok, b * 4 + (hq + 1 if hq < 2 else 4))
                            blocks = iter(blocks)
                            hs = slice(hq * 4, hq * 4 + 4)
                            o = [score[s % 2][:, mt, :].rearrange("p (h m) -> p h m", h=4) for mt in range(LT)]

                            def contents(mt):
                                nc.tensor.matmul(o[mt], q_parts[:, hq, lt * P:(lt + 1) * P],
                                                 k_diag[:, hs, mt * P:(mt + 1) * P],
                                                 start=True, stop=False, skip_group_check=True)
                                for n in range(NLB):
                                    blk = mt * NLB + n
                                    v = lt * P - blk * LB + S - LB
                                    nc.tensor.matmul(o[mt][:, :, n * LB:(n + 1) * LB], eq_tab[:, v:v + P],
                                                     k_blk[:, hs, blk * LB:(blk + 1) * LB], start=False, stop=False,
                                                     skip_group_check=True)
                                    if n == NLB // 2 - 1 and hq > 0:
                                        spread_block(next(blocks, None))

                            def add_relative_keys(mt):
                                for h in range(4):
                                    last = nc.tensor.matmul(o[mt][:, h, :], relk[:, mt, hq * 4 + h, :], ident[:, :],
                                                            start=False, stop=(h == 3), skip_group_check=True)
                                if mt == LT - 1:
                                    last.then_inc(score_full, 1)
                                spread_block(next(blocks, None))

                            if hq == 0:
                                for mt in range(LT):
                                    contents(mt)
                                relative_keys(lt)
                                for mt in range(LT):
                                    for name in rk(lt)[4 * mt + 2:4 * mt + 4]:
                                        out_of(name)
                                    add_relative_keys(mt)
                            else:
                                for mt in range(LT):
                                    contents(mt)
                                    add_relative_keys(mt)

                        def turn(s):
                            pe.wait_ge(exp_done, b * 8 + s + 1)
                            if s >= 1:
                                pe.wait_ge(turn_out, b * 8 + s)
                            for mt in range(LT):
                                for h in range(4):
                                    last = nc.tensor.transpose(turned[mt][:, h * P:(h + 1) * P],
                                                               probs[:, s % 2, h, mt * P:(mt + 1) * P], ident[:, :])
                            last.then_inc(turn_full, 1)

                        def outputs(g):
                            pe.wait_ge(turn_out, b * 8 + 2 * g + 2)
                            lt, hh = g // 2, g % 2
                            if g == 0:
                                pe.wait_ge(values_ok, b + 1)
                            for n, name in enumerate(y(g)):
                                r, full = room(name)
                                for j in range(2):
                                    blk = lt * NLB + 2 * n + j
                                    for mt in range(LT):
                                        w = probsT[:, mt, 2 * n + j, :, :].rearrange("p h l -> p (h l)")
                                        c = hh * (1 + VW)
                                        last = nc.tensor.matmul(r[:, j * YW:(j + 1) * YW], w, values[:, mt, blk, c:c + YW],
                                                                start=(j == 0 and mt == 0), stop=(j == 1 and mt == 1),
                                                                skip_group_check=True)
                                last.then_inc(full, 1)

                        if part == "first":
                            turn_x()
                            out_of("x")
                            project_groups(qs, wq_rep)
                            project_groups(ks, wk_rep)
                            project_v()
                            for name in qb + kb:
                                spread_block(name)
                            return
                        ahead = part == "loop"
                        scores(0)
                        if ahead:
                            turn_x()
                        scores(1)
                        turn(0)
                        if ahead:
                            out_of("x")
                            project_groups(qs, wq_rep)
                        scores(2)
                        turn(1)
                        if ahead:
                            project_groups(ks, wk_rep)
                        scores(3)
                        outputs(0)
                        if ahead:
                            project_v()
                        turn(2)
                        scores(4, qb[:2] if ahead else ())
                        turn(3)
                        scores(5, qb[2:6] if ahead else ())
                        outputs(1)
                        turn(4)
                        scores(6, qb[6:] + kb[:2] if ahead else ())
                        turn(5)
                        scores(7, kb[2:4] if ahead else ())
                        outputs(2)
                        turn(6)
                        if ahead:
                            spread_block(kb[4])
                            spread_block(kb[5])
                        turn(7)
                        if ahead:
                            spread_block(kb[6])
                            spread_block(kb[7])
                        outputs(3)

                    sequence("first", 0)
                    with pe.Fori(0, B - 1) as b:
                        sequence("loop", b)
                    sequence("last", B - 1)

                @block.scalar
                def _(act):
                    def sequence(part, b):
                        def take(name):
                            r, number = ring_fill(part, b, name)
                            act.wait_ge(ring_full[r], number)
                            return ring[r], ring_free[r]

                        def turned_x():
                            r, free = take("x")
                            nc.scalar.copy(xT[:, :], r[:, 0:S]).then_inc(free, 1)

                        def high_parts(names, parts):
                            for name in names:
                                r, _ = take(name)
                                nc.scalar.copy(parts[:, 2 * name[1]:2 * name[1] + 2, :],
                                               r.rearrange("p (g s) -> p g s", g=2)).then_inc(high_ok, 1)

                        def next_queries():
                            for name in qs:
                                r, number = ring_fill(part, b, name)
                                act.wait_ge(ring_free[r], number + 1)
                            nc.scalar.copy(q_parts[:, :, :], q_next[:, :, :].bitcast(F32)).then_inc(queries_ok, 1)

                        def projected_v():
                            r, free = take("v")
                            nc.scalar.copy(v_next[:, :, :].rearrange("p t c -> p (t c)"), r[:, 0:LT * D]).then_inc(free, 1)

                        def next_values():
                            r, number = ring_fill(part, b, "v")
                            act.wait_ge(ring_free[r], number + 1)
                            if part == "loop":
                                take(y(3)[-1])
                            for t in range(LT):
                                for hh in range(2):
                                    c = 1 + hh * (VW + P)
                                    last = nc.scalar.copy(values[:, t, :, c:c + VW],
                                                          v_next[:, t:t + 1, hh * VW:(hh + 1) * VW]
                                                          .broadcast_to((P, LT * NLB, VW)))
                            last.then_inc(values_ok, 1)

                        def exps(s):
                            act.wait_ge(bias_ok, b * 8 + s + 1)
                            for h in range(4):
                                last = nc.scalar.activation(
                                    probs[:, s % 2, h, :].rearrange("p (t m) -> p t m", t=LT),
                                    score[s % 2][:, :, h * P:(h + 1) * P], ACT.Exp,
                                    bias=nbias[:, s % 2, h:h + 1], scale=SCALE_A)
                            last.then_inc(exp_done, 1)

                        def turns(s):
                            act.wait_ge(turn_full, b * 8 + s + 1)
                            for mt in range(LT):
                                last = nc.scalar.copy(probsT[:, mt, :, (s % 2) * 4:(s % 2) * 4 + 4, :],
                                                      turned[mt].rearrange("p (h k l) -> p k h l", h=4, l=LB))
                            last.then_inc(turn_out, 1)

                        if part == "first":
                            turned_x()
                            high_parts(qs, q_next)
                            high_parts(ks, k_parts)
                            projected_v()
                            next_queries()
                            next_values()
                            return
                        ahead = part == "loop"
                        exps(0)
                        if ahead:
                            turned_x()
                        for s in range(1, 8):
                            exps(s)
                            if s == 3 and ahead:
                                projected_v()
                            if s < 7:
                                turns(s - 1)
                            if s == 1 and ahead:
                                high_parts(qs, q_next)
                            if s == 2 and ahead:
                                high_parts(ks, k_parts)
                        turns(6)
                        turns(7)
                        if ahead:
                            next_queries()
                            next_values()

                    sequence("first", 0)
                    with act.Fori(0, B - 1) as b:
                        sequence("loop", b)
                    sequence("last", B - 1)

                @block.vector
                def _(dve):
                    for f in ring_free:
                        dve.sem_inc(f, 1)

                    def sequence(part, b):
                        def take(name):
                            r, number = ring_fill(part, b, name)
                            dve.wait_ge(ring_full[r], number)
                            return ring[r], ring_free[r]

                        def maxima(s):
                            dve.wait_ge(score_full, b * 8 + s + 1)
                            nc.vector.tensor_reduce(nmax[:, s % 2, :],
                                                    score[s % 2].rearrange("p t (h m) -> p h t m", h=4),
                                                    AX.XY, ALU.max).then_inc(row_max, 1)
                            dve.wait_ge(row_max, b * 8 + s + 1)
                            nc.vector.tensor_scalar(nbias[:, s % 2, :], nmax[:, s % 2, :], -SCALE_A, None,
                                                    ALU.mult).then_inc(bias_ok, 1)

                        def low_parts(names, parts, rows):
                            for name in names:
                                r, free = take(name)
                                dve.wait_ge(high_ok, (0 if part == "first" else b * 4 + 4)
                                            + (qs + ks).index(name) + 1)
                                gs = slice(2 * name[1], 2 * name[1] + 2)
                                for at in rows:
                                    last = nc.vector.tensor_tensor(parts[at, gs, :],
                                                                   r[at].rearrange("p (g s) -> p g s", g=2),
                                                                   parts[at, gs, :].bitcast(F32), ALU.subtract)
                                last.then_inc(free, 1)

                        def blocks(names, blk):
                            for name in names:
                                r, free = take(name)
                                nc.vector.tensor_tensor(
                                    blk[:, 2 * name[1]:2 * name[1] + 2, :].rearrange("p h (n l) -> p (h n) l", l=LB),
                                    r.rearrange("p (n l) -> p n l", l=LB),
                                    gmask[:, None, :].broadcast_to((P, 2 * S // LB, LB)), ALU.mult).then_inc(free, 1)

                        def relative_keys(lt):
                            for name in rk(lt):
                                mt, lp = name[2] // 4, name[2] % 4
                                r, free = take(name)
                                pp = pp_tab[:, mt, lt * P + lp * 32:lt * P + lp * 32 + 32]
                                nc.vector.tensor_tensor(
                                    relk[:, mt, :, lp * 32:lp * 32 + 32].rearrange("p h (j l) -> p j h l", j=2),
                                    r.rearrange("p (j h l) -> p j h l", j=2, h=H),
                                    pp.rearrange("p (j l) -> p j l", j=2)[:, :, None, :].broadcast_to((P, 2, H, LB)),
                                    ALU.add).then_inc(free, 1)

                        def outputs(g):
                            for n, name in enumerate(y(g)):
                                r, free = take(name)
                                r = r[:, 0:2 * YW].rearrange("p (j c) -> p j c", j=2)
                                hh = g % 2
                                nc.vector.tensor_tensor(ymask[:, 2 * n:2 * n + 2, :], r[:, :, 1 - hh:YW - hh],
                                                        own[:, None, hh * VW:hh * VW + 24 * HD]
                                                        .broadcast_to((P, 2, 24 * HD)), ALU.mult).then_inc(ymask_ok, 1)
                                nc.vector.reciprocal(rsum[:, g % 2, 2 * n:2 * n + 2],
                                                     r[:, :, hh * (YW - 1)]).then_inc(free, 1)
                            dve.wait_ge(ymask_ok, b * 16 + 4 * g + 4)
                            nc.vector.tensor_reduce(ysum[:, :, :], ymask[:, :, :].rearrange("p n (g d) -> p n d g", d=HD),
                                                    AX.X, ALU.add).then_inc(ysum_ok, 1)
                            dve.wait_ge(ysum_ok, b * 4 + g + 1)
                            rows = yout[:, bass.ds(b * 4 + g, 1), :].rearrange("p a (n d) -> p (a n) d", d=HD)
                            nc.vector.tensor_tensor(rows, ysum[:, :, :], rsum[:, g % 2, :, None].broadcast_to((P, 8, HD)),
                                                    ALU.mult).then_inc(yout_ok, 1)

                        q_low, k_low = [slice(2 * GC, P)], [slice(GC, 2 * GC), slice(3 * GC, P)]
                        if part == "first":
                            low_parts(qs, q_next, q_low)
                            low_parts(ks, k_parts, k_low)
                            blocks(qb, q_blk)
                            blocks(kb, k_blk)
                            return
                        ahead = part == "loop"
                        relative_keys(0)
                        maxima(0)
                        maxima(1)
                        if ahead:
                            low_parts(qs, q_next, q_low)
                        maxima(2)
                        if ahead:
                            low_parts(ks, k_parts, k_low)
                        maxima(3)
                        outputs(0)
                        relative_keys(1)
                        if ahead:
                            blocks(qb[:1], q_blk)
                        maxima(4)
                        if ahead:
                            blocks(qb[1:5], q_blk)
                        maxima(5)
                        if ahead:
                            blocks(qb[5:6], q_blk)
                        outputs(1)
                        if ahead:
                            blocks(qb[6:], q_blk)
                            blocks(kb[:1], k_blk)
                        maxima(6)
                        if ahead:
                            blocks(kb[1:4], k_blk)
                        maxima(7)
                        outputs(2)
                        if ahead:
                            blocks(kb[4:], k_blk)
                        outputs(3)

                    sequence("first", 0)
                    with dve.Fori(0, B - 1) as b:
                        sequence("loop", b)
                    sequence("last", B - 1)

                @block.sync
                def _(sp):
                    with sp.Fori(0, B) as b:
                        for g in range(4):
                            lt, hh = g // 2, g % 2
                            sp.wait_ge(yout_ok, b * 4 + g + 1)
                            for h in range(8):
                                sp.dma_start(
                                    oa[b, lt, :, :, hh, h, :].rearrange("k l d -> l k d"),
                                    yout[LB * h:LB * h + LB, b * 4 + g, :].rearrange("p (k d) -> p k d", d=HD)
                                ).then_inc(oa_st, 16)
                    sp.wait_ge(oa_st, 16 * B * 4 * 8)

        def layer_norm(tag, residual=None, load=None, keep=None, store=None):
            GT = 8
            with ExitStack() as st:
                stats = sb(st, f"{tag}_stats", [P, 2, GT, 6])
                mv = sb(st, f"{tag}_mv", [P, 2, GT, 2])
                var = sb(st, f"{tag}_var", [P, 2, GT])
                rstd = sb(st, f"{tag}_rstd", [P, 2, GT])
                stats_ok, mv_ok, var_ok, rstd_ok, normed = (
                    sem(f"{tag}_{n}") for n in ("stats_ok", "mv_ok", "var_ok", "rstd_ok", "normed"))
                added = sem(f"{tag}_added") if residual is not None else None
                kept = sem(f"{tag}_kept") if keep is not None else None
                loaded = sem(f"{tag}_loaded") if load is not None else None
                stored = sem(f"{tag}_stored") if store is not None else None
                with nc.Block() as block:
                    @block.sync
                    def _(sp):
                        if load is not None:
                            sp.dma_start(residual[:, :, :], load).then_inc(loaded, 16)
                        if store is not None:
                            with sp.Fori(0, NT // GT) as g:
                                sp.wait_ge(normed, (g + 1) * GT)
                                sp.dma_start(store[:, bass.ds(g * GT, GT), :],
                                             X[:, bass.ds(g * GT, GT), :]).then_inc(stored, 16)
                            sp.wait_ge(stored, 16 * (NT // GT))

                    @block.vector
                    def _(dve):
                        if load is not None:
                            dve.wait_ge(loaded, 16)

                        def statistics(n, u):
                            tiles = bass.ds(n * GT, GT)
                            if residual is not None:
                                nc.vector.tensor_tensor(X[:, tiles, :], X[:, tiles, :], residual[:, tiles, :],
                                                        ALU.add).then_inc(added, 1)
                                dve.wait_ge(added, n + 1)
                                nc.vector.memset(pause[:, :], 0.0)
                            for j in range(GT):
                                nc.vector.bn_stats(stats[:, u, j, :], X[:, bass.ds(n * GT + j, 1), :]
                                                   .rearrange("p a c -> p (a c)")).then_inc(stats_ok, 1)
                            dve.wait_ge(stats_ok, (n + 1) * GT)
                            nc.vector.memset(pause[:, :], 0.0)
                            for j in range(GT):
                                nc.vector.bn_aggr(mv[:, u, j, :], stats[:, u, j, :]).then_inc(mv_ok, 1)
                            dve.wait_ge(mv_ok, (n + 1) * GT)
                            nc.vector.tensor_scalar(var[:, u, :], mv[:, u, :, 1], EPS, None, ALU.add).then_inc(var_ok, 1)

                        def normalise(n, u):
                            dve.wait_ge(rstd_ok, n + 1)
                            for j in range(GT):
                                t = X[:, bass.ds(n * GT + j, 1), :].rearrange("p a c -> p (a c)")
                                nc.vector.tensor_scalar(t, t, mv[:, u, j, 0:1], rstd[:, u, j:j + 1], ALU.subtract,
                                                        ALU.mult).then_inc(normed, 1)

                        with dve.Fori(0, NT // (2 * GT)) as g:
                            for u in range(2):
                                statistics(g * 2 + u, u)
                            for u in range(2):
                                normalise(g * 2 + u, u)

                    @block.gpsimd
                    def _(pool):
                        with pool.Fori(0, NT // (2 * GT)) as g:
                            for u in range(2):
                                pool.wait_ge(var_ok, g * 2 + u + 1)
                                nc.gpsimd.tensor_tensor(rstd[:, u, :], var[:, u, :], neghalf[:, 0:GT],
                                                        ALU.pow).then_inc(rstd_ok, 1)

                    if keep is not None:
                        @block.scalar
                        def _(act):
                            with act.Fori(0, NT // GT) as g:
                                tiles = bass.ds(g * GT, GT)
                                act.wait_ge(normed, (g + 1) * GT)
                                nc.scalar.copy(keep[:, tiles, :], X[:, tiles, :]).then_inc(kept, 1)

        oa_tiles = oa.rearrange("b t k l a h d -> (k l) (b t) (a h d)")
        layer_norm("ln1", residual=XR, load=oa_tiles, keep=XR)

        with ExitStack() as st:
            wqkv = sb(st, "b_wqkv", [P, 3 * INNER])
            w_hi, w_lo = sb(st, "b_w_hi", [P, 3 * INNER], F32R), sb(st, "b_w_lo", [P, 3 * INNER], F32R)
            xT_hi, xT_lo = sb(st, "b_xT_hi", [P, S], F32R), sb(st, "b_xT_lo", [P, S], F32R)
            wo = sb(st, "b_wo", [P, INNER // P, D])
            qk_gain = sb(st, "b_qk_gain", [P, 2, BD])
            cos0, sin0, cosg, sing = (sb(st, n, [P, LT, 2, BD]) for n in ("b_cos0", "b_sin0", "b_cosg", "b_sing"))
            w1 = sb(st, "b_w1", [P, 2 * FF])
            w2 = sb(st, "b_w2", [P, 3, D])
            b1 = sb(st, "b_b1", [P, 6])
            lng, lnb = sb(st, "b_lng", [P, 1]), sb(st, "b_lnb", [P, 1])
            shift_in, shift_over = sb(st, "b_shift_in", [P, P]), sb(st, "b_shift_over", [P, P])
            masks0 = sb(st, "b_masks0", [P, P + WIN])
            own_bf = sb(st, "b_own_bf", [P, P], BF16)
            prev_bf = sb(st, "b_prev_bf", [P, WIN], BF16)
            sq = sb(st, "b_sq", [P, 2 * 8 * BD])
            ss = sb(st, "b_ss", [P, 2, 16])
            rnorm = sb(st, "b_rnorm", [P, 2, 16])
            t1, t2 = sb(st, "b_t1", [P, 2, 16, BD]), sb(st, "b_t2", [P, 2, 16, BD])
            rot, qk = sb(st, "b_rot", [P, 2, 16, BD]), sb(st, "b_qk", [P, 2, 16, BD])
            v = sb(st, "b_v", [P, 2 * 4, 8, BD + 1])
            qTs = sb(st, "b_qTs", [P, 4, P])
            kz = sb(st, "b_kz", [P, LT, 4, 2, P])
            m_own, m_prev = sb(st, "b_m_own", [P, 8]), sb(st, "b_m_prev", [WIN, 8])
            pr = sb(st, "b_pr", [P, 2, 8, P])
            pp0 = sb(st, "b_pp0", [WIN, 8, WIN])
            pp = sb(st, "b_pp", [WIN, 8, P])
            prT = sb(st, "b_prT", [P, 8, P])
            ppT = sb(st, "b_ppT", [P, 8, WIN])
            rs = sb(st, "b_rs", [P, 8])
            o = sb(st, "b_o", [P, 8, BD])
            oT = sb(st, "b_oT", [P, 4, P])
            w_out = sb(st, "b_w_out", [P, D])
            st6 = sb(st, "b_st6", [P, 2, LT, 6])
            mv = sb(st, "b_mv", [P, 2, LT, 2])
            fvar, frstd = sb(st, "b_fvar", [P, 2, LT]), sb(st, "b_frstd", [P, 2, LT])
            xn = sb(st, "b_xn", [P, 2, LT, D])
            xnT = sb(st, "b_xnT", [P, 2, S])
            gel = sb(st, "b_gel", [P, 2, 3, S])
            hid = sb(st, "b_hid", [P, 2, 3, S])

            c_ld, wa_ld, wf_ld = sem("b_c_ld"), sem("b_wa_ld"), sem("b_wf_ld")
            gains = sem("b_gains")
            x_copied, x_full, hi_done, lo_done = sem("b_x_copied"), sem("b_x_full"), sem("b_hi_done"), sem("b_lo_done")
            w_split = sem("b_w_split")
            qk_full, sq_done, ss_done = sem("b_qk_full"), sem("b_sq_done"), sem("b_ss_done")
            floor_done, rn_done, t_done, rot_done, qk_done = (
                sem("b_floor_done"), sem("b_rn_done"), sem("b_t_done"), sem("b_rot_done"), sem("b_qk_done"))
            sc_full, mo_done, mp_done, mx_done, sub_done, exp_done = (
                sem("b_sc_full"), sem("b_mo_done"), sem("b_mp_done"), sem("b_mx_done"), sem("b_sub_done"),
                sem("b_exp_done"))
            rs_done, o_done, x_attn = sem("b_rs_done"), sem("b_o_done"), sem("b_x_attn")
            ring_full = [sem(f"b_ring_full{i}") for i in range(4)]
            ring_free = [sem(f"b_ring_free{i}") for i in range(4)]
            x_ffn, st_done, mv_done, var_done, rstd_done, xn_done = (
                sem("b_x_ffn"), sem("b_st_done"), sem("b_mv_done"), sem("b_var_done"), sem("b_rstd_done"),
                sem("b_xn_done"))
            hg_full, gel_done, hid_done = sem("b_hg_full"), sem("b_gel_done"), sem("b_hid_done")
            fr_full = [sem("b_fr_full0"), sem("b_fr_full1")]
            fr_free = [sem("b_fr_free0"), sem("b_fr_free1")]

            wqkv_d, wo_d = T["L0_ffn_Wqkv"], T["L0_ffn_Wo"]
            N_WA, N_WF = 4, 10
            NB = B // 2
            SEQ = 4
            NS = 2 * SEQ

            SLOTS = {"first": range(-4, 0), "loop": range(NS), "last": range(NS)}

            def valid(part, step):
                return {"first": step >= 0, "loop": True, "last": step < NS}[part]

            def x_follows(part, j):
                return part != "last" and j % SEQ == SEQ - 1

            def slot_fills(part, j):
                fills = [("q", j + 2), ("k", j + 2), ("v", j + 4), ("oT", j)]
                probs = [("p0", j + 1), ("p1", j + 1)]
                fills += probs + [("prev", j + 2)] if j % 2 else [("pp", j + 1)] + probs
                fills += [("w", j), ("o0", j + 1), ("o1", j + 1)]
                return [f if valid(part, f[1]) else None for f in fills]

            NR = 4
            ring_at = {part: {} for part in SLOTS}
            ring_count = {part: [0] * NR for part in SLOTS}
            for part in SLOTS:
                for j in SLOTS[part]:
                    fills = slot_fills(part, j)
                    for i, f in enumerate(fills):
                        if f is not None:
                            r = ((j % NS) * len(fills) + i) % NR
                            ring_at[part][f] = (r, ring_count[part][r])
                            ring_count[part][r] += 1
            RF, RL = ring_count["first"], ring_count["loop"]
            assert all(ring_count["last"][r] == RL[r] - RF[r] for r in range(NR))

            def ring_fill(part, l, b, name):
                i, number = ring_at[part][name]
                return i, l * (NB * RL[i]) + (0 if part == "first" else b * RL[i] + RF[i]) + (number + 1)

            with nc.Block() as block:
                @block.sync
                def _(sp):
                    for name, t in (("rot_cos", cos0), ("rot_sin", sin0)):
                        sp.dma_start(t[:, :, :, :].rearrange("p t a d -> p (t a d)"), T[name]).then_inc(c_ld, 16)
                    sp.dma_start(shift_in[:, :], T["shift_in"]).then_inc(c_ld, 16)
                    sp.dma_start(shift_over[:, :], T["shift_over"]).then_inc(c_ld, 16)
                    sp.dma_start(masks0[:, 0:P], T["window_own"]).then_inc(c_ld, 16)
                    sp.dma_start(masks0[:, P:P + WIN], T["window_prev"]).then_inc(c_ld, 16)
                    sp.wait_ge(c_ld, 96)

                @block.gpsimd
                def _(pool):
                    nc.gpsimd.memset(v[:, :, :, :], 1.0)
                    nc.gpsimd.memset(kz[:, :, :, :, :], 0.0)
                    nc.gpsimd.memset(pp[:, :, :], 0.0)
                    nc.gpsimd.memset(hid[:, :, 2, :], 1.0)

                @block.vector
                def _(dve):
                    for part in (xT_hi, xT_lo):
                        nc.vector.memset(part[64:128, 0:1].bitcast(F32), 0.0)
                    dve.wait_ge(c_ld, 96)
                    nc.vector.tensor_copy(own_bf[:, :], masks0[:, 0:P])
                    nc.vector.tensor_copy(prev_bf[:, :], masks0[:, P:P + WIN])

            def pair_fill(part, l, i, kind):
                in_part = {"first": {"x": 1, "xT": 2}, "loop": {"x": 3, "xT": 4, "out": 5}, "last": {"out": 3}}[part]
                return l * (3 * NB) + (0 if part == "first" else i * 3) + in_part[kind]

            ring = [bank[i] for i in (2, 5, 6, 7)]
            fring = bank[6:8]
            NP = NB
            with nc.Block() as block:
                @block.sync
                def _(sp):
                    with sp.Fori(0, DEPTH) as l:
                        sp.wait_ge(x_attn, l * B * SEQ + 1)
                        sp.dma_start(wqkv[:, :], wqkv_d[l]).then_inc(wa_ld, 16)
                        sp.dma_start(wo[:, :, :], wo_d[l].rearrange("(k p) c -> p k c", p=P)).then_inc(wa_ld, 16)
                        for i, n in enumerate(("L0_ffn_q_scale", "L0_ffn_k_scale")):
                            sp.dma_start(qk_gain[:, i, :], T[n][bass.ds(l, 1), :].broadcast_to((P, BD))).then_inc(wa_ld, 16)

                        def fetch(b):
                            sp.wait_ge(x_ffn, l * B + b + 1)
                            sp.wait_ge(x_full, l * B + b + 1)
                            sp.dma_start(xcur[:, :, :], X[:, bass.ds(b * LT, LT), :]).then_inc(x_copied, 16)

                        fetch(0)
                        sp.wait_ge(x_ffn, l * B + B)
                        sp.dma_start(w1[:, :], T["L0_ffn_W1"][l]).then_inc(wf_ld, 16)
                        w2_d = T["L0_ffn_W2"][l]
                        sp.dma_start(w2[:, 0:2, :], w2_d[0:256, :].rearrange("(k p) c -> p k c", p=P)).then_inc(wf_ld, 16)
                        sp.dma_start(w2[0:FCH[2], 2, :], w2_d[256:FF, :]).then_inc(wf_ld, 16)
                        for part in range(2):
                            b1_d = T["L0_ffn_b1"][l][part * FF:(part + 1) * FF]
                            sp.dma_start(b1[:, 3 * part:3 * part + 2], b1_d[0:256].rearrange("(k p) -> p k", p=P),
                                         allow_slow_non_contiguous=True).then_inc(wf_ld, 16)
                            sp.dma_start(b1[0:FCH[2], 3 * part + 2:3 * part + 3],
                                         b1_d[256:FF].rearrange("(p k) -> p k", k=1),
                                         allow_slow_non_contiguous=True).then_inc(wf_ld, 16)
                        sp.dma_start(w2[FCH[2]:FCH[2] + 1, 2, :], T["L0_ffn_b2"][bass.ds(l, 1), :]).then_inc(wf_ld, 16)
                        with sp.Fori(1, B) as b:
                            fetch(b)

                @block.gpsimd
                def _(pool):
                    with pool.Fori(0, DEPTH) as l:
                        for c in range(3):
                            cs = slice(c * INNER, (c + 1) * INNER)
                            pool.wait_ge(wa_ld, (l + 1) * 16 * N_WA)
                            nc.gpsimd.tensor_tensor(w_hi[:, cs], wqkv[:, cs], ones[:, 0:1].broadcast_to((P, INNER)),
                                                    ALU.mult).then_inc(w_split, 1)
                            pool.wait_ge(w_split, l * 6 + 2 * c + 1)
                            nc.gpsimd.tensor_tensor(w_lo[:, cs], wqkv[:, cs], w_hi[:, cs].bitcast(F32),
                                                    ALU.subtract).then_inc(w_split, 1)
                        with pool.Fori(0, B) as b:
                            for s in range(SEQ):
                                m, i = (l * B + b) * SEQ + s + 1, s % 2
                                pool.wait_ge(floor_done, m)
                                nc.gpsimd.tensor_tensor(rnorm[:, i, :], ss[:, i, :], neghalf[:, :],
                                                        ALU.pow).then_inc(rn_done, 1)
                                pool.wait_ge(t_done, m)
                                nc.gpsimd.tensor_tensor(rot[:, i, :, :], t1[:, i, :, :], t2[:, i, :, :],
                                                        ALU.add).then_inc(rot_done, 1)
                                pool.wait_ge(rot_done, m)
                                pool.wait_ge(rn_done, m)
                                nc.gpsimd.tensor_tensor(qk[:, i, :, :], rot[:, i, :, :],
                                                        rnorm[:, i, :, None].broadcast_to((P, 16, BD)),
                                                        ALU.mult).then_inc(qk_done, 1)
                        with pool.Fori(0, NP) as i:
                            n = l * NP + i
                            for q in range(2):
                                pool.wait_ge(var_done, n * 2 + q + 1)
                                nc.gpsimd.tensor_tensor(frstd[:, q, :], fvar[:, q, :], neghalf[:, 0:LT],
                                                        ALU.pow).then_inc(rstd_done, 1)

                @block.tensor
                def _(pe):
                    with pe.Fori(0, DEPTH) as l:
                        def room(part, b, name):
                            i, number = ring_fill(part, l, b, name)
                            pe.wait_ge(ring_free[i], number)
                            return ring[i], ring_full[i]

                        def out_of(part, b, name):
                            i, number = ring_fill(part, l, b, name)
                            pe.wait_ge(ring_free[i], number + 1)

                        def turn_x(seq):
                            pe.wait_ge(x_copied, 16 * (seq + 1))
                            for t in range(LT):
                                last = nc.tensor.transpose(bank[0][:, t * P:(t + 1) * P], xcur[:, t, :], ident[:, :])
                            last.then_inc(x_full, 1)

                        def turn_qk(part, b, s, m):
                            pe.wait_ge(qk_done, m)
                            for a, name in enumerate("qk"):
                                r, full = room(part, b, (name, s))
                                for p in range(4):
                                    last = nc.tensor.transpose(
                                        r[:, p * P:(p + 1) * P],
                                        qk[:, s % 2, a * 8 + 2 * p:a * 8 + 2 * p + 2, :].rearrange("p h d -> p (h d)"),
                                        ident[:, :])
                                last.then_inc(full, 1)

                        def project(part, b, s, m, before):
                            hg, t = s % SEQ // 2, s % 2
                            ts = slice(t * P, (t + 1) * P)
                            cols = [slice(a * INNER + hg * 512, a * INNER + hg * 512 + 512) for a in range(3)]
                            seq = l * B + 2 * b + s // SEQ

                            def by_high(r, a):
                                nc.tensor.matmul(r, xT_hi[:, ts], w_hi[:, cols[a]], start=True, stop=False)
                                nc.tensor.matmul(r, xT_hi[:, ts], w_lo[:, cols[a]], start=False, stop=False)

                            def by_low(r, a):
                                return nc.tensor.matmul(r, xT_lo[:, ts], w_hi[:, cols[a]], start=False, stop=True)

                            if s % SEQ == 0:
                                pe.wait_ge(hi_done, seq + 1)
                            if before:
                                pe.wait_ge(t_done, m - 1)
                            by_high(bank[1], 1)
                            if s % SEQ == 0:
                                pe.wait_ge(lo_done, seq + 1)
                            by_low(bank[1], 1)
                            by_high(bank[0], 0)
                            by_low(bank[0], 0).then_inc(qk_full, 1)
                            r, full = room(part, b, ("v", s))
                            by_high(r, 2)
                            by_low(r, 2).then_inc(full, 1)

                        def turn_probs(part, b, s, m):
                            pe.wait_ge(exp_done, m)
                            if s % 2:
                                r, full = room(part, b, ("pp", s))
                                nc.tensor.matmul(r[:, 0:WIN], pp[:, 0, :], ident[0:WIN, 0:WIN], start=True, stop=True)
                                for h in range(1, 8):
                                    last = nc.tensor.transpose(r[:, h * WIN:(h + 1) * WIN], pp[:, h, :],
                                                               ident[0:WIN, 0:WIN])
                                last.then_inc(full, 1)
                            for half in range(2):
                                r, full = room(part, b, (f"p{half}", s))
                                for h in range(4):
                                    last = nc.tensor.transpose(r[:, h * P:(h + 1) * P], pr[:, s % 2, 4 * half + h, :],
                                                               ident[:, :])
                                last.then_inc(full, 1)

                        def scores(part, b, s):
                            t = s % 2
                            out_of(part, b, ("q", s))
                            out_of(part, b, ("k", s))
                            for half in range(2):
                                sc = bank[3 + half]
                                nc.tensor.matmul(sc.rearrange("p (h j) -> p h j", h=4), ident_bf[:, :],
                                                 own_bf[:, None, :].broadcast_to((P, 4, P)),
                                                 start=True, stop=False, skip_group_check=True)
                                for p in range(2):
                                    last = nc.tensor.matmul(
                                        sc[:, p * 2 * P:(p + 1) * 2 * P], qTs[:, 2 * half + p, :],
                                        kz[:, t, 2 * half + p, :, :].rearrange("p h j -> p (h j)"),
                                        start=False, stop=(p == 1), skip_group_check=True)
                            last.then_inc(sc_full, 1)
                            if t:
                                r, full = room(part, b, ("prev", s))
                                sc = r[:, 0:8 * WIN]
                                nc.tensor.matmul(sc.rearrange("p (h j) -> p h j", h=8), ident_bf[:, :],
                                                 prev_bf[:, None, :].broadcast_to((P, 8, WIN)),
                                                 start=True, stop=False, skip_group_check=True)
                                for p in range(4):
                                    last = nc.tensor.matmul(
                                        sc[:, p * 2 * WIN:(p + 1) * 2 * WIN].rearrange("p (h j) -> p h j", h=2),
                                        qTs[:, p, :], kz[:, 0, p, :, P - WIN:P],
                                        start=False, stop=(p == 3), skip_group_check=True)
                                last.then_inc(full, 1)

                        def outputs(part, b, s):
                            t = s % 2
                            for half in range(2):
                                out_of(part, b, (f"p{half}", s))
                                if t and not half:
                                    out_of(part, b, ("pp", s))
                                r, full = room(part, b, (f"o{half}", s))
                                for h in range(4):
                                    hh = 4 * half + h
                                    c = slice(h * (BD + 1), (h + 1) * (BD + 1))
                                    last = nc.tensor.matmul(r[:, c], prT[:, hh, :], v[:, s % NS, hh, :],
                                                            start=(h == 0), stop=(h == 3 and not t),
                                                            skip_group_check=True)
                                if t:
                                    for h in range(4):
                                        hh = 4 * half + h
                                        c = slice(h * (BD + 1), (h + 1) * (BD + 1))
                                        last = nc.tensor.matmul(r[0:WIN, c], ppT[:, hh, :], v[:, (s - 1) % NS, hh, :],
                                                                start=False, stop=(h == 3), skip_group_check=True)
                                last.then_inc(full, 1)

                        def turn_outputs(part, b, s, m):
                            pe.wait_ge(o_done, 2 * m)
                            r, full = room(part, b, ("oT", s))
                            for p in range(4):
                                last = nc.tensor.transpose(
                                    r[:, p * P:(p + 1) * P],
                                    o[:, 2 * p:2 * p + 2, :].rearrange("p h d -> p (h d)"), ident[:, :])
                            last.then_inc(full, 1)

                        def through_wo(part, b, s):
                            out_of(part, b, ("oT", s))
                            r, full = room(part, b, ("w", s))
                            for p in range(4):
                                last = nc.tensor.matmul(r[:, 0:D], oT[:, p, :], wo[:, 4 * (s % SEQ // 2) + p, :],
                                                        start=(p == 0), stop=(p == 3))
                            last.then_inc(full, 1)

                        def slots(part, b):
                            ok = lambda step: valid(part, step)
                            for j in SLOTS[part]:
                                m = (l * NB + b) * NS + j + 1
                                if part == "first" and j == -SEQ:
                                    turn_x(l * B)
                                if ok(j + 2):
                                    turn_qk(part, b, j + 2, m + 2)
                                if ok(j + 4):
                                    project(part, b, j + 4, m + 4, before=ok(j + 3))
                                if ok(j):
                                    turn_outputs(part, b, j, m)
                                if ok(j + 1):
                                    turn_probs(part, b, j + 1, m + 1)
                                if ok(j + 2):
                                    scores(part, b, j + 2)
                                if ok(j):
                                    through_wo(part, b, j)
                                if x_follows(part, j):
                                    pe.wait_ge(t_done, m + 4)
                                    turn_x(l * B + 2 * b + (j + 5) // SEQ)
                                if ok(j + 1):
                                    outputs(part, b, j + 1)

                        pe.wait_ge(wa_ld, (l + 1) * 16 * N_WA)
                        pe.wait_ge(w_split, (l + 1) * 6)
                        slots("first", 0)
                        with pe.Fori(0, NB - 1) as b:
                            slots("loop", b)
                        slots("last", NB - 1)
                        def pair_room(part, i, q, kind):
                            pe.wait_ge(fr_free[q], pair_fill(part, l, i, kind))
                            return fring[q], fr_full[q]

                        def shift_x(part, i, pair, q):
                            r, full = pair_room(part, i, q, "x")
                            r3 = r[:, 0:S].rearrange("p (t c) -> p t c", t=LT)
                            first = pair * 2 * LT + q * LT
                            half = D // 2
                            nc.tensor.matmul(r3[:, :, half:D], shift_in[:, :], X[:, bass.ds(first, LT), half:D],
                                             start=True, stop=False, skip_group_check=True)
                            nc.tensor.matmul(r3[:, 1:2, half:D], shift_over[:, :], X[:, bass.ds(first, 1), half:D],
                                             start=False, stop=False, skip_group_check=True)
                            nc.tensor.matmul(r3[:, :, 0:half], ident[:, :], X[:, bass.ds(first, LT), 0:half],
                                             start=False, stop=True, skip_group_check=True).then_inc(full, 1)

                        def turn_xn(part, i, pair, q):
                            pe.wait_ge(xn_done, (l * NP + pair) * 4 + 2 * q + 2)
                            r, full = pair_room(part, i, q, "xT")
                            for t in range(LT):
                                last = nc.tensor.transpose(r[:, t * P:(t + 1) * P], xn[:, q, t, :], ident[:, :])
                            last.then_inc(full, 1)

                        def hidden(i, q):
                            for k, (c0, c1) in enumerate(((3, 4), (0, 1), (5, 2))):
                                r = bank[3 * q + k]
                                for j, c in enumerate((c0, c1)):
                                    w, f = FCH[c % 3], (c // 3) * FF + 128 * (c % 3)
                                    last = nc.tensor.matmul(r[0:w, j * S:(j + 1) * S], w1[:, f:f + w], xnT[:, q, :],
                                                            start=(j == 0), stop=(j == 1), skip_group_check=True)
                                last.then_inc(hg_full, 1)

                        def pair_outputs(part, i, q):
                            pe.wait_ge(hid_done, (l * NP + i) * 2 + q + 1)
                            r, full = pair_room(part, i, q, "out")
                            for t in range(LT):
                                for c in range(3):
                                    w = FCH[c] + (c == 2)
                                    last = nc.tensor.matmul(r[:, t * D:(t + 1) * D],
                                                            hid[0:w, q, c, t * P:(t + 1) * P], w2[0:w, c, :],
                                                            start=(t == 0 and c == 0), stop=(t == 1 and c == 2),
                                                            skip_group_check=True)
                            last.then_inc(full, 1)

                        def pair_slot(part, i):
                            ahead = {"first": 0, "loop": i + 1, "last": None}[part]
                            if part != "last":
                                for q in range(2):
                                    shift_x(part, i, ahead, q)
                            if part != "first":
                                for q in range(2):
                                    if part == "loop":
                                        pe.wait_ge(fr_free[q], pair_fill(part, l, i, "x"))
                                    else:
                                        pe.wait_ge(fr_free[q], pair_fill(part, l, i, "out"))
                                    hidden(i, q)
                            if part != "last":
                                for q in range(2):
                                    turn_xn(part, i, ahead, q)
                            if part != "first":
                                for q in range(2):
                                    pair_outputs(part, i, q)

                        for f, c in zip(ring_free, RL):
                            pe.wait_ge(f, (l + 1) * (NB * c) + 1)
                        pe.wait_ge(wf_ld, (l + 1) * 16 * N_WF)
                        pair_slot("first", 0)
                        with pe.Fori(0, NP - 1) as i:
                            pair_slot("loop", i)
                        pair_slot("last", NP - 1)
                        for f in fr_free:
                            pe.wait_ge(f, (l + 1) * (3 * NP) + 1)

                @block.scalar
                def _(act):
                    with act.Fori(0, DEPTH) as l:
                        act.wait_ge(x_ffn, l * B + B)
                        act.dma_start(lng[:, :], T["L0_ffn_ln_g"][bass.ds(l, 1), :].rearrange("a c -> c a"),
                                      allow_slow_non_contiguous=True).then_inc(wf_ld, 16)
                        act.dma_start(lnb[:, :], T["L0_ffn_ln_b"][bass.ds(l, 1), :].rearrange("a c -> c a"),
                                      allow_slow_non_contiguous=True).then_inc(wf_ld, 16)
                        def take(part, b, name):
                            i, number = ring_fill(part, l, b, name)
                            act.wait_ge(ring_full[i], number)
                            return ring[i], ring_free[i]

                        def turned_x(seq):
                            act.wait_ge(x_full, seq + 2)
                            r = bank[0]
                            nc.scalar.copy(xT_hi[0:64, 0:S], r[0:64, 0:S])
                            nc.scalar.copy(xT_hi[64:128, 1:S], r[64:128, 0:S - 1]).then_inc(hi_done, 1)

                        def turned_qk(part, b, s):
                            r, free = take(part, b, ("q", s))
                            nc.scalar.copy(qTs[:, :, :], r.rearrange("p (a i) -> p a i", a=4)).then_inc(free, 1)
                            r, free = take(part, b, ("k", s))
                            for j in range(2):
                                last = nc.scalar.copy(kz[64 * j:64 * j + 64, s % 2, :, j, :],
                                                      r[64 * j:64 * j + 64, :].rearrange("p (a i) -> p a i", a=4))
                            last.then_inc(free, 1)

                        def squares(m, before):
                            act.wait_ge(qk_full, m)
                            if before:
                                act.wait_ge(ss_done, m - 1)
                            nc.scalar.activation(sq[:, :], psum[:, 0:2, :].rearrange("p a c -> p (a c)"),
                                                 ACT.Square).then_inc(sq_done, 1)

                        def turned_probs(part, b, s):
                            if s % 2:
                                r, free = take(part, b, ("pp", s))
                                nc.scalar.copy(ppT[:, :, :], r[:, 0:8 * WIN].rearrange("p (h i) -> p h i", h=8)
                                               ).then_inc(free, 1)
                            for half in range(2):
                                r, free = take(part, b, (f"p{half}", s))
                                nc.scalar.copy(prT[:, 4 * half:4 * half + 4, :],
                                               r.rearrange("p (h i) -> p h i", h=4)).then_inc(free, 1)

                        def turned_outputs(part, b, s):
                            r, free = take(part, b, ("oT", s))
                            nc.scalar.copy(oT[:, :, :], r.rearrange("p (a i) -> p a i", a=4)).then_inc(free, 1)

                        def through_wo(part, b, s, m):
                            r, free = take(part, b, ("w", s))
                            act.wait_ge(x_attn, m)
                            nc.scalar.copy(w_out[:, :], r[:, 0:D]).then_inc(free, 1)

                        def exps(s, m):
                            act.wait_ge(sub_done, m)
                            if s % 2:
                                nc.scalar.activation(pp[:, :, P - WIN:P], pp0[:, :, :], ACT.Exp)
                            nc.scalar.activation(pr[:, s % 2, :, :], pr[:, s % 2, :, :], ACT.Exp).then_inc(exp_done, 1)

                        def slots(part, b):
                            ok = lambda step: valid(part, step)
                            for j in SLOTS[part]:
                                m = (l * NB + b) * NS + j + 1
                                if part == "first" and j == -SEQ:
                                    turned_x(l * B)
                                if ok(j + 2):
                                    turned_qk(part, b, j + 2)
                                if ok(j + 4):
                                    squares(m + 4, before=ok(j + 3))
                                if ok(j):
                                    turned_outputs(part, b, j)
                                if ok(j + 1):
                                    turned_probs(part, b, j + 1)
                                if ok(j):
                                    through_wo(part, b, j, m)
                                if x_follows(part, j):
                                    turned_x(l * B + 2 * b + (j + 5) // SEQ)
                                if ok(j + 2):
                                    exps(j + 2, m + 2)

                        slots("first", 0)
                        with act.Fori(0, NB - 1) as b:
                            slots("loop", b)
                        slots("last", NB - 1)
                        def gates(i, q):
                            for k, c in ((0, 0), (0, 1), (2, 2)):
                                act.wait_ge(hg_full, (l * NP + i) * 6 + 3 * q + k + 1)
                                w = FCH[c]
                                r = bank[3 * q + k][0:w, (c % 2) * S:(c % 2) * S + S]
                                last = nc.scalar.activation(gel[0:w, q, c, :], r, ACT.Gelu,
                                                            bias=b1[0:w, 3 + c:4 + c])
                            last.then_inc(gel_done, 1)

                        def turned_xn(part, i, q):
                            act.wait_ge(fr_full[q], pair_fill(part, l, i, "xT"))
                            nc.scalar.activation(xnT[:, q, :], fring[q][:, 0:S], ACT.Identity, bias=lnb[:, 0:1],
                                                 scale=lng[:, 0:1]).then_inc(fr_free[q], 1)

                        def pair_slot(part, i):
                            if part != "first":
                                for q in range(2):
                                    gates(i, q)
                            if part != "last":
                                for q in range(2):
                                    turned_xn(part, i, q)

                        act.wait_ge(wf_ld, (l + 1) * 16 * N_WF)
                        pair_slot("first", 0)
                        with act.Fori(0, NP - 1) as i:
                            pair_slot("loop", i)
                        pair_slot("last", NP - 1)

                @block.vector
                def _(dve):
                    for f in (*ring_free, *fr_free):
                        dve.sem_inc(f, 1)
                    dve.sem_inc(x_full, 1)
                    dve.sem_inc(x_ffn, B)
                    dve.sem_inc(x_attn, 1)
                    with dve.Fori(0, DEPTH) as l:
                        dve.wait_ge(wa_ld, (l + 1) * 16 * N_WA)
                        g2 = lambda c: qk_gain[:, None, :, c].broadcast_to((P, LT, 2, BD if c == slice(0, BD) else BD // 2))
                        lo, hi = slice(0, BD // 2), slice(BD // 2, BD)
                        nc.vector.tensor_tensor(cosg[:, :, :, :], cos0[:, :, :, :], g2(slice(0, BD)), ALU.mult).then_inc(gains, 1)
                        nc.vector.tensor_tensor(sing[:, :, :, lo], sin0[:, :, :, lo], g2(hi), ALU.mult).then_inc(gains, 1)
                        nc.vector.tensor_tensor(sing[:, :, :, hi], sin0[:, :, :, hi], g2(lo), ALU.mult).then_inc(gains, 1)
                        def take(part, b, name):
                            i, number = ring_fill(part, l, b, name)
                            dve.wait_ge(ring_full[i], number)
                            return ring[i], ring_free[i]

                        def rest_of_x(seq):
                            dve.wait_ge(hi_done, seq + 1)
                            r = bank[0]
                            nc.vector.tensor_tensor(xT_lo[0:64, 0:S], r[0:64, 0:S], xT_hi[0:64, 0:S].bitcast(F32),
                                                    ALU.subtract)
                            nc.vector.tensor_tensor(xT_lo[64:128, 1:S], r[64:128, 0:S - 1],
                                                    xT_hi[64:128, 1:S].bitcast(F32),
                                                    ALU.subtract).then_inc(lo_done, 1)

                        def values(part, b, s):
                            r, free = take(part, b, ("v", s))
                            nc.vector.tensor_copy(v[:, s % NS, :, 0:BD],
                                           r.rearrange("p (h d) -> p h d", h=8)).then_inc(free, 1)

                        def rotate(part, s, m):
                            t, two_back = s % 2, valid(part, s - 2)
                            dve.wait_ge(sq_done, m)
                            if two_back:
                                dve.wait_ge(rn_done, m - 2)
                            nc.vector.tensor_reduce(ss[:, t, :], sq[:, :].rearrange("p (h d) -> p h d", d=BD), AX.X,
                                                    ALU.add).then_inc(ss_done, 1)
                            dve.wait_ge(ss_done, m)
                            nc.vector.tensor_scalar(ss[:, t, :], ss[:, t, :], 1e-24, None, ALU.max).then_inc(floor_done, 1)
                            x4 = psum[:, 0:2, :].rearrange("p a (h d) -> p a h d", d=BD)
                            t14 = t1[:, t, :, :].rearrange("p (a h) d -> p a h d", a=2)
                            t24 = t2[:, t, :, :].rearrange("p (a h) d -> p a h d", a=2)
                            tab = lambda g, c, w: g[:, t, :, None, c].broadcast_to((P, 2, 8, w))
                            if two_back:
                                dve.wait_ge(rot_done, m - 2)
                            nc.vector.tensor_tensor(t14, x4, tab(cosg, slice(0, BD), BD), ALU.mult)
                            nc.vector.tensor_tensor(t24[:, :, :, lo], x4[:, :, :, hi], tab(sing, lo, BD // 2), ALU.mult)
                            nc.vector.tensor_tensor(t24[:, :, :, hi], x4[:, :, :, lo], tab(sing, hi, BD // 2),
                                                    ALU.mult).then_inc(t_done, 1)

                        def less_maxima(part, b, s, m):
                            t = s % 2
                            odd = (l * NB + b) * (NS // 2) + s // 2 + 1
                            dve.wait_ge(sc_full, m)
                            own = psum[:, 3:5, :].rearrange("p a (h j) -> p (a h) j", h=4)
                            nc.vector.tensor_reduce(m_own[:, :], own, AX.X, ALU.max).then_inc(mo_done, 1)
                            if t:
                                r, free = take(part, b, ("prev", s))
                                prev = r[0:WIN, 0:8 * WIN].rearrange("p (h j) -> p h j", h=8)
                                nc.vector.tensor_reduce(m_prev[:, :], prev, AX.X, ALU.max).then_inc(mp_done, 1)
                                dve.wait_ge(mo_done, m)
                                dve.wait_ge(mp_done, odd)
                                nc.vector.tensor_tensor(m_own[0:WIN, :], m_own[0:WIN, :], m_prev[:, :],
                                                        ALU.max).then_inc(mx_done, 1)
                                dve.wait_ge(mx_done, odd)
                                nc.vector.tensor_tensor(pp0[:, :, :], prev,
                                                        m_own[0:WIN, :, None].broadcast_to((WIN, 8, WIN)),
                                                        ALU.subtract).then_inc(free, 1)
                            else:
                                dve.wait_ge(mo_done, m)
                            nc.vector.tensor_tensor(pr[:, t, :, :], own, m_own[:, :, None].broadcast_to((P, 8, P)),
                                                    ALU.subtract).then_inc(sub_done, 1)

                        def residual(part, b, s, m):
                            i, number = ring_fill(part, l, b, ("w", s))
                            dve.wait_ge(ring_free[i], number + 1)
                            xt = X[:, bass.ds(b * 2 * LT + s // SEQ * LT + s % 2, 1), :].rearrange("p a c -> p (a c)")
                            nc.vector.tensor_tensor(xt, w_out[:, :], xt, ALU.add).then_inc(x_attn, 1)

                        def normalise(part, b, s, m):
                            for half in range(2):
                                r, free = take(part, b, (f"o{half}", s))
                                r4 = r[:, 0:4 * (BD + 1)].rearrange("p (h d) -> p h d", h=4)
                                hs = slice(4 * half, 4 * half + 4)
                                nc.vector.reciprocal(rs[:, hs], r4[:, :, BD]).then_inc(rs_done, 1)
                                dve.wait_ge(rs_done, 2 * (m - 1) + half + 1)
                                nc.vector.tensor_tensor(o[:, hs, :], r4[:, :, 0:BD],
                                                        rs[:, hs, None].broadcast_to((P, 4, BD)),
                                                        ALU.mult).then_inc(o_done, 1)
                                dve.wait_ge(o_done, 2 * (m - 1) + half + 1)
                                dve.sem_inc(free, 1)

                        def slots(part, b):
                            ok = lambda step: valid(part, step)
                            for j in SLOTS[part]:
                                m = (l * NB + b) * NS + j + 1
                                if part == "first" and j == -SEQ:
                                    rest_of_x(l * B)
                                if ok(j + 4):
                                    values(part, b, j + 4)
                                    rotate(part, j + 4, m + 4)
                                if ok(j + 2):
                                    less_maxima(part, b, j + 2, m + 2)
                                if x_follows(part, j):
                                    rest_of_x(l * B + 2 * b + (j + 5) // SEQ)
                                if ok(j):
                                    residual(part, b, j, m)
                                if ok(j + 1):
                                    normalise(part, b, j + 1, m + 1)

                        dve.wait_ge(gains, l * 3 + 3)
                        slots("first", 0)
                        with dve.Fori(0, NB - 1) as b:
                            slots("loop", b)
                        slots("last", NB - 1)
                        def norm_x(part, i, pair, q):
                            n = l * NP + pair
                            xs = fring[q][:, 0:S].rearrange("p (t c) -> p t c", t=LT)
                            dve.wait_ge(fr_full[q], pair_fill(part, l, i, "x"))
                            nc.vector.memset(pause[:, :], 0.0)
                            for t in range(LT):
                                nc.vector.bn_stats(st6[:, q, t, :], xs[:, t, :]).then_inc(st_done, 1)
                            dve.wait_ge(st_done, n * 4 + 2 * q + 2)
                            nc.vector.memset(pause[:, :], 0.0)
                            for t in range(LT):
                                nc.vector.bn_aggr(mv[:, q, t, :], st6[:, q, t, :]).then_inc(mv_done, 1)
                            dve.wait_ge(mv_done, n * 4 + 2 * q + 2)
                            nc.vector.tensor_scalar(fvar[:, q, :], mv[:, q, :, 1], EPS, None,
                                                    ALU.add).then_inc(var_done, 1)

                        def scale_x(part, i, pair, q):
                            n = l * NP + pair
                            xs = fring[q][:, 0:S].rearrange("p (t c) -> p t c", t=LT)
                            dve.wait_ge(rstd_done, n * 2 + q + 1)
                            for t in range(LT):
                                nc.vector.tensor_scalar(xn[:, q, t, :], xs[:, t, :], mv[:, q, t, 0:1],
                                                        frstd[:, q, t:t + 1], ALU.subtract,
                                                        ALU.mult).then_inc(xn_done, 1)
                            dve.wait_ge(xn_done, n * 4 + 2 * q + 2)
                            dve.sem_inc(fr_free[q], 1)

                        def gated(i, q):
                            n = l * NP + i
                            dve.wait_ge(hg_full, n * 6 + 3 * q + 3)
                            dve.wait_ge(gel_done, n * 2 + q + 1)
                            for c in range(3):
                                w = FCH[c]
                                r = bank[3 * q + (2 if c == 2 else 1)]
                                r = r[0:w, S:2 * S] if c in (1, 2) else r[0:w, 0:S]
                                last = nc.vector.scalar_tensor_tensor(
                                    out=hid[0:w, q, c, :], in0=r, scalar=b1[0:w, c:c + 1],
                                    in1=gel[0:w, q, c, :], op0=ALU.add, op1=ALU.mult)
                            last.then_inc(hid_done, 1)

                        def pair_residual(part, i, q):
                            dve.wait_ge(fr_full[q], pair_fill(part, l, i, "out"))
                            xt = X[:, bass.ds(i * 2 * LT + q * LT, LT), :]
                            nc.vector.tensor_tensor(xt, fring[q][:, 0:S].rearrange("p (t c) -> p t c", t=LT), xt,
                                                    ALU.add).then_inc(x_ffn, 1)
                            dve.wait_ge(x_ffn, B + (l * NP + i) * 2 + q + 1)
                            dve.sem_inc(fr_free[q], 1)

                        def pair_slot(part, i):
                            ahead = {"first": 0, "loop": i + 1, "last": None}[part]
                            if part != "last":
                                for q in range(2):
                                    norm_x(part, i, ahead, q)
                                for q in range(2):
                                    scale_x(part, i, ahead, q)
                            if part != "first":
                                for q in range(2):
                                    gated(i, q)
                                for q in range(2):
                                    pair_residual(part, i, q)

                        dve.wait_ge(wf_ld, (l + 1) * 16 * N_WF)
                        pair_slot("first", 0)
                        with dve.Fori(0, NP - 1) as i:
                            pair_slot("loop", i)
                        pair_slot("last", NP - 1)

        layer_norm("ln2", residual=XR)

        with ExitStack() as st:
            wqkv_c = sb(st, "c_wqkv", [P, 3 * D])
            wq_rep, wk_rep = (sb(st, n, [P, NG, 4, GC]) for n in ("c_wq_rep", "c_wk_rep"))
            bias_q, bias_k = sb(st, "c_bias_q", [P, NG]), sb(st, "c_bias_k", [P, NG])
            head_rows = sb(st, "c_head_rows", [P, 4])
            bias_v, bias_o = sb(st, "c_bias_v", [P, D]), sb(st, "c_bias_o", [1, D])
            wout = sb(st, "c_wout", [P, D])
            mask0 = sb(st, "c_mask0", [P, P])
            mask_in, mask_all = sb(st, "c_mask_in", [P, P], BF16), sb(st, "c_mask_all", [P, P], BF16)
            ident80 = sb(st, "c_ident80", [P, P], BF16)
            q_parts, k_parts = sb(st, "c_q_parts", [P, 2, NG, S], F32R), sb(st, "c_k_parts", [P, NG, S], F32R)
            k_diag = sb(st, "c_k_diag", [P, 2, H, S], F32R)
            vones = sb(st, "c_vones", [P, 2, LT, H, HD + 1])
            probs = sb(st, "c_probs", [P, 2, 4, S])
            probsT = sb(st, "c_probsT", [P, 2, LT, 4, P])
            nmax = sb(st, "c_nmax", [P, 2, 4])
            rsum = sb(st, "c_rsum", [P, H])
            o = sb(st, "c_o", [P, H, HD])
            oT = sb(st, "c_oT", [P, P])

            ld = sem("c_ld")
            with nc.Block() as block:
                @block.sync
                def _(sp):
                    bq = T["L1_attn_bqkv"]
                    sp.dma_start(wqkv_c[:, :], T["L1_attn_Wqkv"]).then_inc(ld, 16)
                    sp.dma_start(wout[:, :], T["L1_attn_Wout"]).then_inc(ld, 16)
                    for t, bias in ((0, bias_q), (1, bias_k)):
                        for copy in range(4):
                            sp.dma_start(bias[copy * GC:(copy + 1) * GC, :],
                                         bq[t * D:(t + 1) * D].rearrange("(g c) -> c g", g=NG),
                                         allow_slow_non_contiguous=True).then_inc(ld, 16)
                    sp.dma_start(head_rows[:, :], T["head_rows"]).then_inc(ld, 16)
                    sp.dma_start(bias_v[:, :],
                                 bq[2 * D:3 * D].rearrange("(a p) -> a p", a=1).broadcast_to((P, D))).then_inc(ld, 16)
                    sp.dma_start(bias_o[:, :], T["L1_attn_bout"].rearrange("(a p) -> a p", a=1)).then_inc(ld, 16)
                    sp.dma_start(mask0[:, :], T["causal"]).then_inc(ld, 16)
                    sp.wait_ge(ld, 16 * 14)

                @block.gpsimd
                def _(pool):
                    nc.gpsimd.memset(vones[:, :, :, :, :], 1.0)

                @block.vector
                def _(dve):
                    nc.vector.memset(mask_all[:, :], -125.0)
                    nc.vector.tensor_scalar(ident80[:, :], ident[:, :], 80.0, None, ALU.mult)
                    dve.wait_ge(ld, 16 * 14)
                    for t, rep in ((0, wq_rep), (1, wk_rep)):
                        w = wqkv_c[:, t * D:(t + 1) * D].rearrange("p (g c) -> p g c", g=NG)[:, :, None, :]
                        nc.vector.tensor_scalar(rep[:, :, :, :], w.broadcast_to((P, NG, 4, GC)),
                                                1.0 if t == 0 else SCALE_A, None, ALU.mult)
                    nc.vector.tensor_scalar(bias_k[:, :], bias_k[:, :], SCALE_A, None, ALU.mult)
                    nc.vector.tensor_copy(mask_in[:, :], mask0[:, :])

            CS = 4 * LT
            NSC = 2 * CS
            CSLOTS = {"first": range(-4, 0), "loop": range(NSC), "last": range(NSC)}

            def cvalid(part, step):
                return {"first": step >= 0, "loop": True, "last": step < NSC}[part]

            def prepares(part, s):
                what = {2: "x", 3: "k0", 4: "k1", 5: "q0", 6: "q1", 0: "v"}.get(s % CS)
                q = s // CS + (what != "v") + (2 if part == "first" else 0)
                return (what, q) if what and cvalid(part, s) and cvalid(part, q * CS) else None

            def sequence_of(part, b, q):
                return q - 2 if part == "first" else b * 2 + q

            def misc_fills(part):
                fills = [(what, 2) for what in ("x", "k0", "k1", "q0", "q1")] if part == "first" else []
                for j in CSLOTS[part]:
                    if prepares(part, j + 4):
                        what, q = prepares(part, j + 4)
                        fills.append((what, q))
                    if (j + 1) % 4 == 3 and cvalid(part, j + 1):
                        fills.append(("oT", (j + 1) // 4))
                    if j % 4 == 3 and cvalid(part, j):
                        fills.append(("w", j // 4))
                return fills

            misc_fill, _ = ring_plan({part: misc_fills(part) for part in CSLOTS}, 1)
            o_bank, misc = bank[0], bank[1]
            score, turned = [psum[:, 2:4, :], psum[:, 4:6, :]], bank[6:8]
            x_copied, misc_full, misc_free, high_ok, k_ok, diag_ok = (
                sem(f"c_{n}") for n in ("x_copied", "misc_full", "misc_free", "high_ok", "k_ok", "diag_ok"))
            score_full, max_ok, exp_done = sem("c_score_full"), sem("c_max_ok"), sem("c_exp_done")
            turn_full, turn_out, o_full = sem("c_turn_full"), sem("c_turn_out"), sem("c_o_full")
            rsum_ok, o_ok = sem("c_rsum_ok"), sem("c_o_ok")

            with nc.Block() as block:
                @block.gpsimd
                def _(pool):
                    with pool.Fori(0, B // 2) as b:
                        for q in range(2):
                            nc.gpsimd.tensor_copy(xcur[:, :, :],
                                                  X[:, bass.ds(b * 2 * LT + q * LT, LT), :]).then_inc(x_copied, 1)
                            for hq in range(NG):
                                pool.wait_ge(k_ok, (b * 2 + q) * 2 + hq // 2 + 1)
                                nc.gpsimd.tensor_tensor(k_diag[:, q, hq * 4:hq * 4 + 4, :],
                                                        k_parts[:, hq:hq + 1, :].bitcast(F32).broadcast_to((P, 4, S)),
                                                        head_rows[:, :, None].broadcast_to((P, 4, S)),
                                                        ALU.mult).then_inc(diag_ok, 1)

                @block.tensor
                def _(pe):
                    def slots(part, b):
                        def room(name):
                            _, number = misc_fill(part, b, name)
                            pe.wait_ge(misc_free, number)
                            return misc

                        def out_of(name):
                            _, number = misc_fill(part, b, name)
                            pe.wait_ge(misc_free, number + 1)

                        def turn_x(q, seq):
                            pe.wait_ge(x_copied, seq + 1)
                            r = room(("x", q))
                            for t in range(LT):
                                last = nc.tensor.transpose(r[:, t * P:(t + 1) * P], xcur[:, t, :], ident[:, :])
                            last.then_inc(misc_full, 1)

                        def project_groups(what, q):
                            if what == "k0":
                                out_of(("x", q))
                            rep, g = {"q": wq_rep, "k": wk_rep}[what[0]], 2 * int(what[1])
                            r = room((what, q))
                            for j in range(2):
                                last = nc.tensor.matmul(r[:, j * S:(j + 1) * S],
                                                        rep[:, g + j, :, :].rearrange("p a c -> p (a c)"), xT[:, :],
                                                        start=(j == 0), stop=(j == 1), skip_group_check=True)
                            last.then_inc(misc_full, 1)

                        def project_v(q):
                            r = room(("v", q))
                            for t in range(LT):
                                last = nc.tensor.matmul(r[:, t * D:(t + 1) * D], xT[:, t * P:(t + 1) * P],
                                                        wqkv_c[:, 2 * D:3 * D], start=(t == 0), stop=(t == 1),
                                                        skip_group_check=True)
                            last.then_inc(misc_full, 1)

                        def scores(s, m):
                            q, lt, hq = s // CS, s % CS // 4, s % 4
                            if cvalid(part, s - 2):
                                pe.wait_ge(exp_done, m - 2)
                            if lt == 0:
                                pe.wait_ge(diag_ok, (b * 2 + q) * 4 + hq + 1)
                                if hq == 0:
                                    out_of(("q1", 2 if part == "first" else q))
                            for mt in range(LT):
                                sc = score[s % 2][:, mt, :]
                                last = nc.tensor.matmul(sc.rearrange("p (h m) -> p h m", h=4),
                                                        q_parts[:, q % 2, hq, lt * P:(lt + 1) * P],
                                                        k_diag[:, q % 2, hq * 4:hq * 4 + 4, mt * P:(mt + 1) * P],
                                                        start=True, stop=(mt < lt), skip_group_check=True)
                                if mt >= lt:
                                    mask = mask_in if mt == lt else mask_all
                                    last = nc.tensor.matmul(sc.rearrange("p (h m) -> p h m", h=4), ident80[:, :],
                                                            mask[:, None, :].broadcast_to((P, 4, P)),
                                                            start=False, stop=True, skip_group_check=True)
                            last.then_inc(score_full, 1)

                        def turn(s, m):
                            pe.wait_ge(exp_done, m)
                            if cvalid(part, s - 1):
                                pe.wait_ge(turn_out, m - 1)
                            for mt in range(LT):
                                for h in range(4):
                                    last = nc.tensor.transpose(turned[mt][:, h * P:(h + 1) * P],
                                                               probs[:, s % 2, h, mt * P:(mt + 1) * P], ident[:, :])
                            last.then_inc(turn_full, 1)

                        def outputs(s, m):
                            q, hq, tile = s // CS, s % 4, s // 4
                            pe.wait_ge(turn_out, m)
                            if hq == 0 and not (part == "first"):
                                pe.wait_ge(o_ok, b * 4 + tile)
                            for h in range(4):
                                hh = hq * 4 + h
                                for mt in range(LT):
                                    last = nc.tensor.matmul(o_bank[:, hh * (HD + 1):(hh + 1) * (HD + 1)],
                                                            probsT[:, s % 2, mt, h, :], vones[:, q % 2, mt, hh, :],
                                                            start=(hh == 0 and mt == 0), stop=(hh == H - 1 and mt == 1),
                                                            skip_group_check=True)
                            if hq == 3:
                                last.then_inc(o_full, 1)

                        def turn_outputs(tile):
                            pe.wait_ge(o_ok, b * 4 + tile + 1)
                            r = room(("oT", tile))
                            nc.tensor.transpose(r[:, 0:P], o[:, :, :].rearrange("p h d -> p (h d)"),
                                                ident[:, :]).then_inc(misc_full, 1)

                        def project_out(tile):
                            out_of(("oT", tile))
                            r = room(("w", tile))
                            nc.tensor.matmul(r[:, 0:D], oT[:, :], wout[:, :], start=True, stop=False)
                            nc.tensor.matmul(r[:, 0:D], ones[0:1, :], bias_o[:, :], start=False,
                                             stop=True).then_inc(misc_full, 1)

                        if part == "first":
                            turn_x(2, 0)
                            for what in ("k0", "k1", "q0", "q1"):
                                project_groups(what, 2)
                        for j in CSLOTS[part]:
                            m = b * NSC + j + 1
                            if cvalid(part, j + 4):
                                scores(j + 4, m + 4)
                            if cvalid(part, j + 3):
                                turn(j + 3, m + 3)
                            if prepares(part, j + 4):
                                what, q = prepares(part, j + 4)
                                if what == "x":
                                    turn_x(q, sequence_of(part, b, q))
                                elif what != "v":
                                    project_groups(what, q)
                                else:
                                    project_v(q)
                            if cvalid(part, j + 2):
                                outputs(j + 2, m + 2)
                            if (j + 1) % 4 == 3 and cvalid(part, j + 1):
                                turn_outputs((j + 1) // 4)
                            if j % 4 == 3 and cvalid(part, j):
                                project_out(j // 4)

                    slots("first", 0)
                    with pe.Fori(0, B // 2 - 1) as b:
                        slots("loop", b)
                    slots("last", B // 2 - 1)

                @block.scalar
                def _(act):
                    def slots(part, b):
                        def take(name):
                            _, number = misc_fill(part, b, name)
                            act.wait_ge(misc_full, number)

                        def turned_x(q):
                            take(("x", q))
                            nc.scalar.copy(xT[:, :], misc[:, 0:S]).then_inc(misc_free, 1)

                        def high_parts(what, q):
                            take((what, q))
                            parts = k_parts if what[0] == "k" else q_parts[:, q % 2, :, :]
                            bias = bias_k if what[0] == "k" else bias_q
                            for j in range(2):
                                g = 2 * int(what[1]) + j
                                last = nc.scalar.activation(parts[:, g, :], misc[:, j * S:(j + 1) * S], ACT.Identity,
                                                            bias=bias[:, g:g + 1])
                            last.then_inc(high_ok, 1)

                        def exps(s, m):
                            act.wait_ge(max_ok, m)
                            for h in range(4):
                                last = nc.scalar.activation(
                                    probs[:, s % 2, h, :].rearrange("p (t m) -> p t m", t=LT),
                                    score[s % 2][:, :, h * P:(h + 1) * P], ACT.Exp, bias=nmax[:, s % 2, h:h + 1])
                            last.then_inc(exp_done, 1)

                        def turns(s, m):
                            act.wait_ge(turn_full, m)
                            for mt in range(LT):
                                last = nc.scalar.copy(probsT[:, s % 2, mt, :, :],
                                                      turned[mt].rearrange("p (h l) -> p h l", h=4))
                            last.then_inc(turn_out, 1)

                        if part == "first":
                            turned_x(2)
                            for what in ("k0", "k1", "q0", "q1"):
                                high_parts(what, 2)
                        for j in CSLOTS[part]:
                            m = b * NSC + j + 1
                            if cvalid(part, j + 3):
                                turns(j + 3, m + 3)
                            if prepares(part, j + 4):
                                what, q = prepares(part, j + 4)
                                if what == "x":
                                    turned_x(q)
                                elif what != "v":
                                    high_parts(what, q)
                            if cvalid(part, j + 4):
                                exps(j + 4, m + 4)

                    slots("first", 0)
                    with act.Fori(0, B // 2 - 1) as b:
                        slots("loop", b)
                    slots("last", B // 2 - 1)

                @block.vector
                def _(dve):
                    dve.sem_inc(misc_free, 1)

                    def slots(part, b):
                        def take(name):
                            _, number = misc_fill(part, b, name)
                            dve.wait_ge(misc_full, number)

                        def maxima(s, m):
                            dve.wait_ge(score_full, m)
                            nc.vector.tensor_reduce(nmax[:, s % 2, :],
                                                    score[s % 2].rearrange("p t (h m) -> p h t m", h=4),
                                                    AX.XY, ALU.max, negate=True).then_inc(max_ok, 1)

                        def low_parts(what, q):
                            take((what, q))
                            half, of_k = int(what[1]), what[0] == "k"
                            parts, bias = (k_parts, bias_k) if of_k else (q_parts[:, q % 2, :, :], bias_q)
                            dve.wait_ge(high_ok, sequence_of(part, b, q) * 4 + ("k0", "k1", "q0", "q1").index(what) + 1)
                            for j in range(2):
                                g = 2 * half + j
                                for at in ([slice(GC, 2 * GC), slice(3 * GC, P)] if of_k else [slice(2 * GC, P)]):
                                    last = nc.vector.scalar_tensor_tensor(
                                        parts[at, g, :], misc[at, j * S:(j + 1) * S], bias[at, g:g + 1],
                                        parts[at, g, :].bitcast(F32), ALU.add, ALU.subtract)
                            last.then_inc(misc_free, 1)
                            if of_k:
                                dve.wait_ge(misc_free, misc_fill(part, b, (what, q))[1] + 1)
                                dve.sem_inc(k_ok, 1)

                        def projected_v(q):
                            take(("v", q))
                            nc.vector.tensor_tensor(vones[:, q % 2, :, :, 1:HD + 1],
                                                    misc[:, 0:LT * D].rearrange("p (t h d) -> p t h d", t=LT, h=H),
                                                    bias_v[:, :].rearrange("p (h d) -> p h d", h=H)[:, None, :, :]
                                                    .broadcast_to((P, LT, H, HD)), ALU.add).then_inc(misc_free, 1)

                        def normalise(tile):
                            n = b * 4 + tile + 1
                            dve.wait_ge(o_full, n)
                            r3 = o_bank[:, 0:H * (HD + 1)].rearrange("p (h d) -> p h d", h=H)
                            nc.vector.reciprocal(rsum[:, :], r3[:, :, 0]).then_inc(rsum_ok, 1)
                            dve.wait_ge(rsum_ok, n)
                            nc.vector.tensor_tensor(o[:, :, :], r3[:, :, 1:HD + 1],
                                                    rsum[:, :, None].broadcast_to((P, H, HD)),
                                                    ALU.mult).then_inc(o_ok, 1)

                        def turned_outputs(tile):
                            take(("oT", tile))
                            nc.vector.tensor_copy(oT[:, :], misc[:, 0:P]).then_inc(misc_free, 1)

                        def residual(tile):
                            take(("w", tile))
                            xt = X[:, bass.ds(b * 2 * LT + tile, 1), :].rearrange("p a c -> p (a c)")
                            nc.vector.tensor_tensor(xt, misc[:, 0:D], xt, ALU.add).then_inc(misc_free, 1)

                        if part == "first":
                            for what in ("k0", "k1", "q0", "q1"):
                                low_parts(what, 2)
                        for j in CSLOTS[part]:
                            m = b * NSC + j + 1
                            if cvalid(part, j + 4):
                                maxima(j + 4, m + 4)
                            if prepares(part, j + 4):
                                what, q = prepares(part, j + 4)
                                if what[0] in "kq":
                                    low_parts(what, q)
                                elif what == "v":
                                    projected_v(q)
                            if (j + 2) % 4 == 3 and cvalid(part, j + 2):
                                normalise((j + 2) // 4)
                            if (j + 1) % 4 == 3 and cvalid(part, j + 1):
                                turned_outputs((j + 1) // 4)
                            if j % 4 == 3 and cvalid(part, j):
                                residual(j // 4)

                    slots("first", 0)
                    with dve.Fori(0, B // 2 - 1) as b:
                        slots("loop", b)
                    slots("last", B // 2 - 1)

        layer_norm("ln3")

        with ExitStack() as st:
            gate_w = sb(st, "d_gate_w", [P, NEXP])
            w1 = sb(st, "d_w1", [P, NEXP, EH])
            b1 = sb(st, "d_b1", [P, NPR])
            w2 = sb(st, "d_w2", [P, NPR, D])
            b2 = sb(st, "d_b2", [NEXP, D])
            rows = sb(st, "d_rows", [NEXP, NPR, P])
            lower = sb(st, "d_lower", [P, NEXP, NEXP])
            xT_all = sb(st, "d_xT_all", [P, B * S])
            GD = 8
            x_group, xT_group = sb(st, "d_x_group", [P, GD, D]), sb(st, "d_xT_group", [P, GD * P])
            gmax, gsum, grec, tokw = (sb(st, n, [P, GD]) for n in ("d_gmax", "d_gsum", "d_grec", "d_tokw"))
            less, gexp, gate, rank, sel, top, coef = (
                sb(st, f"d_{n}", [P, GD, NEXP]) for n in ("less", "gexp", "gate", "rank", "sel", "top", "coef"))
            above, equal = (sb(st, n, [P, GD, NEXP, NEXP]) for n in ("d_above", "d_equal"))
            coefT_all = sb(st, "d_coefT_all", [NEXP, B * S])
            coefT = sb(st, "d_coefT", [NEXP, 2, S])
            hid = sb(st, "d_hid", [P, NPR, S])
            hidw = sb(st, "d_hidw", [P, NPR, S])

            ld = sem("d_ld")
            x_copied, xT_full, xT_ok, lg_full, exp_ok, coef_ok, ct_full, ct_ok = (
                sem(f"d_{n}") for n in ("x_copied", "xT_full", "xT_ok", "lg_full", "exp_ok", "coef_ok", "ct_full", "ct_ok"))
            less_ok, step_ok, top_ok, tokw_ok = sem("d_less_ok"), sem("d_step_ok"), sem("d_top_ok"), sem("d_tokw_ok")
            with nc.Block() as block:
                @block.sync
                def _(sp):
                    sp.dma_start(gate_w[:, :], T["L1_ffn_gate_w"]).then_inc(ld, 16)
                    sp.dma_start(lower[:, :, :].rearrange("p a c -> p (a c)"), T["lower"]).then_inc(ld, 16)
                    sp.dma_start(w1[:, :, :], T["L1_ffn_w1"].rearrange("e d h -> d e h")).then_inc(ld, 16)
                    sp.dma_start(b1[:, :], T["L1_ffn_b1"].rearrange("(a e) h -> (e h) a", e=2),
                                 allow_slow_non_contiguous=True).then_inc(ld, 16)
                    sp.dma_start(w2[:, :, :], T["L1_ffn_w2"].rearrange("(a e) h d -> (e h) a d", e=2)).then_inc(ld, 16)
                    sp.dma_start(b2[:, :], T["L1_ffn_b2"]).then_inc(ld, 16)
                    sp.dma_start(rows[:, :, :].rearrange("p a c -> p (a c)"), T["expert_rows"]).then_inc(ld, 16)
                    sp.wait_ge(ld, 16 * 7)

            xT_b, ct_b = (psum[:, i:i + 2, :].rearrange("p a c -> p (a c)") for i in (0, 4))
            lg_b = bank[2][:, 0:GD * NEXP].rearrange("p (t e) -> p t e", t=GD)
            with nc.Block() as block:
                @block.gpsimd
                def _(pool):
                    with pool.Fori(0, NT // GD) as g:
                        nc.gpsimd.tensor_copy(x_group[:, :, :], X[:, bass.ds(g * GD, GD), :]).then_inc(x_copied, 1)
                        pool.wait_ge(xT_full, g + 1)

                @block.tensor
                def _(pe):
                    with pe.Fori(0, NT // GD) as g:
                        pe.wait_ge(x_copied, g + 1)
                        for t in range(GD):
                            last = nc.tensor.transpose(xT_b[:, t * P:(t + 1) * P], x_group[:, t, :], ident[:, :])
                        last.then_inc(xT_full, 1)
                        pe.wait_ge(xT_ok, g + 1)
                        for t in range(GD):
                            last = nc.tensor.matmul(lg_b[:, t, :], xT_group[:, t * P:(t + 1) * P], gate_w[:, :],
                                                    start=(t == 0), stop=(t == GD - 1), skip_group_check=True)
                        last.then_inc(lg_full, 1)
                        pe.wait_ge(coef_ok, g + 1)
                        for t in range(GD):
                            last = nc.tensor.transpose(ct_b[0:NEXP, t * P:(t + 1) * P], coef[:, t, :], ident[:, :])
                        last.then_inc(ct_full, 1)

                @block.scalar
                def _(act):
                    with act.Fori(0, NT // GD) as g:
                        act.wait_ge(xT_full, g + 1)
                        nc.scalar.copy(xT_group[:, :], xT_b)
                        nc.scalar.copy(xT_all[:, bass.ds(g * GD * P, GD * P)], xT_b).then_inc(xT_ok, 1)
                        act.wait_ge(less_ok, g + 1)
                        nc.scalar.activation(gexp[:, :, :], less[:, :, :], ACT.Exp).then_inc(exp_ok, 1)
                        act.wait_ge(ct_full, g + 1)
                        nc.scalar.copy(coefT_all[:, bass.ds(g * GD * P, GD * P)], ct_b[0:NEXP, :]).then_inc(ct_ok, 1)

                @block.vector
                def _(dve):
                    with dve.Fori(0, NT // GD) as g:
                        STEPS = 9

                        def done(n):
                            dve.wait_ge(step_ok, g * STEPS + n)

                        by_gate = lambda t: t[:, :, None].broadcast_to((P, GD, NEXP))
                        dve.wait_ge(lg_full, g + 1)
                        nc.vector.tensor_reduce(gmax[:, :], lg_b, AX.X, ALU.max).then_inc(step_ok, 1)
                        done(1)
                        nc.vector.tensor_tensor(less[:, :, :], lg_b, by_gate(gmax), ALU.subtract).then_inc(less_ok, 1)
                        dve.wait_ge(exp_ok, g + 1)
                        nc.vector.tensor_reduce(gsum[:, :], gexp[:, :, :], AX.X, ALU.add).then_inc(step_ok, 1)
                        done(2)
                        nc.vector.reciprocal(grec[:, :], gsum[:, :]).then_inc(step_ok, 1)
                        done(3)
                        nc.vector.tensor_tensor(gate[:, :, :], gexp[:, :, :], by_gate(grec), ALU.mult).then_inc(step_ok, 1)
                        done(4)
                        mine = gate[:, :, :, None].broadcast_to((P, GD, NEXP, NEXP))
                        other = gate[:, :, None, :].broadcast_to((P, GD, NEXP, NEXP))
                        nc.vector.tensor_tensor(equal[:, :, :, :], other, mine, ALU.is_equal).then_inc(step_ok, 1)
                        nc.vector.tensor_tensor(above[:, :, :, :], other, mine, ALU.is_gt)
                        done(5)
                        nc.vector.tensor_tensor(equal[:, :, :, :], equal[:, :, :, :],
                                                lower[:, None, :, :].broadcast_to((P, GD, NEXP, NEXP)),
                                                ALU.mult).then_inc(step_ok, 1)
                        done(6)
                        nc.vector.tensor_tensor(above[:, :, :, :], above[:, :, :, :], equal[:, :, :, :],
                                                ALU.add).then_inc(step_ok, 1)
                        done(7)
                        nc.vector.tensor_reduce(rank[:, :, :], above[:, :, :, :], AX.X, ALU.add).then_inc(step_ok, 1)
                        done(8)
                        nc.vector.tensor_scalar(sel[:, :, :], rank[:, :, :], 2.0, None, ALU.is_lt).then_inc(step_ok, 1)
                        done(9)
                        nc.vector.tensor_tensor(top[:, :, :], sel[:, :, :], gate[:, :, :], ALU.mult).then_inc(top_ok, 1)
                        dve.wait_ge(top_ok, g + 1)
                        nc.vector.tensor_reduce(tokw[:, :], top[:, :, :], AX.X, ALU.add).then_inc(tokw_ok, 1)
                        dve.wait_ge(tokw_ok, g + 1)
                        nc.vector.tensor_tensor(coef[:, :, :], sel[:, :, :], by_gate(tokw), ALU.mult).then_inc(coef_ok, 1)

            c_copied, h_full, h_ok, cb_full, hw_ok, o_full, o_out = (
                sem(f"d2_{n}") for n in ("c_copied", "h_full", "h_ok", "cb_full", "hw_ok", "o_full", "o_out"))
            h_b, cb_b, o_b = psum[:, 0:2, :], psum[:, 2:4, :], bank[4:6]
            pair_parts = lambda part: range(2) if part != "first" else range(0)
            with nc.Block() as block:
                @block.gpsimd
                def _(pool):
                    for n in range(2):
                        nc.gpsimd.tensor_copy(coefT[:, n, :], coefT_all[:, n * S:(n + 1) * S]).then_inc(c_copied, 1)
                    with pool.Fori(0, B // 2 - 1) as b:
                        for q in range(2):
                            pool.wait_ge(o_full, b * 2 + q + 1)
                            nc.gpsimd.tensor_copy(coefT[:, q, :], coefT_all[:, bass.ds(b * 2 * S + (2 + q) * S, S)]
                                                  ).then_inc(c_copied, 1)

                @block.tensor
                def _(pe):
                    def hidden(n):
                        for a in range(NPR):
                            last = nc.tensor.matmul(h_b[:, a // 2, (a % 2) * S:(a % 2) * S + S],
                                                    w1[:, 2 * a:2 * a + 2, :].rearrange("p e h -> p (e h)"),
                                                    xT_all[:, bass.ds(n * S, S)], start=(a % 2 == 0), stop=(a % 2 == 1),
                                                    skip_group_check=True)
                        last.then_inc(h_full, 1)

                    def weights(n, q):
                        pe.wait_ge(c_copied, n + 1)
                        for a in range(NPR):
                            last = nc.tensor.matmul(cb_b[:, a // 2, (a % 2) * S:(a % 2) * S + S], rows[:, a, :],
                                                    coefT[:, q % 2, :], start=(a % 2 == 0), stop=(a % 2 == 1),
                                                    skip_group_check=True)
                        last.then_inc(cb_full, 1)

                    def outputs(n, q):
                        pe.wait_ge(o_out, n + 1)
                        for t in range(LT):
                            c, o = slice(t * P, (t + 1) * P), o_b[q][:, t * D:(t + 1) * D]
                            for a in range(NPR):
                                nc.tensor.matmul(o, hidw[:, a, c], w2[:, a, :], start=(t == 0 and a == 0), stop=False,
                                                 skip_group_check=True)
                            last = nc.tensor.matmul(o, coefT[:, q, c], b2[:, :], start=False, stop=(t == LT - 1),
                                                    skip_group_check=True)
                        last.then_inc(o_full, 1)

                    def pair(part, b):
                        for q in pair_parts(part):
                            n = b * 2 + q
                            more = part == "loop" or q == 0
                            if more:
                                pe.wait_ge(h_ok, n + 1)
                                hidden(n + 1)
                            pe.wait_ge(hw_ok, n + 1)
                            outputs(n, q)
                            if more:
                                weights(n + 1, q + 1)

                    hidden(0)
                    weights(0, 0)
                    with pe.Fori(0, B // 2 - 1) as b:
                        pair("loop", b)
                    pair("last", B // 2 - 1)

                @block.scalar
                def _(act):
                    def gelu(n):
                        act.wait_ge(h_full, n + 1)
                        for a in range(NPR):
                            last = nc.scalar.activation(hid[:, a, :], h_b[:, a // 2, (a % 2) * S:(a % 2) * S + S],
                                                        ACT.Gelu, bias=b1[:, a:a + 1])
                        last.then_inc(h_ok, 1)

                    gelu(0)
                    with act.Fori(1, B) as n:
                        act.wait_ge(hw_ok, n)
                        gelu(n)

                @block.vector
                def _(dve):
                    dve.sem_inc(o_out, 2)

                    def weighted(n):
                        dve.wait_ge(h_ok, n + 1)
                        dve.wait_ge(cb_full, n + 1)
                        nc.vector.tensor_tensor(hidw[:, :, :].rearrange("p a s -> p (a s)"),
                                                cb_b.rearrange("p a s -> p (a s)"),
                                                hid[:, :, :].rearrange("p a s -> p (a s)"), ALU.mult).then_inc(hw_ok, 1)

                    def residual(n, q):
                        dve.wait_ge(o_full, n + 1)
                        xt = X[:, bass.ds(n * LT, LT), :].rearrange("p a c -> p (a c)")
                        nc.vector.tensor_tensor(xt, o_b[q][:, 0:LT * D], xt, ALU.add).then_inc(o_out, 1)

                    weighted(0)
                    with dve.Fori(0, B // 2 - 1) as b:
                        for q in range(2):
                            residual(b * 2 + q, q)
                            weighted(b * 2 + q + 1)
                    residual(B - 2, 0)
                    weighted(B - 1)
                    residual(B - 1, 1)

        layer_norm("ln4", store=out_v)


_INS = ['L0_attn_x', 'L0_attn_Wq', 'L0_attn_Wk', 'L0_attn_Wv', 'L0_attn_Eq', 'L0_attn_Ek', 'L0_attn_Ev',
        'L0_ffn_Wqkv', 'L0_ffn_q_scale', 'L0_ffn_k_scale', 'L0_ffn_Wo', 'L0_ffn_ln_g', 'L0_ffn_ln_b', 'L0_ffn_W1',
        'L0_ffn_b1', 'L0_ffn_W2', 'L0_ffn_b2', 'L1_attn_Wqkv', 'L1_attn_bqkv', 'L1_attn_Wout', 'L1_attn_bout',
        'L1_ffn_gate_w', 'L1_ffn_w1', 'L1_ffn_b1', 'L1_ffn_w2', 'L1_ffn_b2']


def kernel(**inputs):
    import numpy as _np
    import concourse.bacc as _bacc
    from concourse import mybir as _mybir
    from concourse.bass_utils import run_bass_kernel_spmd as _run

    nc = _bacc.Bacc("TRN2", target_bir_lowering=False, num_devices=1)
    arrays, args = {}, {}
    for name in _INS:
        a = _np.ascontiguousarray(inputs[name])
        arrays[f"in_{name}_dram"] = a
        args[name] = nc.dram_tensor(f"in_{name}_dram", a.shape, _mybir.dt.from_np(a.dtype), kind="ExternalInput").ap()
    for name, a in shape_constants().items():
        arrays[f"const_{name}_dram"] = a
        args[name] = nc.dram_tensor(f"const_{name}_dram", a.shape, _mybir.dt.from_np(a.dtype),
                                    kind="ExternalInput").ap()
    out = nc.dram_tensor("out_0_dram", (B, S, D), _mybir.dt.float32, kind="ExternalOutput").ap()
    build_program(nc, args, out)
    r = _run(nc, [arrays], core_ids=[0])
    return r.results[0]["out_0_dram"]
```
